# Optimizing a Trainium2 kernel written in Bass

```python
import numpy as np
import jax
import jax.numpy as jnp

def _softmax(x, axis=-1):
    return jax.nn.softmax(x, axis=axis)

def _gelu(x):
    return jax.nn.gelu(x, approximate=True)

def _silu(x):
    return jax.nn.silu(x)

def _sigmoid(x):
    return jax.nn.sigmoid(x)

def _layernorm(x, axis=-1, eps=1e-05):
    m = jnp.mean(x, axis=axis, keepdims=True)
    v = jnp.var(x, axis=axis, keepdims=True)
    return (x - m) / jnp.sqrt(v + eps)

def _scatter_add(tgt, idx, src, axis=0):
    return tgt.at[idx].add(src)

def _segment_sum(src, seg, n):
    return jax.ops.segment_sum(src, seg, n)
kernel_name = 'mk_decoder_preln_d2_seqx_r4_7eca59'

def setup_inputs(seed: int=0):
    np.random.seed(seed)
    _w = jnp.asarray

    def _rec_inputs():
        import jax
        import jax.numpy as jnp
        _rk = jax.random.key(seed)
        x = -0.0002928 + 1 * jax.random.normal(jax.random.fold_in(_rk, 1), (2, 1024, 256), jnp.float32)
        _lenS = 1024 - jax.random.randint(jax.random.fold_in(_rk, 7), (2,), 0, max(1, 1024 // 4) + 1, jnp.int32)
        _lenS2 = 154 - jax.random.randint(jax.random.fold_in(_rk, 8), (2,), 0, max(1, 154 // 4) + 1, jnp.int32)
        _ctx_768P = jax.random.normal(jax.random.fold_in(_rk, 11), (2, 16, 192), jnp.float32)
        _ctx_768c = jax.random.dirichlet(jax.random.fold_in(_rk, 511), 0.3 * jnp.ones((16,), jnp.float32), (2, 154))
        _ctx_768t = jnp.einsum('bsk,bkd->bsd', _ctx_768c, _ctx_768P)
        _ctx_768t = _ctx_768t * jax.lax.rsqrt(jnp.mean(jnp.square(_ctx_768t)) + 1e-12) * 0.953939
        ctx_768 = -0.00055796 + 0.999787 * (_ctx_768t + 0.3 * jax.random.normal(jax.random.fold_in(_rk, 611), (2, 154, 192), jnp.float32))
        return (x, ctx_768)
    x, ctx_768 = _rec_inputs()

    def _L0_attn_setup():
        import jax, jax.numpy as jnp
        import numpy as np
        import math
        DIM = 256
        N_HEADS = 16
        HEAD_DIM = DIM // N_HEADS
        B, S = (2, 512)
        key = jax.random.key(seed)
        k_x, k_wqkv, k_bqkv, k_wout, k_bout = jax.random.split(key, 5)
        scale_in = 1.0 / math.sqrt(DIM)
        x = jax.random.normal(k_x, (B, S, DIM), dtype=jnp.float32)
        Wqkv = jax.random.uniform(k_wqkv, (N_HEADS, DIM, 3 * HEAD_DIM), dtype=jnp.float32, minval=-scale_in, maxval=scale_in)
        bqkv = jax.random.uniform(k_bqkv, (N_HEADS, 3 * HEAD_DIM), dtype=jnp.float32, minval=-scale_in, maxval=scale_in)
        Wout = jax.random.uniform(k_wout, (DIM, DIM), dtype=jnp.float32, minval=-scale_in, maxval=scale_in)
        bout = jax.random.uniform(k_bout, (DIM,), dtype=jnp.float32, minval=-scale_in, maxval=scale_in)
        return {'x': x, 'Wqkv': Wqkv, 'bqkv': bqkv, 'Wout': Wout, 'bout': bout}
    _L0_attn_all = _L0_attn_setup()
    _L0_attn_in = {k: v for k, v in _L0_attn_all.items() if k in ('Wqkv', 'bqkv', 'Wout', 'bout')}
    del _L0_attn_all

    def _L0_xattn_setup():
        import jax, jax.numpy as jnp
        import numpy as np
        HEADS = 16
        DIM_HEAD = 64
        key = jax.random.key(seed)
        ks = jax.random.split(key, 7)
        b, n, m = (2, 512, 256)
        query_dim, context_dim = (256, 192)
        inner = HEADS * DIM_HEAD
        s_q = 1.0 / np.sqrt(query_dim)
        s_c = 1.0 / np.sqrt(context_dim)
        s_i = 1.0 / np.sqrt(inner)
        return {'x': jax.random.normal(ks[0], (b, n, query_dim), jnp.float32), 'context': jax.random.normal(ks[1], (b, m, context_dim), jnp.float32), 'Wq': jax.random.normal(ks[2], (query_dim, inner), jnp.float32) * s_q, 'Wk': jax.random.normal(ks[3], (context_dim, inner), jnp.float32) * s_c, 'Wv': jax.random.normal(ks[4], (context_dim, inner), jnp.float32) * s_c, 'Wo': jax.random.normal(ks[5], (inner, query_dim), jnp.float32) * s_i, 'bo': jax.random.normal(ks[6], (query_dim,), jnp.float32) * 0.01}
    _L0_xattn_all = _L0_xattn_setup()
    _L0_xattn_in = {k: v for k, v in _L0_xattn_all.items() if k in ('Wq', 'Wk', 'Wv', 'Wo', 'bo')}
    del _L0_xattn_all

    def _L0_ffn_setup():
        import jax, jax.numpy as jnp
        import numpy as np
        B, T, C, H, E, K = (4, 256, 256, 256, 8, 2)

        def _swiglu(x):
            a, b = jnp.split(x, 2, axis=-1)
            return jax.nn.silu(a) * b
        key = jax.random.key(seed)
        ks = jax.random.split(key, 6)
        s = 0.02
        x = jax.random.normal(ks[0], (B, T, C), jnp.float32)
        w_shared_in = jax.random.normal(ks[1], (C, 2 * H), jnp.float32) * s
        w_shared_out = jax.random.normal(ks[2], (H, C), jnp.float32) * s
        w1_shared = jax.random.normal(ks[3], (C, 2 * H), jnp.float32) * s
        w2 = jax.random.normal(ks[4], (E, H, C), jnp.float32) * s
        w_gate = jax.random.normal(ks[5], (C, E), jnp.float32) * s
        gate_bias = jnp.zeros((E,), jnp.float32)
        return {'x': x, 'w_shared_in': w_shared_in, 'w_shared_out': w_shared_out, 'w1_shared': w1_shared, 'w2': w2, 'w_gate': w_gate, 'gate_bias': gate_bias}
    _L0_ffn_all = _L0_ffn_setup()
    _L0_ffn_in = {k: v for k, v in _L0_ffn_all.items() if k in ('w_shared_in', 'w_shared_out', 'w1_shared', 'w2', 'w_gate', 'gate_bias')}
    del _L0_ffn_all

    def _L1_attn_setup():
        import jax, jax.numpy as jnp
        import numpy as np
        EPS = 1e-05

        def _rmsnorm(x, w):
            var = jnp.mean(jnp.square(x), axis=-1, keepdims=True)
            return x * jax.lax.rsqrt(var + EPS) * w

        def _act_quant(x):
            scale = 127.0 / jnp.clip(jnp.max(jnp.abs(x), axis=-1, keepdims=True), 1e-05, None)
            return jnp.clip(jnp.round(x * scale), -128.0, 127.0) / scale

        def _weight_quant(w):
            scale = 1.0 / jnp.clip(jnp.mean(jnp.abs(w)), 1e-05, None)
            return jnp.clip(jnp.round(w * scale), -1.0, 1.0) / scale

        def _bitlinear(x, w, nw):
            xn = _rmsnorm(x, nw)
            xq = xn + jax.lax.stop_gradient(_act_quant(xn) - xn)
            wq = w + jax.lax.stop_gradient(_weight_quant(w) - w)
            return jnp.einsum('bld,ed->ble', xq, wq)
        key = jax.random.key(seed)
        B, T, D = (4, 1024, 256)
        ks = jax.random.split(key, 6)
        std = 2.0 ** (-2.5) * np.sqrt(2.0 / (D + D))
        return {'hidden_states': jax.random.normal(ks[0], (B, T, D), jnp.float32), 'w_i': jax.random.normal(ks[1], (D, D), jnp.float32) * std, 'w_f': jax.random.normal(ks[2], (D, D), jnp.float32) * std, 'w_g': jax.random.normal(ks[3], (D, D), jnp.float32) * std, 'w_o': jax.random.normal(ks[4], (D, D), jnp.float32) * std, 'nw_i': jnp.ones((D,), jnp.float32), 'nw_f': jnp.ones((D,), jnp.float32), 'nw_g': jnp.ones((D,), jnp.float32), 'nw_o': jnp.ones((D,), jnp.float32), 'g_norm_w': jnp.ones((D,), jnp.float32)}
    _L1_attn_all = _L1_attn_setup()
    _L1_attn_in = {k: v for k, v in _L1_attn_all.items() if k in ('w_i', 'w_f', 'w_g', 'w_o', 'nw_i', 'nw_f', 'nw_g', 'nw_o', 'g_norm_w')}
    del _L1_attn_all

    def _L1_xattn_setup():
        import math
        import jax, jax.numpy as jnp
        import numpy as np
        B, SQ, SKV = (4, 512, 512)
        D_EMBED, D_CROSS, D_ATT, N_HEADS = (256, 192, 256, 16)
        D_HEAD = D_ATT // N_HEADS

        def _split_heads(t):
            b, s, _ = t.shape
            return t.reshape(b, s, N_HEADS, D_HEAD).transpose(0, 2, 1, 3)
        key = jax.random.key(seed)
        ks = jax.random.split(key, 10)
        s_e = 1.0 / math.sqrt(D_EMBED)
        s_c = 1.0 / math.sqrt(D_CROSS)
        s_a = 1.0 / math.sqrt(D_ATT)
        return {'x': jax.random.normal(ks[0], (B, SQ, D_EMBED), jnp.float32), 'y': jax.random.normal(ks[1], (B, SKV, D_CROSS), jnp.float32), 'Wq': jax.random.normal(ks[2], (D_EMBED, D_ATT), jnp.float32) * s_e, 'bq': jax.random.normal(ks[3], (D_ATT,), jnp.float32) * 0.01, 'Wk': jax.random.normal(ks[4], (D_CROSS, D_ATT), jnp.float32) * s_c, 'bk': jax.random.normal(ks[5], (D_ATT,), jnp.float32) * 0.01, 'Wv': jax.random.normal(ks[6], (D_CROSS, D_ATT), jnp.float32) * s_c, 'bv': jax.random.normal(ks[7], (D_ATT,), jnp.float32) * 0.01, 'Wo': jax.random.normal(ks[8], (D_ATT, D_EMBED), jnp.float32) * s_a, 'bo': jax.random.normal(ks[9], (D_EMBED,), jnp.float32) * 0.01}
    _L1_xattn_all = _L1_xattn_setup()
    _L1_xattn_in = {k: v for k, v in _L1_xattn_all.items() if k in ('Wq', 'bq', 'Wk', 'bk', 'Wv', 'bv', 'Wo', 'bo')}
    del _L1_xattn_all

    def _L1_ffn_setup():
        import jax, jax.numpy as jnp
        import numpy as np
        D_IN, D_H, D_OUT = (256, 256, 256)
        D_MOE = 1024
        N_EXPERTS = 8
        TOP_K = 2
        key = jax.random.key(seed)
        ks = jax.random.split(key, 10)
        s = lambda d: 1.0 / np.sqrt(d)
        x = jax.random.normal(ks[0], (2, 512, D_IN), dtype=jnp.float32)
        W_in = jax.random.normal(ks[1], (D_IN, D_H), dtype=jnp.float32) * s(D_IN)
        b_in = jnp.zeros((D_H,), jnp.float32)
        W_gate = jax.random.normal(ks[2], (D_H, N_EXPERTS), dtype=jnp.float32) * s(D_H)
        b_gate = jnp.zeros((N_EXPERTS,), jnp.float32)
        W1 = jax.random.normal(ks[3], (N_EXPERTS, D_H, D_MOE), dtype=jnp.float32) * s(D_H)
        b1 = jnp.zeros((N_EXPERTS, D_MOE), jnp.float32)
        W2 = jax.random.normal(ks[4], (N_EXPERTS, D_MOE, D_H), dtype=jnp.float32) * s(D_MOE)
        b2 = jnp.zeros((N_EXPERTS, D_H), jnp.float32)
        W_out = jax.random.normal(ks[5], (D_H, D_OUT), dtype=jnp.float32) * s(D_H)
        b_out = jnp.zeros((D_OUT,), jnp.float32)
        return {'x': x, 'W_in': W_in, 'b_in': b_in, 'W_gate': W_gate, 'b_gate': b_gate, 'W1': W1, 'b1': b1, 'W2': W2, 'b2': b2, 'W_out': W_out, 'b_out': b_out}
    _L1_ffn_all = _L1_ffn_setup()
    _L1_ffn_in = {k: v for k, v in _L1_ffn_all.items() if k in ('W_in', 'b_in', 'W_gate', 'b_gate', 'W1', 'b1', 'W2', 'b2', 'W_out', 'b_out')}
    del _L1_ffn_all
    return {'x': x, 'ctx_768': ctx_768, 'L0_attn_Wqkv': _L0_attn_in['Wqkv'], 'L0_attn_bqkv': _L0_attn_in['bqkv'], 'L0_attn_Wout': _L0_attn_in['Wout'], 'L0_attn_bout': _L0_attn_in['bout'], 'L0_xattn_Wq': _L0_xattn_in['Wq'], 'L0_xattn_Wk': _L0_xattn_in['Wk'], 'L0_xattn_Wv': _L0_xattn_in['Wv'], 'L0_xattn_Wo': _L0_xattn_in['Wo'], 'L0_xattn_bo': _L0_xattn_in['bo'], 'L0_ffn_w_shared_in': _L0_ffn_in['w_shared_in'], 'L0_ffn_w_shared_out': _L0_ffn_in['w_shared_out'], 'L0_ffn_w1_shared': _L0_ffn_in['w1_shared'], 'L0_ffn_w2': _L0_ffn_in['w2'], 'L0_ffn_w_gate': _L0_ffn_in['w_gate'], 'L0_ffn_gate_bias': _L0_ffn_in['gate_bias'], 'L1_attn_w_i': _L1_attn_in['w_i'], 'L1_attn_w_f': _L1_attn_in['w_f'], 'L1_attn_w_g': _L1_attn_in['w_g'], 'L1_attn_w_o': _L1_attn_in['w_o'], 'L1_attn_nw_i': _L1_attn_in['nw_i'], 'L1_attn_nw_f': _L1_attn_in['nw_f'], 'L1_attn_nw_g': _L1_attn_in['nw_g'], 'L1_attn_nw_o': _L1_attn_in['nw_o'], 'L1_attn_g_norm_w': _L1_attn_in['g_norm_w'], 'L1_xattn_Wq': _L1_xattn_in['Wq'], 'L1_xattn_bq': _L1_xattn_in['bq'], 'L1_xattn_Wk': _L1_xattn_in['Wk'], 'L1_xattn_bk': _L1_xattn_in['bk'], 'L1_xattn_Wv': _L1_xattn_in['Wv'], 'L1_xattn_bv': _L1_xattn_in['bv'], 'L1_xattn_Wo': _L1_xattn_in['Wo'], 'L1_xattn_bo': _L1_xattn_in['bo'], 'L1_ffn_W_in': _L1_ffn_in['W_in'], 'L1_ffn_b_in': _L1_ffn_in['b_in'], 'L1_ffn_W_gate': _L1_ffn_in['W_gate'], 'L1_ffn_b_gate': _L1_ffn_in['b_gate'], 'L1_ffn_W1': _L1_ffn_in['W1'], 'L1_ffn_b1': _L1_ffn_in['b1'], 'L1_ffn_W2': _L1_ffn_in['W2'], 'L1_ffn_b2': _L1_ffn_in['b2'], 'L1_ffn_W_out': _L1_ffn_in['W_out'], 'L1_ffn_b_out': _L1_ffn_in['b_out']}

def reference(x, ctx_768, L0_attn_Wqkv, L0_attn_bqkv, L0_attn_Wout, L0_attn_bout, L0_xattn_Wq, L0_xattn_Wk, L0_xattn_Wv, L0_xattn_Wo, L0_xattn_bo, L0_ffn_w_shared_in, L0_ffn_w_shared_out, L0_ffn_w1_shared, L0_ffn_w2, L0_ffn_w_gate, L0_ffn_gate_bias, L1_attn_w_i, L1_attn_w_f, L1_attn_w_g, L1_attn_w_o, L1_attn_nw_i, L1_attn_nw_f, L1_attn_nw_g, L1_attn_nw_o, L1_attn_g_norm_w, L1_xattn_Wq, L1_xattn_bq, L1_xattn_Wk, L1_xattn_bk, L1_xattn_Wv, L1_xattn_bv, L1_xattn_Wo, L1_xattn_bo, L1_ffn_W_in, L1_ffn_b_in, L1_ffn_W_gate, L1_ffn_b_gate, L1_ffn_W1, L1_ffn_b1, L1_ffn_W2, L1_ffn_b2, L1_ffn_W_out, L1_ffn_b_out):
    import jax
    import jax.numpy as jnp

    def _L0_attn_ref(x, Wqkv, bqkv, Wout, bout):
        import jax, jax.numpy as jnp
        import numpy as np
        import math
        DIM = 256
        N_HEADS = 16
        HEAD_DIM = DIM // N_HEADS
        B, S = (2, 512)
        b, s, d = x.shape
        qkv = jnp.einsum('bsd,hde->bhse', x, Wqkv) + bqkv[None, :, None, :]
        q, k, v = jnp.split(qkv, 3, axis=-1)
        score = jnp.einsum('bhsd,bhtd->bhst', q, k)
        causal = jnp.tril(jnp.ones((s, s), dtype=bool))
        score = jnp.where(causal[None, None], score, -jnp.inf)
        attn = jax.nn.softmax(score / jnp.sqrt(jnp.asarray(HEAD_DIM, x.dtype)), axis=-1)
        y = jnp.einsum('bhst,bhtd->bhsd', attn, v)
        y = jnp.transpose(y, (0, 2, 1, 3)).reshape(b, s, d)
        out = y @ Wout + bout
        return out

    def _L0_xattn_ref(x, context, Wq, Wk, Wv, Wo, bo):
        import jax, jax.numpy as jnp
        import numpy as np
        HEADS = 16
        DIM_HEAD = 64
        b, n, _ = x.shape
        h, d = (HEADS, DIM_HEAD)
        scale = d ** (-0.5)
        q = (x @ Wq).reshape(b, n, h, d).transpose(0, 2, 1, 3)
        k = (context @ Wk).reshape(b, -1, h, d).transpose(0, 2, 1, 3)
        v = (context @ Wv).reshape(b, -1, h, d).transpose(0, 2, 1, 3)
        sim = jnp.einsum('bhid,bhjd->bhij', q, k) * scale
        attn = jax.nn.softmax(sim, axis=-1)
        out = jnp.einsum('bhij,bhjd->bhid', attn, v)
        out = out.transpose(0, 2, 1, 3).reshape(b, n, h * d)
        return out @ Wo + bo

    def _L0_ffn_ref(x, w_shared_in, w_shared_out, w1_shared, w2, w_gate, gate_bias):
        import jax, jax.numpy as jnp
        import numpy as np
        B, T, C, H, E, K = (4, 256, 256, 256, 8, 2)

        def _swiglu(x):
            a, b = jnp.split(x, 2, axis=-1)
            return jax.nn.silu(a) * b
        Bx, Tx, Cx = x.shape
        S = Bx * Tx
        fx = x.reshape(S, Cx)
        shared_out = _swiglu(fx @ w_shared_in) @ w_shared_out
        logits = fx @ w_gate + gate_bias
        probs = jax.nn.softmax(logits, axis=-1)
        top_val, top_idx = jax.lax.top_k(probs, K)
        wdense = jnp.zeros((S, E), probs.dtype).at[jnp.arange(S)[:, None], top_idx].add(top_val)
        hid = _swiglu(fx @ w1_shared)
        routed_out = jnp.zeros_like(shared_out)
        for e in range(E):
            routed_out = routed_out + wdense[:, e:e + 1] * (hid @ w2[e])
        return (shared_out + routed_out).reshape(Bx, Tx, Cx)

    def _L1_attn_ref(hidden_states, w_i, w_f, w_g, w_o, nw_i, nw_f, nw_g, nw_o, g_norm_w):
        import jax, jax.numpy as jnp
        import numpy as np
        EPS = 1e-05

        def _rmsnorm(x, w):
            var = jnp.mean(jnp.square(x), axis=-1, keepdims=True)
            return x * jax.lax.rsqrt(var + EPS) * w

        def _act_quant(x):
            scale = 127.0 / jnp.clip(jnp.max(jnp.abs(x), axis=-1, keepdims=True), 1e-05, None)
            return jnp.clip(jnp.round(x * scale), -128.0, 127.0) / scale

        def _weight_quant(w):
            scale = 1.0 / jnp.clip(jnp.mean(jnp.abs(w)), 1e-05, None)
            return jnp.clip(jnp.round(w * scale), -1.0, 1.0) / scale

        def _bitlinear(x, w, nw):
            xn = _rmsnorm(x, nw)
            xq = xn + jax.lax.stop_gradient(_act_quant(xn) - xn)
            wq = w + jax.lax.stop_gradient(_weight_quant(w) - w)
            return jnp.einsum('bld,ed->ble', xq, wq)
        i = _bitlinear(hidden_states, w_i, nw_i)
        f = jax.nn.sigmoid(_bitlinear(hidden_states, w_f, nw_f))
        g = _bitlinear(hidden_states, w_g, nw_g)
        f_t = jnp.swapaxes(f, 0, 1)
        i_t = jnp.swapaxes(i, 0, 1)

        def step(h, xs):
            ft, it = xs
            h = ft * h + (1.0 - ft) * it
            return (h, h)
        h0 = jnp.zeros_like(i[:, 0])
        _, o = jax.lax.scan(step, h0, (f_t, i_t))
        o = jnp.swapaxes(o, 0, 1)
        o = _rmsnorm(o, g_norm_w) * g * jax.nn.sigmoid(g)
        return _bitlinear(o, w_o, nw_o)

    def _L1_xattn_ref(x, y, Wq, bq, Wk, bk, Wv, bv, Wo, bo):
        import math
        import jax, jax.numpy as jnp
        import numpy as np
        B, SQ, SKV = (4, 512, 512)
        D_EMBED, D_CROSS, D_ATT, N_HEADS = (256, 192, 256, 16)
        D_HEAD = D_ATT // N_HEADS

        def _split_heads(t):
            b, s, _ = t.shape
            return t.reshape(b, s, N_HEADS, D_HEAD).transpose(0, 2, 1, 3)
        q = _split_heads(x @ Wq + bq)
        k = _split_heads(y @ Wk + bk)
        v = _split_heads(y @ Wv + bv)
        scale = 1.0 / math.sqrt(D_HEAD)
        scores = jnp.einsum('bhqd,bhkd->bhqk', q, k) * scale
        weights = jax.nn.softmax(scores, axis=-1)
        out = jnp.einsum('bhqk,bhkd->bhqd', weights, v)
        out = out.transpose(0, 2, 1, 3).reshape(x.shape[0], x.shape[1], D_ATT)
        return out @ Wo + bo

    def _L1_ffn_ref(x, W_in, b_in, W_gate, b_gate, W1, b1, W2, b2, W_out, b_out):
        import jax, jax.numpy as jnp
        import numpy as np
        D_IN, D_H, D_OUT = (256, 256, 256)
        D_MOE = 1024
        N_EXPERTS = 8
        TOP_K = 2
        B, S, _ = x.shape
        h = x @ W_in + b_in
        t = h.reshape(B * S, -1)
        logits = t @ W_gate + b_gate
        probs = jax.nn.softmax(logits, axis=-1)
        topv, topi = jax.lax.top_k(probs, TOP_K)
        topv = topv / jnp.sum(topv, axis=-1, keepdims=True)
        route = jnp.zeros_like(probs).at[jnp.arange(t.shape[0])[:, None], topi].set(topv)
        mid = jax.nn.relu(jnp.einsum('nd,edh->neh', t, W1) + b1)
        eout = jnp.einsum('neh,ehd->ned', mid, W2) + b2
        moe_out = jnp.einsum('ne,ned->nd', route, eout)
        out = moe_out.reshape(B, S, -1) @ W_out + b_out
        return out
    x = x + _L0_attn_ref(_layernorm(x, axis=-1), L0_attn_Wqkv, L0_attn_bqkv, L0_attn_Wout, L0_attn_bout)
    x = x + _L0_xattn_ref(_layernorm(x, axis=-1), ctx_768, L0_xattn_Wq, L0_xattn_Wk, L0_xattn_Wv, L0_xattn_Wo, L0_xattn_bo)
    x = x + _L0_ffn_ref(_layernorm(x, axis=-1), L0_ffn_w_shared_in, L0_ffn_w_shared_out, L0_ffn_w1_shared, L0_ffn_w2, L0_ffn_w_gate, L0_ffn_gate_bias)
    x = x + _L1_attn_ref(_layernorm(x, axis=-1), L1_attn_w_i, L1_attn_w_f, L1_attn_w_g, L1_attn_w_o, L1_attn_nw_i, L1_attn_nw_f, L1_attn_nw_g, L1_attn_nw_o, L1_attn_g_norm_w)
    x = x + _L1_xattn_ref(_layernorm(x, axis=-1), ctx_768, L1_xattn_Wq, L1_xattn_bq, L1_xattn_Wk, L1_xattn_bk, L1_xattn_Wv, L1_xattn_bv, L1_xattn_Wo, L1_xattn_bo)
    x = x + _L1_ffn_ref(_layernorm(x, axis=-1), L1_ffn_W_in, L1_ffn_b_in, L1_ffn_W_gate, L1_ffn_b_gate, L1_ffn_W1, L1_ffn_b1, L1_ffn_W2, L1_ffn_b2, L1_ffn_W_out, L1_ffn_b_out)
    return x

_drawn_inputs = setup_inputs


def setup_inputs(seed=0):
    import zlib

    import numpy as np

    out = dict(_drawn_inputs(seed))
    spreads = {'L0_ffn_gate_bias': (0.0, 0.519),
     'L1_attn_nw_i': (1.0, 0.2),
     'L1_attn_nw_f': (1.0, 0.6),
     'L1_attn_nw_g': (1.0, 0.2),
     'L1_attn_nw_o': (1.0, 0.2),
     'L1_attn_g_norm_w': (1.0, 0.2),
     'L1_ffn_b_in': (0.0, 0.1),
     'L1_ffn_b_gate': (0.0, 0.1),
     'L1_ffn_b1': (0.0, 0.1),
     'L1_ffn_b2': (0.0, 0.1),
     'L1_ffn_b_out': (0.0, 0.1)}
    factors = {'L0_ffn_w1_shared': 3.223,
     'L0_ffn_w2': 4.701,
     'L0_ffn_w_gate': 4.347,
     'L1_attn_w_f': 2.682,
     'L1_xattn_bq': 8.0,
     'L1_xattn_bk': 8.0,
     'L1_xattn_bv': 2.814}
    for name, (base, spread) in spreads.items():
        noise = np.random.default_rng([zlib.crc32(name.encode()), seed]).standard_normal(out[name].shape)
        drawn = base * np.exp(spread * noise) if base else spread * noise
        out[name] = jnp.asarray(drawn.astype(out[name].dtype))
    for name, factor in factors.items():
        out[name] = (out[name] * factor).astype(out[name].dtype)
    return out
```

```python
from contextlib import ExitStack

import concourse.bass as bass
from concourse import mybir

ALU = mybir.AluOpType
ACT = mybir.ActivationFunctionType
AX = mybir.AxisListType
F32 = mybir.dt.float32
F32R = mybir.dt.float32r
BF16 = mybir.dt.bfloat16
U32 = mybir.dt.uint32

P = 128
B = 2
S = 1024
D = 256
N = B * S
NT = N // P
ST = S // P
KD = D // P
H = 16
DH = D // H
M = 154
MH = M // 2
DC = 192
EPS = 1e-5
MASKED = -1e30
VW = 32
HPU = 4
PARTS = 3
Q_ROWS = (0, 0, 1, 1, 0, 2)
K_ROWS = (0, 1, 0, 1, 2, 0)
KROWS = len(Q_ROWS) * DH + PARTS


def raw(ap):
    return ap.bitcast(F32) if ap.dtype == F32R else ap


class Signal:

    def __init__(self, sem):
        self.sem = sem
        self.base = 0

    def at(self, n):
        return self.base + n

    def passed(self, n):
        self.base += n


class Chain:

    def __init__(self, signal):
        self.sem, self.base, self.n = signal.sem, signal.base, 0

    def next(self):
        self.n = self.n + 1
        return self.base + self.n


class Core:

    def __init__(self, nc, ctx, arg):
        self.nc, self.ctx, self.arg = nc, ctx, arg
        self.signals = {}
        self.named = {}
        self.x = self.sb(ctx, "x", [P, NT, D], F32)
        self.ident = self.sb(ctx, "ident", [P, P], F32)
        self.identb = self.sb(ctx, "identb", [P, P], BF16)
        self.maxmask = self.sb(ctx, "maxmask", [P, P], BF16)
        self.expmask = self.sb(ctx, "expmask", [P, P], BF16)
        self.iota = self.sb(ctx, "iota8", [P, 8], F32)
        self.ps = ctx.enter_context(nc.psum_tensor("ps", [P, 8, 512], F32))

    def sb(self, ctx, name, shape, dt):
        self.named[name] = self.named.get(name, 0) + 1
        if self.named[name] > 1:
            name = f"{name}_{self.named[name]}"
        return ctx.enter_context(self.nc.sbuf_tensor(name, shape, dt))

    def sig(self, name):
        if name not in self.signals:
            self.signals[name] = Signal(self.ctx.enter_context(self.nc.semaphore(name)))
        return self.signals[name]


def setup(c):
    nc = c.nc
    x_in, const, cast = c.sig("x_in"), c.sig("const"), c.sig("const_cast")
    with nc.Block() as block:
        @block.sync
        def _(sp):
            for b in range(4):
                sp.dma_start(c.x[:, 4 * b:4 * b + 4, :],
                                      c.arg["x"].rearrange("b (t p) d -> p (b t) d", p=P)[:, 4 * b:4 * b + 4, :]).then_inc(x_in.sem, 16)
            sp.wait_ge(x_in.sem, x_in.at(64))

        @block.gpsimd
        def _(pool):
            link = Chain(const)
            pool.memset(c.ident[:, :], 0.0).then_inc(link.sem, 1)
            pool.wait_ge(link.sem, link.next())
            pool.affine_select(out=c.ident[:, :], in_=c.ident[:, :], compare_op=ALU.not_equal, fill=1.0,
                                    base=0, pattern=[[-1, P]], channel_multiplier=1).then_inc(link.sem, 1)
            pool.wait_ge(link.sem, link.next())
            pool.memset(c.maxmask[:, :], 0.0).then_inc(link.sem, 1)
            pool.wait_ge(link.sem, link.next())
            pool.affine_select(out=c.maxmask[:, :], in_=c.maxmask[:, :], compare_op=ALU.is_ge, fill=MASKED,
                                    base=0, pattern=[[-1, P]], channel_multiplier=1).then_inc(link.sem, 1)
            pool.wait_ge(link.sem, link.next())
            pool.memset(c.expmask[:, :], 0.0).then_inc(link.sem, 1)
            pool.wait_ge(link.sem, link.next())
            pool.affine_select(out=c.expmask[:, :], in_=c.expmask[:, :], compare_op=ALU.is_ge, fill=MASKED,
                                    base=0, pattern=[[1, P]], channel_multiplier=-1).then_inc(link.sem, 1)
            pool.wait_ge(link.sem, link.next())
            pool.iota(c.iota[:, :], [[1, 8]], base=0, channel_multiplier=0,
                           allow_small_or_imprecise_dtypes=True).then_inc(link.sem, 1)
            pool.wait_ge(link.sem, link.next())

        @block.vector
        def _(dve):
            dve.wait_ge(const.sem, const.at(2))
            dve.tensor_copy(c.identb[:, :], c.ident[:, :]).then_inc(cast.sem, 1)


class LayerNorm:

    def __init__(self, c, ctx, name):
        self.c = c
        self.stats = c.sb(ctx, name + "_stats", [P, NT, 6], F32)
        self.mv = c.sb(ctx, name + "_mv", [P, NT, 2], F32)
        self.ve = c.sb(ctx, name + "_ve", [P, NT], F32)
        self.sd = c.sb(ctx, name + "_sd", [P, NT], F32)
        self.rstd = c.sb(ctx, name + "_rstd", [P, NT], F32)
        self.xn = c.sb(ctx, name + "_xn", [P, NT, D], F32)
        self.s = {k: c.sig("ln_" + k) for k in ("stats", "meanvar", "vareps", "std", "rstd", "xn", "turned",
                                                "xt_act", "xt_dve")}

    def vector(self, dve):
        c, s = self.c, self.s
        for t in range(NT):
            dve.bn_stats(self.stats[:, t, :], c.x[:, t, :]).then_inc(s["stats"].sem, 1)
        for t in range(NT):
            dve.wait_ge(s["stats"].sem, s["stats"].at(t + 1))
            dve.bn_aggr(self.mv[:, t, :], self.stats[:, t, :]).then_inc(s["meanvar"].sem, 1)
        dve.wait_ge(s["meanvar"].sem, s["meanvar"].at(NT))
        dve.tensor_scalar(self.ve[:, :], self.mv[:, :, 1], EPS, None, ALU.add).then_inc(s["vareps"].sem, 1)
        dve.wait_ge(s["std"].sem, s["std"].at(1))
        dve.reciprocal(self.rstd[:, :], self.sd[:, :]).then_inc(s["rstd"].sem, 1)
        dve.wait_ge(s["rstd"].sem, s["rstd"].at(1))
        for t in range(NT):
            dve.tensor_scalar(self.xn[:, t, :], c.x[:, t, :], self.mv[:, t, 0:1],
                                          self.rstd[:, t:t + 1], ALU.subtract, ALU.mult).then_inc(s["xn"].sem, 1)

    def vector_xt(self, dve, xt):
        for g in range(NT // 4):
            dve.wait_ge(self.s["turned"].sem, self.s["turned"].at(2 * g + 2))
            dve.tensor_copy(xt[:, 1, 512 * g:512 * g + 512], self.c.ps[:, 2 * g + 1, :]).then_inc(self.s["xt_dve"].sem, 1)

    def scalar(self, act):
        act.wait_ge(self.s["vareps"].sem, self.s["vareps"].at(1))
        act.activation(self.sd[:, :], self.ve[:, :], ACT.Sqrt).then_inc(self.s["std"].sem, 1)

    def scalar_xt(self, act, xt):
        for g in range(NT // 4):
            act.wait_ge(self.s["turned"].sem, self.s["turned"].at(2 * g + 1))
            act.activation(xt[:, 0, 512 * g:512 * g + 512], self.c.ps[:, 2 * g, :], ACT.Copy).then_inc(self.s["xt_act"].sem, 1)

    def tensor(self, pe):
        c = self.c
        for g in range(NT // 4):
            for k in range(KD):
                for j in range(4):
                    t = 4 * g + j
                    if k == 0:
                        pe.wait_ge(self.s["xn"].sem, self.s["xn"].at(t + 1))
                    last = pe.transpose(c.ps[:, 2 * g + k, P * j:P * j + P], self.xn[:, t, P * k:P * k + P],
                                        c.ident[:, :])
                last.then_inc(self.s["turned"].sem, 1)

    def wait_xt(self, eng, g):
        eng.wait_ge(self.s["xt_act"].sem, self.s["xt_act"].at(g + 1))
        eng.wait_ge(self.s["xt_dve"].sem, self.s["xt_dve"].at(g + 1))

    def done(self, turned=True):
        for k, n in (("stats", NT), ("meanvar", NT), ("vareps", 1), ("std", 1), ("rstd", 1), ("xn", NT),
                     ("turned", 8 * turned), ("xt_act", 4 * turned), ("xt_dve", 4 * turned)):
            self.s[k].passed(n)


def head_parts(c, ctx, name):
    t = {}
    t["full"] = c.sb(ctx, name + "_full", [P, 2, 512], F32)
    t["rest"] = c.sb(ctx, name + "_rest", [P, 2, 512], F32)
    t["part"] = c.sb(ctx, name + "_part", [P, 2, PARTS, N], BF16)
    return t


def project_self(c, v_all, scr_q, scr_k):
    nc, ps = c.nc, c.ps
    wqkv, bqkv = c.arg["L0_attn_Wqkv"], c.arg["L0_attn_bqkv"]
    with ExitStack() as ctx:
        ln = LayerNorm(c, ctx, "ln0")
        xt = c.sb(ctx, "xt0", [P, KD, N], F32)
        w = c.sb(ctx, "w_qkv", [P, KD, H, 3 * DH], F32)
        w_qk = c.sb(ctx, "w_qk", [P, 2, KD, D], F32)
        bias = c.sb(ctx, "b_qk", [P, 2, KD], F32)
        bias_v = c.sb(ctx, "b_v", [P, H, DH], F32)
        t = head_parts(c, ctx, "h0")
        w_in, full, high, rest, mid, low, sent, v_set, v_zero = (
            c.sig("w_in"), c.sig("pr_full"), c.sig("pr_high"), c.sig("pr_rest"), c.sig("pr_mid"), c.sig("pr_low"),
            c.sig("pr_sent"), c.sig("pr_v"), c.sig("pr_vzero"))
        mm = c.sig("pr_mm")
        w_set = c.sig("pr_wset")
        blocks = [(i, mb) for i in range(2) for mb in range(KD)]
        NC = N // 512
        with nc.Block() as block:
            @block.sync
            def _(sp):
                for k in range(KD):
                    sp.dma_start(w[:, k, :, :], wqkv.rearrange("h (k p) e -> k p h e", p=P)[k]).then_inc(w_in.sem, 16)
                for i in range(2):
                    for h in range(H):
                        sp.dma_start(bias[DH * (h % 8):DH * (h % 8) + DH, i, h // 8:h // 8 + 1],
                                              bqkv[h:h + 1, DH * i:DH * i + DH].rearrange("a b -> b a")).then_inc(w_in.sem, 16)
                sp.dma_start(bias_v[:, :, :], bqkv[:, 2 * DH:3 * DH].partition_broadcast(P)).then_inc(w_in.sem, 16)
                for n, (i, mb) in enumerate(blocks):
                    sp.wait_ge(mid.sem, mid.at(NC * (n + 1)))
                    sp.wait_ge(low.sem, low.at(NC * (n + 1)))
                    for part in range(PARTS):
                        sp.dma_start((scr_q, scr_k)[i][part, P * mb:P * mb + P, :],
                                              t["part"][:, n % 2, part, :]).then_inc(sent.sem, 16)
                sp.wait_ge(sent.sem, sent.at(16 * PARTS * len(blocks)))

            @block.gpsimd
            def _(pool):
                pool.memset(v_all[:, :, :, DH:VW], 0.0).then_inc(v_zero.sem, 1)
                pool.wait_ge(v_zero.sem, v_zero.at(1))
                pool.memset(v_all[:, :, :, DH:DH + 1], 1.0).then_inc(v_zero.sem, 1)
                pool.wait_ge(w_in.sem, w_in.at(16 * (KD + 2 * H + 1)))
                for i in range(2):
                    for k in range(KD):
                        pool.tensor_copy(w_qk[:, i, k, :].rearrange("p (h e) -> p h e", h=H),
                                                   w[:, k, :, DH * i:DH * i + DH]).then_inc(w_set.sem, 1)

            @block.tensor
            def _(pe):
                ln.tensor(pe)
                pe.wait_ge(w_in.sem, w_in.at(16 * (KD + 2 * H + 1)))
                pe.wait_ge(w_set.sem, w_set.at(2 * KD))
                n = 0
                for i, mb in blocks:
                    for g in range(NC):
                        if n < NC:
                            ln.wait_xt(pe, 3)
                        if n >= 8:
                            pe.wait_ge(high.sem, high.at(n - 7))
                        for k in range(KD):
                            last = pe.matmul(ps[:, n % 8, :], w_qk[:, i, k, P * mb:P * mb + P],
                                             xt[:, k, 512 * g:512 * g + 512], start=(k == 0), stop=(k == KD - 1))
                        last.then_inc(mm.sem, 1)
                        n += 1
                for u in range(NT):
                    if u < 8:
                        pe.wait_ge(high.sem, high.at(n - 7 + u))
                    else:
                        pe.wait_ge(v_set.sem, v_set.at(u - 7))
                    for k in range(KD):
                        last = pe.matmul(ps[:, (n + u) % 8, 0:D], xt[:, k, P * u:P * u + P],
                                         w[:, k, :, 2 * DH:3 * DH], start=(k == 0), stop=(k == KD - 1))
                    last.then_inc(mm.sem, 1)

            @block.scalar
            def _(act):
                ln.scalar(act)
                ln.scalar_xt(act, xt)
                act.wait_ge(w_in.sem, w_in.at(16 * (KD + 2 * H + 1)))
                n = 0
                for m, (i, mb) in enumerate(blocks):
                    for g in range(NC):
                        act.wait_ge(mm.sem, mm.at(n + 1))
                        if n >= 2:
                            act.wait_ge(rest.sem, rest.at(n - 1))
                        if m >= 2 and g == 0:
                            act.wait_ge(sent.sem, sent.at(16 * PARTS * (m - 1)))
                        act.activation(t["full"][:, n % 2, :], ps[:, n % 8, :], ACT.Identity,
                                                bias=bias[:, i, mb:mb + 1]).then_inc(full.sem, 1)
                        act.activation(t["part"][:, m % 2, 0, 512 * g:512 * g + 512], ps[:, n % 8, :],
                                                ACT.Identity, bias=bias[:, i, mb:mb + 1]).then_inc(high.sem, 1)
                        if n >= 1:
                            act.wait_ge(rest.sem, rest.at(n))
                            o, q = (n - 1) % 2, n - 1
                            act.activation(t["part"][:, (q // NC) % 2, 1, 512 * (q % NC):512 * (q % NC) + 512],
                                                   t["rest"][:, o, :], ACT.Copy).then_inc(mid.sem, 1)
                        n += 1
                act.wait_ge(rest.sem, rest.at(n))
                act.activation(t["part"][:, (n - 1) // NC % 2, 1, 512 * (NC - 1):], t["rest"][:, (n - 1) % 2, :],
                                       ACT.Copy).then_inc(mid.sem, 1)

            @block.vector
            def _(dve):
                ln.vector(dve)
                ln.vector_xt(dve, xt)
                dve.wait_ge(w_in.sem, w_in.at(16 * (KD + 2 * H + 1)))

                def lows(q):
                    dve.wait_ge(mid.sem, mid.at(q + 1))
                    a = slice(512 * (q % NC), 512 * (q % NC) + 512)
                    dve.tensor_tensor(t["part"][:, (q // NC) % 2, 2, a], t["rest"][:, q % 2, :],
                                              t["part"][:, (q // NC) % 2, 1, a], ALU.subtract).then_inc(low.sem, 1)
                for n in range(len(blocks) * NC):
                    a = slice(512 * (n % NC), 512 * (n % NC) + 512)
                    dve.wait_ge(full.sem, full.at(n + 1))
                    dve.wait_ge(high.sem, high.at(n + 1))
                    if n >= 2:
                        dve.wait_ge(low.sem, low.at(n - 1))
                    dve.tensor_tensor(t["rest"][:, n % 2, :], t["full"][:, n % 2, :],
                                               t["part"][:, (n // NC) % 2, 0, a], ALU.subtract).then_inc(rest.sem, 1)
                    if n >= 1:
                        lows(n - 1)
                n = len(blocks) * NC
                lows(n - 1)
                dve.wait_ge(v_zero.sem, v_zero.at(2))
                for u in range(NT):
                    dve.wait_ge(mm.sem, mm.at(n + u + 1))
                    dve.tensor_tensor(v_all[:, u, :, 0:DH],
                                                ps[:, (n + u) % 8, 0:D].rearrange("p (h e) -> p h e", h=H),
                                                bias_v[:, :, :], ALU.add).then_inc(v_set.sem, 1)
        ln.done()
        n = len(blocks) * NC
        for s, k in ((w_in, 16 * (KD + 2 * H + 1)), (mm, n + NT), (full, n), (high, n), (rest, n), (mid, n), (low, n),
                     (sent, 16 * PARTS * len(blocks)), (v_set, NT), (v_zero, 2), (w_set, 2 * KD)):
            s.passed(k)


MAX_BANK = (0, 1)
EXP_BANK = (2, 4)
OUT_BANK = 6


class Turns:

    def __init__(self, filled, freed):
        self.filled, self.freed, self.n = filled, freed, 0

    def used(self):
        self.n = self.n + 1


class Attention:

    def __init__(self, c, ctx, name, units, heads, width, v_width, ahead, neg_parts, neg_dt):
        self.c, self.units, self.heads, self.width, self.v_width = c, units, heads, width, v_width
        self.ahead, self.ring, self.slots = ahead, ahead + 1, ahead + 3
        self.qb = heads * ST
        self.rows = heads * v_width
        self.neg_parts = neg_parts
        self.o_raw = c.sb(ctx, name + "_o_raw", [self.rows, 2, S], F32)
        self.top = c.sb(ctx, name + "_top", [P, self.ring, self.qb], F32)
        self.neg_rest = c.sb(ctx, name + "_neg_rest", [self.qb, 2, P], F32)
        self.neg = c.sb(ctx, name + "_neg", [self.qb, self.ring, neg_parts, P], neg_dt)
        self.rinv = c.sb(ctx, name + "_rinv", [P, 4, heads], F32)
        self.staged = [c.sig(f"a_staged{i}") for i in range(self.slots)]
        self.rows_in = [c.sig(f"a_rows{i}") for i in range(self.ring)]
        self.top_ready, self.neg_ready, self.weighed = c.sig("a_top"), c.sig("a_neg"), c.sig("a_weighed")
        self.chain, self.made = c.sig("a_chain"), c.sig("a_made")
        self.area = {k: (c.sig(f"a_{k}_filled"), c.sig(f"a_{k}_freed")) for k in ("max0", "max1", "exp0", "exp1")}
        self.out_freed = c.sig("a_out_freed")

    def turns(self):
        return {k: Turns(*v) for k, v in self.area.items()}

    def order(self):
        nu, nc, ahead = len(self.units), self.n_chunks, self.ahead
        for u in range(ahead):
            yield from (("piece", u, n) for n in range(self.n_pieces))
            yield "turn", u, 0
        weighs = [(nc * u + need, u, k) for u in range(nu) for k, need in enumerate(self.steps)]
        for u in range(nu):
            for n in range(nc):
                yield "chunk", u, n
                while weighs and weighs[0][0] + self.lag <= nc * u + n + 1:
                    yield "weigh", *weighs.pop(0)[1:]
                if n == self.out_chunk and u > 0:
                    yield "out", u - 1, 0
                if u + ahead < nu:
                    a, b = (self.n_pieces * min(m, self.piece_chunks) // self.piece_chunks for m in (n, n + 1))
                    yield from (("piece", u + ahead, m) for m in range(a, b))
                    if n == self.turn_chunk:
                        yield "turn", u + ahead, 0
        yield from (("weigh", u, k) for _, u, k in weighs)
        yield "out", nu - 1, 0

    def freed_after_out(self, u):
        n = [0, 0]
        for what, v, m in self.order():
            if what == "piece":
                n[m % 2] += 1
            elif what == "turn":
                n[0] += 1
            elif what == "out":
                n[0] += 1
                n[1] += 1
                if v == u:
                    return n

    def run(self):
        c, nc = self.c, self.c.nc
        ps, nu, ahead = c.ps, len(self.units), self.ahead
        with nc.Block() as block:
            @block.gpsimd
            def _(pool):
                self.pool(pool)

            @block.sync
            def _(sp):
                sp.wait_ge(self.made.sem, self.made.at(self.n_made))
                self.load(sp)

                def stage(u):
                    if u >= self.slots:
                        sp.wait_ge(self.weighed.sem, self.weighed.at(len(self.steps) * (u - self.slots + 1)))
                    self.stage(sp, u)

                def max_rows(u):
                    sp.wait_ge(self.neg_ready.sem, self.neg_ready.at(u + 1))
                    for part in range(self.neg_parts):
                        sp.dma_start(
                            raw(self.neg_row(u, part)).rearrange("p h (b s) -> p (h b) s", s=P),
                            raw(self.neg[:, u % self.ring, part:part + 1, :])).then_inc(self.rows_in[u % self.ring].sem, 16)

                for u in range(min(ahead + 1, nu)):
                    stage(u)
                for u in range(ahead):
                    max_rows(u)
                for u in range(nu):
                    if u + ahead + 1 < nu:
                        stage(u + ahead + 1)
                    if u + ahead < nu:
                        max_rows(u + ahead)

            @block.tensor
            def _(pe):
                t = self.turns()
                self.loaded(pe)

                def piece(u, n):
                    a = t[f"max{n % 2}"]
                    if n == 0:
                        pe.wait_ge(self.staged[u % self.slots].sem, self.staged[u % self.slots].at(self.stage_dmas * 16 * (u // self.slots + 1)))
                    pe.wait_ge(a.freed.sem, a.freed.at(a.n))
                    self.piece_scores(pe, u, n, MAX_BANK[n % 2]).then_inc(a.filled.sem, 1)
                    a.used()

                def turn(u, _):
                    a = t["max0"]
                    pe.wait_ge(a.freed.sem, a.freed.at(a.n))
                    pe.wait_ge(self.top_ready.sem, self.top_ready.at(u + 1))
                    pe.transpose(ps[0:self.qb, MAX_BANK[0], 0:P], self.top[:, u % self.ring, :],
                                        c.ident[:, :]).then_inc(a.filled.sem, 1)
                    a.used()

                def chunk(u, n):
                    if n == 0:
                        pe.wait_ge(self.rows_in[u % self.ring].sem, self.rows_in[u % self.ring].at(16 * self.neg_parts * (u // self.ring + 1)))
                    a = t[f"exp{n % 2}"]
                    pe.wait_ge(a.freed.sem, a.freed.at(a.n))
                    self.chunk_scores(pe, u, n, EXP_BANK[n % 2]).then_inc(a.filled.sem, 1)
                    a.used()

                def weigh(u, k):
                    if k == 0:
                        pe.wait_ge(self.out_freed.sem, self.out_freed.at(u))
                    for i in range(2):
                        pe.wait_ge(self.area[f"exp{i}"][1].sem, self.area[f"exp{i}"][1].at(self.n_chunks // 2 * u + (self.steps[k] + 1 - i) // 2))
                    self.weigh(pe, u, k).then_inc(self.weighed.sem, 1)

                def turn_out(u, _):
                    pe.wait_ge(self.out_freed.sem, self.out_freed.at(u + 1))
                    for half in range(2):
                        a = t[f"max{1 - half}"]
                        pe.wait_ge(a.freed.sem, a.freed.at(a.n))
                        for j in range(4):
                            q = 512 * half + P * j
                            last = pe.transpose(ps[:, MAX_BANK[1 - half], P * j:P * j + self.rows],
                                                self.o_raw[:, u % 2, q:q + P], c.ident[0:self.rows, 0:self.rows])
                        last.then_inc(a.filled.sem, 1)
                        a.used()

                for what, u, n in self.order():
                    {"piece": piece, "turn": turn, "chunk": chunk, "weigh": weigh, "out": turn_out}[what](u, n)

            @block.scalar
            def _(act):
                t = self.turns()

                def copy_out(u):
                    act.wait_ge(self.weighed.sem, self.weighed.at(len(self.steps) * (u + 1)))
                    if u >= 2:
                        for i, n in enumerate(self.freed_after_out(u - 2)):
                            act.wait_ge(self.area[f"max{i}"][1].sem, self.area[f"max{i}"][1].at(n))
                    act.activation(
                        self.o_raw[:, u % 2, :],
                        ps[0:self.rows, OUT_BANK:OUT_BANK + 2, :].rearrange("p b s -> p (b s)"), ACT.Copy).then_inc(self.out_freed.sem, 1)

                for u in range(nu):
                    for n in range(self.n_chunks):
                        a = t[f"exp{n % 2}"]
                        act.wait_ge(a.filled.sem, a.filled.at(a.n + 1))
                        g = len(self.steps) * u + self.step_of(n)
                        if g >= 2:
                            act.wait_ge(self.weighed.sem, self.weighed.at(g - 1))
                        self.chunk_exp(act, u, n, EXP_BANK[n % 2]).then_inc(a.freed.sem, 1)
                        a.used()
                        if n == self.copy_chunk and u > 0:
                            copy_out(u - 1)
                copy_out(nu - 1)

            @block.vector
            def _(dve):
                t = self.turns()
                link = Chain(self.chain)
                self.prepare(dve, link)

                def piece(u, n):
                    a = t[f"max{n % 2}"]
                    dve.wait_ge(a.filled.sem, a.filled.at(a.n + 1))
                    if n == 0 and u >= self.ring:
                        dve.wait_ge(self.neg_ready.sem, self.neg_ready.at(u - self.ring + 1))
                    self.piece_max(dve, u, n, MAX_BANK[n % 2]).then_inc(a.freed.sem, 1)
                    a.used()

                def minus(u, _):
                    for k in ("max0", "max1"):
                        dve.wait_ge(t[k].freed.sem, t[k].freed.at(t[k].n))
                    self.join_max(dve, u).then_inc(self.top_ready.sem, 1)
                    a = t["max0"]
                    dve.wait_ge(a.filled.sem, a.filled.at(a.n + 1))
                    src = ps[0:self.qb, MAX_BANK[0], 0:P]
                    if u >= self.ring:
                        dve.wait_ge(self.rows_in[u % self.ring].sem, self.rows_in[u % self.ring].at(16 * self.neg_parts * (u // self.ring)))
                    neg = self.neg[:, u % self.ring, :, :]
                    rest = self.neg_rest
                    dve.tensor_scalar(rest[:, 0, :], src, -1.0, None, ALU.mult).then_inc(a.freed.sem, 1)
                    a.used()
                    dve.wait_ge(a.freed.sem, a.freed.at(a.n))
                    dve.tensor_copy(neg[:, 0, :], rest[:, 0, :]).then_inc(link.sem, 1)
                    dve.wait_ge(link.sem, link.next())
                    for part in range(1, self.neg_parts):
                        former = raw(neg[:, part - 1, :])
                        if part < self.neg_parts - 1:
                            dve.tensor_tensor(rest[:, part, :], rest[:, part - 1, :], former, ALU.subtract).then_inc(link.sem, 1)
                            dve.wait_ge(link.sem, link.next())
                            dve.tensor_copy(neg[:, part, :], rest[:, part, :]).then_inc(link.sem, 1)
                            dve.wait_ge(link.sem, link.next())
                        else:
                            dve.tensor_tensor(neg[:, part, :], rest[:, part - 1, :], former,
                                                                 ALU.subtract).then_inc(self.neg_ready.sem, 1)

                def normalize(u, _):
                    b, g = self.units[u]
                    for half in range(2):
                        a = t[f"max{1 - half}"]
                        dve.wait_ge(a.filled.sem, a.filled.at(a.n + 1))
                        src = ps[:, MAX_BANK[1 - half], :].rearrange("p (t r) -> p t r", t=4)[:, :, 0:self.rows]
                        src = src.rearrange("p t (h e) -> p t h e", h=self.heads)
                        w = self.width
                        dve.reciprocal(self.rinv[:, :, :], src[:, :, :, w]).then_inc(link.sem, 1)
                        dve.wait_ge(link.sem, link.next())
                        tile = ST * b + 4 * half
                        dst = self.o_tok[:, tile:tile + 4, self.heads * w * g:self.heads * w * (g + 1)]
                        dve.tensor_tensor(dst.rearrange("p t (h e) -> p t h e", h=self.heads),
                                                 src[:, :, :, 0:w],
                                                 self.rinv[:, :, :].unsqueeze(3).to_broadcast([P, 4, self.heads, w]),
                                                 ALU.mult).then_inc(a.freed.sem, 1)
                        a.used()
                        dve.wait_ge(a.freed.sem, a.freed.at(a.n))

                for what, u, n in self.order():
                    if what in ("piece", "turn", "out"):
                        {"piece": piece, "turn": minus, "out": normalize}[what](u, n)
                self.chained = link.n
        n = self.freed_after_out(nu - 1)
        for i in range(2):
            for s in self.area[f"max{i}"]:
                s.passed(n[i])
            for s in self.area[f"exp{i}"]:
                s.passed(nu * self.n_chunks // 2)
        for i in range(self.slots):
            self.staged[i].passed(16 * self.stage_dmas * len(range(i, nu, self.slots)))
        for i in range(self.ring):
            self.rows_in[i].passed(16 * self.neg_parts * len(range(i, nu, self.ring)))
        for s, k in ((self.top_ready, nu), (self.neg_ready, nu), (self.weighed, len(self.steps) * nu),
                     (self.out_freed, nu), (self.made, self.n_made), (self.chain, self.chained)):
            s.passed(k)


class SelfAttention(Attention):

    def __init__(self, c, ctx, v_all, scr_q, scr_k, o_tok):
        gps = H // HPU
        super().__init__(c, ctx, "sa", [(b, g) for b in range(B) for g in range(gps)], HPU, DH, VW, 1, PARTS, BF16)
        self.v_all, self.scr, self.o_tok = v_all, (scr_q, scr_k), o_tok
        self.q_st = c.sb(ctx, "sa_q", [P, self.slots, HPU, S], BF16)
        self.k_st = c.sb(ctx, "sa_k", [P, self.slots, HPU, S], BF16)
        self.v_st = c.sb(ctx, "sa_v", [P, self.slots, ST, HPU, VW], F32)
        self.probs = c.sb(ctx, "sa_probs", [P, 2, HPU, S], F32)
        self.top2 = c.sb(ctx, "sa_top2", [P, 2, self.qb], F32)
        self.pieces = [(h, sb, k0, min(512, (sb + 1) * P - k0)) for sb in reversed(range(ST)) for h in range(HPU)
                       for k0 in range(0, (sb + 1) * P, 512)]
        self.chunks = [(kb, (h,)) for kb in range(ST // 2) for h in range(HPU)]
        self.chunks += [(kb, (h, h + 1)) for kb in range(ST // 2, ST) for h in range(0, HPU, 2)]
        self.n_pieces, self.n_chunks, self.piece_chunks = len(self.pieces), len(self.chunks), 16
        self.steps = [sum(kb <= k for kb, _ in self.chunks) for k in range(ST)]
        self.lag, self.turn_chunk, self.copy_chunk, self.out_chunk = 4, 20, 1, 7
        self.n_made, self.stage_dmas = self.slots, 13

    def load(self, sp):
        pass

    def loaded(self, pe):
        pass

    def step_of(self, n):
        return self.chunks[n][0]

    def pool(self, pool):
        for i in range(self.slots):
            pool.memset(self.k_st[96:P, i, :, :], 1.0).then_inc(self.made.sem, 1)

    def prepare(self, dve, link):
        dve.memset(self.q_st[96:P, :, :, :].rearrange("p a h s -> p (a h s)").bitcast(U32), 0).then_inc(link.sem, 1)
        dve.wait_ge(link.sem, link.next())
        dve.memset(self.top2[:, :, :], -3e38).then_inc(link.sem, 1)
        dve.wait_ge(link.sem, link.next())

    def stage(self, sp, u):
        b, g = self.units[u]
        done = self.staged[u % self.slots]
        rows = slice(HPU * DH * g, HPU * DH * (g + 1))
        for dst, src, parts in ((self.q_st, self.scr[0], Q_ROWS), (self.k_st, self.scr[1], K_ROWS)):
            for j, part in enumerate(parts):
                sp.dma_start(dst[DH * j:DH * j + DH, u % self.slots, :, :],
                                      src[part, rows, S * b:S * b + S].rearrange("(h e) s -> e h s", e=DH)).then_inc(done.sem, 16)
        sp.dma_start(self.v_st[:, u % self.slots, :, :, :],
                              self.v_all[:, ST * b:ST * b + ST, HPU * g:HPU * g + HPU, :]).then_inc(done.sem, 16)

    def neg_row(self, u, part):
        r = len(Q_ROWS) * DH + part
        return self.q_st[r:r + 1, u % self.slots, :, :]

    def piece_scores(self, pe, u, n, bank):
        c, slot = self.c, u % self.slots
        h, sb, k0, w = self.pieces[n]
        diagonal = k0 + w == (sb + 1) * P
        last = pe.matmul(c.ps[:, bank, 0:w], self.q_st[0:96, slot, h, P * sb:P * sb + P],
                         self.k_st[0:96, slot, h, k0:k0 + w], start=True, stop=not diagonal)
        if diagonal:
            last = pe.matmul(c.ps[:, bank, w - P:w], c.identb[:, :], c.maxmask[:, :], start=False, stop=True)
        return last

    def piece_max(self, dve, u, n, bank):
        h, sb, k0, w = self.pieces[n]
        return dve.tensor_reduce(self.top2[:, k0 // 512, ST * h + sb:ST * h + sb + 1], self.c.ps[:, bank, 0:w],
                                 AX.X, ALU.max)

    def join_max(self, dve, u):
        return dve.tensor_tensor(self.top[:, u % self.ring, :], self.top2[:, 0, :], self.top2[:, 1, :], ALU.max)

    def chunk_scores(self, pe, u, n, bank):
        c, slot = self.c, u % self.slots
        kb, heads = self.chunks[n]
        for j, h in enumerate(heads):
            for q0 in range(0, S - P * kb, 512):
                qw = min(512, S - P * kb - q0)
                out = c.ps[:, bank + j + q0 // 512, :]
                last = pe.matmul(out[:, 0:qw], self.k_st[0:KROWS, slot, h, P * kb:P * kb + P],
                                 self.q_st[0:KROWS, slot, h, P * kb + q0:P * kb + q0 + qw],
                                 start=True, stop=q0 > 0)
                if q0 == 0:
                    last = pe.matmul(out[:, 0:P], c.identb[:, :], c.expmask[:, :], start=False, stop=True)
        return last

    def chunk_exp(self, act, u, n, bank):
        kb, heads = self.chunks[n]
        w = S - P * kb
        if len(heads) == 2:
            src, dst = self.c.ps[:, bank:bank + 2, 0:w], self.probs[:, kb % 2, heads[0]:heads[0] + 2, 0:w]
        else:
            src = self.c.ps[:, bank:bank + 2, :].rearrange("p b s -> p (b s)")[:, 0:w]
            dst = self.probs[:, kb % 2, heads[0], 0:w]
        return act.activation(dst, src, ACT.Exp, scale=self.width ** -0.5)

    def weigh(self, pe, u, kb):
        for half in range(2):
            q0, q1 = max(P * kb, 512 * half), 512 * (half + 1)
            if q0 >= q1:
                continue
            for h in range(HPU):
                last = pe.matmul(self.c.ps[VW * h:VW * h + VW, OUT_BANK + half, q0 - 512 * half:512],
                                 self.v_st[:, u % self.slots, kb, h, :], self.probs[:, kb % 2, h, q0 - P * kb:q1 - P * kb],
                                 start=(kb == 0), stop=(kb == 4 * half + 3))
        return last


class CrossAttention(Attention):

    def __init__(self, c, ctx, wide, v_all, scr_q, scr_k, o_tok):
        heads, width = (1, 64) if wide else (HPU, DH)
        ahead = 3 if wide else 1
        super().__init__(c, ctx, "ca", [(b, g) for b in range(B) for g in range(H // heads)], heads, width,
                         width + 1 if wide else VW, ahead, 2 if wide else PARTS, F32R if wide else BF16)
        self.wide, self.v_all, self.scr, self.o_tok = wide, v_all, (scr_q, scr_k), o_tok
        self.dt = F32R if wide else BF16
        self.q_st = c.sb(ctx, "ca_q", [P, self.slots, heads, S], self.dt)
        self.kcols = self.slots * 256 if wide else H * B * M
        self.k_st = c.sb(ctx, "ca_k", [P, self.kcols], self.dt)
        if wide:
            self.qb_st = c.sb(ctx, "ca_qb", [P, self.slots, heads, S], self.dt)
            self.kb_max = c.sb(ctx, "ca_kb_max", [P, self.kcols], self.dt)
            self.kb_exp = c.sb(ctx, "ca_kb_exp", [P, self.kcols], self.dt)
        self.probs = c.sb(ctx, "ca_probs", [MH, 2, heads, S], F32)
        self.top_raw = c.sb(ctx, "ca_top_raw", [P, self.qb], F32)
        self.group = 2 if wide else 3
        self.step = 256 if wide else M
        self.n_pieces = -(-self.qb // self.group)
        self.n_chunks = 2 * heads
        self.piece_chunks = self.n_chunks - (0 if wide else 1)
        self.steps = [heads, 2 * heads]
        if wide:
            self.lag, self.turn_chunk, self.copy_chunk, self.out_chunk = 1, 1, 0, 1
        else:
            self.lag, self.turn_chunk, self.copy_chunk, self.out_chunk = 1, 7, 1, 3
        self.n_made = 5 if wide else 2
        self.stage_dmas = 7 if wide else 6
        self.k_in = c.sig("ca_k_in")

    def step_of(self, n):
        return n // self.heads

    def key(self, u, h):
        if self.wide:
            return 256 * (u % self.slots)
        b, g = self.units[u]
        return M * (B * (self.heads * g + h) + b)

    def pool(self, pool):
        if self.wide:
            link = Chain(self.made)
            pool.memset(self.kb_max[:, :].bitcast(F32), 0.0).then_inc(link.sem, 1)
            pool.wait_ge(link.sem, link.next())
            pool.memset(self.kb_exp[:, :].bitcast(F32), 0.0).then_inc(link.sem, 1)
            pool.wait_ge(link.sem, link.next())
            pool.memset(self.kb_exp[64:66, :].bitcast(F32), 1.0).then_inc(link.sem, 1)
            pool.wait_ge(link.sem, link.next())
            pool.memset(self.k_st[:, :].bitcast(F32), 0.0).then_inc(link.sem, 1)
            pool.wait_ge(link.sem, link.next())
            pool.memset(self.qb_st[64:P, :, :, :].bitcast(F32), 0.0).then_inc(link.sem, 1)
            pool.wait_ge(link.sem, link.next())
        else:
            pool.memset(self.k_st[96:P, :], 1.0).then_inc(self.made.sem, 1)
            pool.memset(self.q_st[96:P, :, :, :], 0.0).then_inc(self.made.sem, 1)

    def prepare(self, dve, link):
        pass

    def load(self, sp):
        scr = self.scr[1]
        n = H * B * M
        if not self.wide:
            for j, part in enumerate(K_ROWS):
                sp.dma_start(self.k_st[DH * j:DH * j + DH, 0:n].rearrange("e (h k) -> e h k", h=H),
                                           scr[part].rearrange("(h e) k -> e h k", e=DH)).then_inc(self.k_in.sem, 16)

    def loaded(self, pe):
        if not self.wide:
            pe.wait_ge(self.k_in.sem, self.k_in.at(16 * len(K_ROWS)))

    def stage(self, sp, u):
        b, g = self.units[u]
        done = self.staged[u % self.slots]
        slot = u % self.slots
        if self.wide:
            for dst, part, row in ((self.q_st, 0, 0), (self.q_st, 1, 64), (self.qb_st, 0, 0)):
                sp.dma_start(raw(dst[row:row + 64, slot, 0, :]),
                                      self.scr[0][part, 64 * g:64 * g + 64, S * b:S * b + S]).then_inc(done.sem, 16)
            k0 = self.key(u, 0)
            for dst, part, row in ((self.k_st, 0, 0), (self.k_st, 0, 64), (self.kb_max, 1, 0), (self.kb_exp, 1, 0)):
                sp.dma_start(raw(dst[row:row + 64, k0:k0 + M]),
                                      self.scr[1][part, 64 * g:64 * g + 64, M * b:M * b + M]).then_inc(done.sem, 16)
        else:
            rows = slice(HPU * DH * g, HPU * DH * (g + 1))
            for j, part in enumerate(Q_ROWS):
                sp.dma_start(self.q_st[DH * j:DH * j + DH, slot, :, :],
                                      self.scr[0][part, rows, S * b:S * b + S].rearrange("(h e) s -> e h s", e=DH)).then_inc(done.sem, 16)

    def neg_row(self, u, part):
        if self.wide:
            return self.qb_st[64 + part:65 + part, u % self.slots, :, :]
        r = len(Q_ROWS) * DH + part
        return self.q_st[r:r + 1, u % self.slots, :, :]

    def piece_scores(self, pe, u, n, bank):
        slot = u % self.slots
        for j in range(min(self.group, self.qb - self.group * n)):
            h, sb = divmod(self.group * n + j, ST)
            k0 = self.key(u, h)
            out = self.c.ps[:, bank, self.step * j:self.step * (j + 1)]
            q = slice(P * sb, P * sb + P)
            if self.wide:
                pe.matmul(out, self.q_st[:, slot, h, q], self.k_st[:, k0:k0 + 256], start=True, stop=False)
                last = pe.matmul(out, self.qb_st[:, slot, h, q], self.kb_max[:, k0:k0 + 256], start=False, stop=True)
            else:
                last = pe.matmul(out, self.q_st[0:96, slot, h, q], self.k_st[0:96, k0:k0 + M], start=True, stop=True)
        return last

    def piece_max(self, dve, u, n, bank):
        k = min(self.group, self.qb - self.group * n)
        src = self.c.ps[:, bank, 0:self.step * k].rearrange("p (k m) -> p k m", k=k)[:, :, 0:M]
        return dve.tensor_reduce(self.top_raw[:, self.group * n:self.group * n + k], src, AX.X, ALU.max)

    def join_max(self, dve, u):
        return dve.tensor_copy(self.top[:, u % self.ring, :], self.top_raw[:, :])

    def chunk_scores(self, pe, u, n, bank):
        slot = u % self.slots
        half, h = divmod(n, self.heads)
        k0 = self.key(u, h) + MH * half
        for q in range(2):
            out = self.c.ps[0:MH, bank + q, :]
            cols = slice(512 * q, 512 * q + 512)
            if self.wide:
                pe.matmul(out, self.k_st[:, k0:k0 + MH], self.q_st[:, slot, h, cols], start=True, stop=False)
                last = pe.matmul(out, self.kb_exp[:, k0:k0 + MH], self.qb_st[:, slot, h, cols],
                                 start=False, stop=True)
            else:
                last = pe.matmul(out, self.k_st[0:KROWS, k0:k0 + MH], self.q_st[0:KROWS, slot, h, cols],
                                 start=True, stop=True)
        return last

    def chunk_exp(self, act, u, n, bank):
        half, h = divmod(n, self.heads)
        return act.activation(self.probs[:, half, h, :],
                              self.c.ps[0:MH, bank:bank + 2, :].rearrange("p b s -> p (b s)"), ACT.Exp,
                              scale=self.width ** -0.5)

    def weigh(self, pe, u, half):
        b, g = self.units[u]
        for q in range(2):
            for h in range(self.heads):
                w = self.v_width
                last = pe.matmul(self.c.ps[w * h:w * h + w, OUT_BANK + q, :],
                                 self.v_all[:, 2 * b + half, self.heads * g + h, :],
                                 self.probs[:, half, h, 512 * q:512 * q + 512], start=(half == 0), stop=(half == 1))
        return last


def make_context(c, ct):
    nc = c.nc
    with ExitStack() as ctx:
        raw = c.sb(ctx, "ctx_raw", [MH, 4, DC], F32)
        c_in, turned, set_ = c.sig("c_in"), c.sig("c_turned"), c.sig("c_set")
        with nc.Block() as block:
            @block.sync
            def _(sp):
                sp.dma_start(raw[:, :, :], c.arg["ctx_768"].rearrange("b (i m) d -> m (b i) d", m=MH)).then_inc(c_in.sem, 16)

            @block.tensor
            def _(pe):
                pe.wait_ge(c_in.sem, c_in.at(16))
                for k in range(2):
                    for j in range(4):
                        last = pe.transpose(c.ps[0:96, k, MH * j:MH * j + MH], raw[:, j, 96 * k:96 * k + 96],
                                            c.ident[0:MH, 0:MH])
                last.then_inc(turned.sem, 1)

            @block.vector
            def _(dve):
                dve.wait_ge(turned.sem, turned.at(1))
                dve.tensor_copy(ct[:, :, :], c.ps[0:96, 0:2, 0:B * M]).then_inc(set_.sem, 1)
    for s, k in ((c_in, 16), (turned, 1), (set_, 1)):
        s.passed(k)


def project_cross(c, layer, wide, ct, v_all, scr_q, scr_k):
    nc, ps = c.nc, c.ps
    width = 64 if wide else DH
    rows = H * width
    blocks = rows // P
    dt = F32R if wide else BF16
    parts = 2 if wide else PARTS
    biased = not wide
    arg = {k: c.arg[f"L{layer}_xattn_{k}"] for k in ("Wq", "Wk", "Wv") + (("bq", "bk", "bv") if biased else ())}
    vw = v_all.shape[3]
    with ExitStack() as ctx:
        ln = LayerNorm(c, ctx, f"lnx{layer}")
        xt = c.sb(ctx, "xc_t", [P, KD, N], F32)
        wq = c.sb(ctx, "xc_wq", [P, KD, rows], F32)
        wk = c.sb(ctx, "xc_wk", [96, 2, rows], F32)
        wv = c.sb(ctx, "xc_wv", [96, 2, rows], F32)
        bias = c.sb(ctx, "xc_bias", [P, 2, KD], F32)
        bias_v = c.sb(ctx, "xc_bias_v", [P, D], F32)
        full = c.sb(ctx, "xc_full", [P, 2, 512], F32)
        rest = c.sb(ctx, "xc_rest", [P, 2, 512], F32)
        part = c.sb(ctx, "xc_part", [P, 2, parts, 512], dt)
        w_in, mm, s_full, high, s_rest, mid, low, sent, v_set, v_zero = (
            c.sig(k) for k in ("w_in", "pr_mm", "pr_full", "pr_high", "pr_rest", "pr_mid", "pr_low", "xc_sent",
                               "pr_v", "pr_vzero"))
        sent2 = c.sig("xc_sent2")
        sents = (sent, sent2)
        jobs = [(1, m, 0, B * M) for m in range(blocks)]
        jobs += [(0, m, 512 * g, 512) for g in range(N // 512) for m in range(blocks)]
        nj = len(jobs)
        vjobs = [(j, n0) for j in range(4) for n0 in range(0, rows, 512)]
        vcols = min(512, rows)
        loads = 2 * KD + 2 + (2 * KD + 1 if biased else 0)
        with nc.Block() as block:
            @block.sync
            def _(sp):
                for k in range(2):
                    sp.dma_start(wk[:, k, :], arg["Wk"][96 * k:96 * k + 96, :]).then_inc(w_in.sem, 16)
                    sp.dma_start(wv[:, k, :], arg["Wv"][96 * k:96 * k + 96, :]).then_inc(w_in.sem, 16)
                for k in range(KD):
                    sp.dma_start(wq[:, k, :], arg["Wq"][P * k:P * k + P, :]).then_inc(w_in.sem, 16)
                if biased:
                    for i, b in enumerate(("bq", "bk")):
                        for k in range(KD):
                            sp.dma_start(bias[:, i, k:k + 1],
                                                  arg[b].rearrange("(a b) -> b a", a=KD)[:, k:k + 1]).then_inc(w_in.sem, 16)
                    sp.dma_start(bias_v[:, :], arg["bv"].rearrange("(a b) -> a b", a=1)
                                          .partition_broadcast(P)).then_inc(w_in.sem, 16)
                for n, (i, m, c0, w) in enumerate(jobs):
                    if biased:
                        sp.wait_ge(low.sem, low.at(n + 1))
                    else:
                        sp.wait_ge(s_rest.sem, s_rest.at(n + 1))
                    for k in range(parts):
                        sp.dma_start((scr_q, scr_k)[i][k, P * m:P * m + P, c0:c0 + w],
                                                      raw(part[:, n % 2, k, 0:w])).then_inc(sents[n % 2].sem, 16)
                for i in range(2):
                    sp.wait_ge(sents[i].sem, sents[i].at(16 * parts * len(range(i, nj, 2))))

            @block.gpsimd
            def _(pool):
                pool.memset(v_all[:, :, :, width:vw], 0.0).then_inc(v_zero.sem, 1)
                pool.wait_ge(v_zero.sem, v_zero.at(1))
                pool.memset(v_all[:, :, :, width:width + 1], 1.0).then_inc(v_zero.sem, 1)

            @block.tensor
            def _(pe):
                ln.tensor(pe)
                pe.wait_ge(w_in.sem, w_in.at(16 * loads))
                ln.wait_xt(pe, 3)
                for n, (i, m, c0, w) in enumerate(jobs):
                    if n >= 8:
                        pe.wait_ge(s_rest.sem, s_rest.at(n - 7))
                    for k in range(2):
                        src, wt = (ct, wk) if i else (xt, wq)
                        last = pe.matmul(ps[:, n % 8, 0:w], wt[:, k, P * m:P * m + P], src[:, k, c0:c0 + w],
                                         start=(k == 0), stop=(k == 1))
                    last.then_inc(mm.sem, 1)
                for u, (j, n0) in enumerate(vjobs):
                    if u < 8:
                        pe.wait_ge(s_rest.sem, s_rest.at(nj - 7 + u))
                    else:
                        pe.wait_ge(v_set.sem, v_set.at(u - 7))
                    for k in range(2):
                        last = pe.matmul(ps[0:MH, (nj + u) % 8, 0:vcols], ct[:, k, MH * j:MH * j + MH],
                                         wv[:, k, n0:n0 + vcols], start=(k == 0), stop=(k == 1))
                    last.then_inc(mm.sem, 1)

            @block.scalar
            def _(act):
                ln.scalar(act)
                ln.scalar_xt(act, xt)
                act.wait_ge(w_in.sem, w_in.at(16 * loads))
                for n, (i, m, c0, w) in enumerate(jobs):
                    act.wait_ge(mm.sem, mm.at(n + 1))
                    if n >= 2:
                        act.wait_ge(s_rest.sem, s_rest.at(n - 1))
                        act.wait_ge(sents[n % 2].sem, sents[n % 2].at(16 * parts * (n // 2)))
                    b = bias[:, i, m:m + 1] if biased else 0.0
                    if biased:
                        act.activation(full[:, n % 2, 0:w], ps[:, n % 8, 0:w], ACT.Identity, bias=b).then_inc(s_full.sem, 1)
                        act.activation(part[:, n % 2, 0, 0:w], ps[:, n % 8, 0:w], ACT.Identity, bias=b).then_inc(high.sem, 1)
                        if n >= 1:
                            pw = jobs[n - 1][3]
                            act.wait_ge(s_rest.sem, s_rest.at(n))
                            act.activation(part[:, (n - 1) % 2, 1, 0:pw], rest[:, (n - 1) % 2, 0:pw], ACT.Copy).then_inc(mid.sem, 1)
                    else:
                        act.activation(part[:, n % 2, 0, 0:w], ps[:, n % 8, 0:w], ACT.Copy).then_inc(high.sem, 1)
                if biased:
                    act.wait_ge(s_rest.sem, s_rest.at(nj))
                    pw = jobs[-1][3]
                    act.activation(part[:, (nj - 1) % 2, 1, 0:pw], rest[:, (nj - 1) % 2, 0:pw], ACT.Copy).then_inc(mid.sem, 1)

            @block.vector
            def _(dve):
                ln.vector(dve)
                ln.vector_xt(dve, xt)
                dve.wait_ge(w_in.sem, w_in.at(16 * loads))

                def lows(q):
                    w = jobs[q][3]
                    dve.wait_ge(mid.sem, mid.at(q + 1))
                    dve.tensor_tensor(part[:, q % 2, 2, 0:w], rest[:, q % 2, 0:w], part[:, q % 2, 1, 0:w],
                                              ALU.subtract).then_inc(low.sem, 1)
                for n, (i, m, c0, w) in enumerate(jobs):
                    dve.wait_ge(high.sem, high.at(n + 1))
                    if biased:
                        dve.wait_ge(s_full.sem, s_full.at(n + 1))
                        if n >= 2:
                            dve.wait_ge(low.sem, low.at(n - 1))
                        dve.tensor_tensor(rest[:, n % 2, 0:w], full[:, n % 2, 0:w], part[:, n % 2, 0, 0:w],
                                                     ALU.subtract).then_inc(s_rest.sem, 1)
                        if n >= 1:
                            lows(n - 1)
                    else:
                        dve.tensor_tensor(part[:, n % 2, 1, 0:w], ps[:, n % 8, 0:w],
                                                     part[:, n % 2, 0, 0:w].bitcast(F32), ALU.subtract).then_inc(s_rest.sem, 1)
                if biased:
                    lows(nj - 1)
                dve.wait_ge(v_zero.sem, v_zero.at(2))
                for u, (j, n0) in enumerate(vjobs):
                    dve.wait_ge(mm.sem, mm.at(nj + u + 1))
                    h0, hn = n0 // width, vcols // width
                    src = ps[0:MH, (nj + u) % 8, 0:vcols].rearrange("p (h e) -> p h e", h=hn)
                    dst = v_all[:, j, h0:h0 + hn, 0:width]
                    if biased:
                        dve.tensor_tensor(dst, src, bias_v[0:MH, :].rearrange("p (h e) -> p h e", h=hn),
                                                    ALU.add).then_inc(v_set.sem, 1)
                    else:
                        dve.tensor_copy(dst, src).then_inc(v_set.sem, 1)
        ln.done()
        for s, k in ((w_in, 16 * loads), (mm, nj + len(vjobs)), (s_full, nj * biased), (high, nj), (s_rest, nj),
                     (mid, nj * biased), (low, nj * biased), (v_set, len(vjobs)), (v_zero, 2),
                     (sent, 16 * parts * ((nj + 1) // 2)), (sent2, 16 * parts * (nj // 2))):
            s.passed(k)


def project_out(c, name, o_tok, blocks, weight, bias):
    nc, ps = c.nc, c.ps
    banks = -(-blocks // 4)
    with ExitStack() as ctx:
        w = c.sb(ctx, name + "_w", [P, blocks, D], F32)
        bb = c.sb(ctx, name + "_b", [P, D], F32)
        ot = c.sb(ctx, name + "_ot", [P, 2, blocks * P], F32)
        w_in, turned, copied, mm, added, biased = (c.sig(k) for k in ("w_in", "po_turned", "po_copied", "po_mm",
                                                                      "po_added", "po_biased"))
        with nc.Block() as block:
            @block.sync
            def _(sp):
                sp.dma_start(bb[:, :], bias.rearrange("(a b) -> a b", a=1).partition_broadcast(P)).then_inc(w_in.sem, 16)
                sp.dma_start(w[:, :, :], weight.rearrange("(k p) n -> p k n", p=P)).then_inc(w_in.sem, 16)

            @block.gpsimd
            def _(pool):
                pool.wait_ge(w_in.sem, w_in.at(32))
                for t in range(NT):
                    pool.tensor_tensor(c.x[:, t, :], c.x[:, t, :], bb[:, :], ALU.add).then_inc(biased.sem, 1)

            @block.tensor
            def _(pe):
                def turn(t):
                    if t >= 2:
                        pe.wait_ge(copied.sem, copied.at(t - 1))
                    for k in range(blocks):
                        last = pe.transpose(ps[:, 2 * (t % 2) + k // 4, P * (k % 4):P * (k % 4) + P],
                                            o_tok[:, t, P * k:P * k + P], c.ident[:, :])
                    last.then_inc(turned.sem, 1)
                pe.wait_ge(w_in.sem, w_in.at(32))
                turn(0)
                for t in range(NT):
                    if t + 1 < NT:
                        turn(t + 1)
                    pe.wait_ge(copied.sem, copied.at(t + 1))
                    if t >= 2:
                        pe.wait_ge(added.sem, added.at(t - 1))
                    for k in range(blocks):
                        last = pe.matmul(ps[:, 4 + t % 2, 0:D], ot[:, t % 2, P * k:P * k + P], w[:, k, :],
                                         start=(k == 0), stop=(k == blocks - 1))
                    last.then_inc(mm.sem, 1)

            @block.scalar
            def _(act):
                for t in range(NT):
                    act.wait_ge(turned.sem, turned.at(t + 1))
                    if t >= 2:
                        act.wait_ge(mm.sem, mm.at(t - 1))
                    b = 2 * (t % 2)
                    act.activation(ot[:, t % 2, :],
                                              ps[:, b:b + banks, :].rearrange("p b s -> p (b s)")[:, 0:blocks * P],
                                              ACT.Copy).then_inc(copied.sem, 1)

            @block.vector
            def _(dve):
                for t in range(NT):
                    dve.wait_ge(mm.sem, mm.at(t + 1))
                    dve.wait_ge(biased.sem, biased.at(t + 1))
                    dve.tensor_tensor(c.x[:, t, :], ps[:, 4 + t % 2, 0:D], c.x[:, t, :], ALU.add).then_inc(added.sem, 1)
        for s, k in ((w_in, 32), (turned, NT), (copied, NT), (mm, NT), (added, NT), (biased, NT)):
            s.passed(k)


E8 = 8


class Route:

    def __init__(self, c, ctx, name, normalized, weight):
        self.c, self.normalized, self.weight = c, normalized, weight
        self.bias = c.sb(ctx, name + "_bias", [P, E8], F32)
        self.logits = c.sb(ctx, name + "_logits", [P, NT, E8], F32)
        self.exps = c.sb(ctx, name + "_exps", [P, NT, E8], F32)
        self.col = c.sb(ctx, name + "_col", [P, 4, NT], F32)
        self.top = c.sb(ctx, name + "_top", [P, NT, E8], F32)
        self.index = c.sb(ctx, name + "_index", [P, NT, E8], U32)
        self.index_f = c.sb(ctx, name + "_index_f", [P, NT, 2], F32)
        self.pick = c.sb(ctx, name + "_pick", [P, 2, NT, E8], F32)
        self.filled, self.shifted, self.exped, self.chain, self.weighted = (
            c.sig(k) for k in ("rt_logits", "rt_shifted", "rt_exp", "rt_chain", "rt_weighted"))
        self.bank = 7

    def tensor(self, pe, tokens, w):
        for t in range(NT):
            for k in range(KD):
                last = pe.matmul(self.c.ps[:, self.bank, E8 * t:E8 * t + E8], tokens[:, k, P * t:P * t + P],
                                 w[:, k, :], start=(k == 0), stop=(k == KD - 1))
        last.then_inc(self.filled.sem, 1)

    def scalar(self, act):
        act.wait_ge(self.shifted.sem, self.shifted.at(1))
        act.activation(self.exps[:, :, :], self.logits[:, :, :], ACT.Exp).then_inc(self.exped.sem, 1)

    def vector(self, dve):
        def rows(a):
            return a.unsqueeze(2).to_broadcast([P, NT, E8])
        link = Chain(self.chain)
        dve.wait_ge(self.filled.sem, self.filled.at(1))
        ps = self.c.ps[:, self.bank, 0:NT * E8].rearrange("p (t e) -> p t e", e=E8)
        dve.tensor_tensor(self.logits[:, :, :], ps, self.bias[:, :].unsqueeze(1).to_broadcast([P, NT, E8]),
                               ALU.add).then_inc(link.sem, 1)
        dve.wait_ge(link.sem, link.next())
        top, total, inverse, scale = (self.col[:, i, :] for i in range(4))
        dve.tensor_reduce(top, self.logits[:, :, :], AX.X, ALU.max).then_inc(link.sem, 1)
        dve.wait_ge(link.sem, link.next())
        dve.tensor_tensor(self.logits[:, :, :], self.logits[:, :, :], rows(top), ALU.subtract).then_inc(self.shifted.sem, 1)
        dve.wait_ge(self.exped.sem, self.exped.at(1))
        dve.tensor_reduce(total, self.exps[:, :, :], AX.X, ALU.add).then_inc(link.sem, 1)
        dve.wait_ge(link.sem, link.next())
        dve.reciprocal(inverse, total).then_inc(link.sem, 1)
        dve.wait_ge(link.sem, link.next())
        probs = self.logits
        dve.tensor_tensor(probs[:, :, :], self.exps[:, :, :], rows(inverse), ALU.mult).then_inc(link.sem, 1)
        dve.wait_ge(link.sem, link.next())
        for t in range(NT):
            dve.max(self.top[:, t, :], probs[:, t, :]).then_inc(self.chain.sem, 1)
        link.n += NT
        dve.wait_ge(self.chain.sem, self.chain.at(link.n))
        for t in range(NT):
            dve.max_index(self.index[:, t, :], self.top[:, t, :], probs[:, t, :]).then_inc(self.chain.sem, 1)
        link.n += NT
        dve.wait_ge(self.chain.sem, self.chain.at(link.n))
        dve.tensor_copy(self.index_f[:, :, :], self.index[:, :, 0:2]).then_inc(link.sem, 1)
        dve.wait_ge(link.sem, link.next())
        iota = self.c.iota[:, :].unsqueeze(1).to_broadcast([P, NT, E8])
        for j in range(2):
            dve.tensor_tensor(self.pick[:, j, :, :], iota, rows(self.index_f[:, :, j]), ALU.is_equal).then_inc(link.sem, 1)
            dve.wait_ge(link.sem, link.next())
            dve.tensor_tensor(self.pick[:, j, :, :], self.pick[:, j, :, :], rows(self.top[:, :, j]), ALU.mult).then_inc(link.sem, 1)
            dve.wait_ge(link.sem, link.next())
        last = dve.tensor_tensor(self.weight[:, :, :], self.pick[:, 0, :, :], self.pick[:, 1, :, :], ALU.add)
        if self.normalized:
            last.then_inc(link.sem, 1)
            dve.wait_ge(link.sem, link.next())
            dve.tensor_tensor(total, self.top[:, :, 0], self.top[:, :, 1], ALU.add).then_inc(link.sem, 1)
            dve.wait_ge(link.sem, link.next())
            dve.reciprocal(scale, total).then_inc(link.sem, 1)
            dve.wait_ge(link.sem, link.next())
            last = dve.tensor_tensor(self.weight[:, :, :], self.weight[:, :, :], rows(scale), ALU.mult)
        last.then_inc(self.weighted.sem, 1)
        dve.wait_ge(self.weighted.sem, self.weighted.at(1))
        self.chained = link.n

    def done(self):
        for s, n in ((self.filled, 1), (self.shifted, 1), (self.exped, 1), (self.weighted, 1),
                     (self.chain, self.chained)):
            s.passed(n)


def ffn_shared(c):
    nc, ps = c.nc, c.ps
    NC, HB = N // 512, D // P
    with ExitStack() as ctx:
        ln = LayerNorm(c, ctx, "lnf0")
        route = Route(c, ctx, "rt0", False, c.sb(ctx, "rt0_weight", [P, NT, E8], F32))
        xt = c.sb(ctx, "f0_xt", [P, KD, N], F32)
        w1 = c.sb(ctx, "f0_w1", [P, 2, KD, 2 * D], F32)
        w_gate = c.sb(ctx, "f0_gate", [P, KD, E8], F32)
        w2 = c.sb(ctx, "f0_w2", [P, HB, (E8 + 1) * D], F32)
        w2_high = c.sb(ctx, "f0_w2_high", [P, HB, (E8 + 1) * D], F32R)
        w2_low = c.sb(ctx, "f0_w2_low", [P, HB, (E8 + 1) * D], F32R)
        silu = c.sb(ctx, "f0_silu", [P, 2, 512], F32)
        full = c.sb(ctx, "f0_full", [P, 2, 512], F32)
        hid = c.sb(ctx, "f0_hid", [P, 2, 2, HB, 2, 512], F32R)
        w_in, w2_in, w2_h, w2_l = (c.sig(k) for k in ("w_in", "f0_w2_in", "f0_w2_high", "f0_w2_low"))
        pair, s_silu, s_full, s_high, s_low, out, added = (
            c.sig(k) for k in ("f0_pair", "f0_silu", "f0_full", "f0_high", "f0_low", "f0_out", "f0_added"))
        loads = 2 * KD + KD + 1
        pairs = [(g, net, m) for g in range(NC) for net in range(2) for m in range(HB)]
        ppg, OUTS = 2 * HB, E8 // 2 + 1
        with nc.Block() as block:
            @block.sync
            def _(sp):
                for k in range(KD):
                    sp.dma_start(w_gate[:, k, :], c.arg["L0_ffn_w_gate"][P * k:P * k + P, :]).then_inc(w_in.sem, 16)
                    for net, name in enumerate(("L0_ffn_w_shared_in", "L0_ffn_w1_shared")):
                        sp.dma_start(w1[:, net, k, :], c.arg[name][P * k:P * k + P, :]).then_inc(w_in.sem, 16)
                sp.dma_start(route.bias[:, :], c.arg["L0_ffn_gate_bias"].rearrange("(a b) -> a b", a=1)
                                      .partition_broadcast(P)).then_inc(w_in.sem, 16)
                for k in range(HB):
                    sp.dma_start(w2[:, k, 0:E8 * D].rearrange("p (e n) -> p e n", e=E8),
                                           c.arg["L0_ffn_w2"].rearrange("e (k p) n -> k p e n", p=P)[k]).then_inc(w2_in.sem, 16)
                    sp.dma_start(w2[:, k, E8 * D:], c.arg["L0_ffn_w_shared_out"][P * k:P * k + P, :]).then_inc(w2_in.sem, 16)

            @block.tensor
            def _(pe):
                ln.tensor(pe)
                pe.wait_ge(w_in.sem, w_in.at(16 * loads))
                ln.wait_xt(pe, NC - 1)
                route.tensor(pe, xt, w_gate)

                def hidden(g):
                    for n in range(ppg * g, ppg * g + ppg):
                        _, net, m = pairs[n]
                        if n >= 2:
                            pe.wait_ge(s_full.sem, s_full.at(n - 1))
                        for half in range(2):
                            for k in range(KD):
                                last = pe.matmul(ps[:, 2 * (n % 2) + half, :],
                                                 w1[:, net, k, D * half + P * m:D * half + P * m + P],
                                                 xt[:, k, 512 * g:512 * g + 512], start=(k == 0), stop=(k == KD - 1))
                        last.then_inc(pair.sem, 1)

                def outputs(g):
                    pe.wait_ge(s_low.sem, s_low.at(ppg * (g + 1)))
                    if g == 0:
                        pe.wait_ge(w2_h.sem, w2_h.at(HB))
                        pe.wait_ge(w2_l.sem, w2_l.at(HB))
                        pe.wait_ge(route.shifted.sem, route.shifted.at(1))
                    for t in range(4):
                        cols = slice(P * t, P * t + P)
                        for q in range(OUTS):
                            n = OUTS * (4 * g + t) + q
                            if n >= 4:
                                pe.wait_ge(added.sem, added.at(n - 3))
                            net, w = (1, 2 * D) if q < OUTS - 1 else (0, D)
                            w0 = 2 * D * q
                            terms = [(m, part, wt) for m in range(HB)
                                     for part, wt in ((0, w2_high), (1, w2_high), (0, w2_low))]
                            for i, (m, part, wt) in enumerate(terms):
                                last = pe.matmul(ps[:, 4 + n % 4, 0:w], hid[:, g % 2, net, m, part, cols],
                                                 wt[:, m, w0:w0 + w], start=(i == 0), stop=(i == len(terms) - 1))
                            last.then_inc(out.sem, 1)

                hidden(0)
                for g in range(NC):
                    if g + 1 < NC:
                        hidden(g + 1)
                    outputs(g)

            @block.scalar
            def _(act):
                ln.scalar(act)
                ln.scalar_xt(act, xt)
                route.scalar(act)
                act.wait_ge(w2_in.sem, w2_in.at(16 * 2 * HB))
                for k in range(HB):
                    act.activation(w2_high[:, k, :], w2[:, k, :], ACT.Copy).then_inc(w2_h.sem, 1)

                def high(n):
                    g, net, m = pairs[n]
                    if n % ppg == 0 and g >= 2:
                        act.wait_ge(out.sem, out.at(4 * OUTS * (g - 1)))
                    act.wait_ge(s_full.sem, s_full.at(n + 1))
                    act.activation(hid[:, g % 2, net, m, 0, :], full[:, n % 2, :], ACT.Copy).then_inc(s_high.sem, 1)
                for n in range(len(pairs)):
                    act.wait_ge(pair.sem, pair.at(n + 1))
                    if n >= 2:
                        act.wait_ge(s_full.sem, s_full.at(n - 1))
                    act.activation(silu[:, n % 2, :], ps[:, 2 * (n % 2), :], ACT.Silu).then_inc(s_silu.sem, 1)
                    if n % ppg:
                        high(n - 1)
                    if n % ppg == ppg - 1:
                        high(n)

            @block.vector
            def _(dve):
                ln.vector(dve)
                ln.vector_xt(dve, xt)
                dve.wait_ge(w_in.sem, w_in.at(16 * loads))
                route.vector(dve)

                def low(n):
                    g, net, m = pairs[n]
                    dve.wait_ge(s_high.sem, s_high.at(n + 1))
                    dve.tensor_tensor(hid[:, g % 2, net, m, 1, :], full[:, n % 2, :],
                                                hid[:, g % 2, net, m, 0, :].bitcast(F32), ALU.subtract).then_inc(s_low.sem, 1)

                def hidden(g):
                    for n in range(ppg * g, ppg * g + ppg):
                        dve.wait_ge(s_silu.sem, s_silu.at(n + 1))
                        if n >= 2:
                            dve.wait_ge(s_low.sem, s_low.at(n - 1))
                        dve.tensor_tensor(full[:, n % 2, :], silu[:, n % 2, :], ps[:, 2 * (n % 2) + 1, :],
                                                     ALU.mult).then_inc(s_full.sem, 1)
                        if n > ppg * g:
                            low(n - 1)
                    low(ppg * g + ppg - 1)

                def outputs(g):
                    for t in range(4 * g, 4 * g + 4):
                        x = c.x[:, t, :]
                        for q in range(OUTS):
                            n = OUTS * t + q
                            dve.wait_ge(out.sem, out.at(n + 1))
                            o = ps[:, 4 + n % 4, :]
                            if q == OUTS - 1:
                                dve.tensor_tensor(x, o[:, 0:D], x, ALU.add).then_inc(added.sem, 1)
                            else:
                                dve.scalar_tensor_tensor(x, o[:, 0:D], route.weight[:, t, 2 * q:2 * q + 1], x,
                                                               ALU.mult, ALU.add).then_inc(chain.sem, 1)
                                dve.wait_ge(chain.sem, chain.next())
                                dve.scalar_tensor_tensor(x, o[:, D:2 * D],
                                                                   route.weight[:, t, 2 * q + 1:2 * q + 2], x,
                                                                   ALU.mult, ALU.add).then_inc(added.sem, 1)
                            dve.wait_ge(added.sem, added.at(n + 1))

                dve.wait_ge(w2_in.sem, w2_in.at(16 * 2 * HB))
                for k in range(HB):
                    dve.wait_ge(w2_h.sem, w2_h.at(k + 1))
                    dve.tensor_tensor(w2_low[:, k, :], w2[:, k, :], w2_high[:, k, :].bitcast(F32),
                                               ALU.subtract).then_inc(w2_l.sem, 1)
                chain = Chain(c.sig("f0_chain"))
                hidden(0)
                for g in range(NC):
                    if g + 1 < NC:
                        hidden(g + 1)
                    outputs(g)
        ln.done()
        route.done()
        np_, no = len(pairs), NT * OUTS
        for s, k in ((w_in, 16 * loads), (w2_in, 32 * HB), (w2_h, HB), (w2_l, HB), (pair, np_), (s_silu, np_),
                     (s_full, np_), (s_high, np_), (s_low, np_), (out, no), (added, no)):
            s.passed(k)


ROUND = 1.5 * 2 ** 23


def quantize_weights(c, ctx):
    nc, ps = c.nc, c.ps
    names = ("w_i", "w_f", "w_g", "w_o")
    NW, EB = len(names), D // P
    wt = c.sb(ctx, "hg_wt", [P, NW, KD, D], BF16)
    unit = c.sb(ctx, "hg_unit", [P, NW], F32)
    with ExitStack() as tmp:
        w = c.sb(tmp, "hg_w", [P, NW, EB, D], F32)
        wq = c.sb(tmp, "hg_wq", [P, NW, EB, D], BF16)
        ones = c.sb(tmp, "hg_ones", [P, P], F32)
        total = c.sb(tmp, "hg_total", [P, NW], F32)
        inverse = c.sb(tmp, "hg_inverse", [P, NW], F32)
        w_in, chain, totals, summed, quant, turned, copied = (c.sig(k) for k in (
            "w_in", "hw_chain", "hw_totals", "hw_summed", "hw_quant", "hw_turned", "hw_copied"))
        with nc.Block() as block:
            @block.sync
            def _(sp):
                for i, name in enumerate(names):
                    sp.dma_start(w[:, i, :, :], c.arg["L1_attn_" + name].rearrange("(b p) d -> p b d", p=P)).then_inc(w_in.sem, 16)

            @block.tensor
            def _(pe):
                pe.wait_ge(totals.sem, totals.at(2))
                pe.matmul(ps[:, 0, 0:NW], ones[:, :], total[:, :], start=True, stop=True).then_inc(summed.sem, 1)
                pe.wait_ge(quant.sem, quant.at(1))
                for i in range(NW):
                    for k in range(KD):
                        for e in range(EB):
                            last = pe.transpose(ps[:, 1 + i, :].bitcast(BF16)[:, D * k + P * e:D * k + P * e + P],
                                                wq[:, i, e, P * k:P * k + P], c.identb[:, :])
                    last.then_inc(turned.sem, 1)

            @block.scalar
            def _(act):
                for i in range(NW):
                    act.wait_ge(turned.sem, turned.at(i + 1))
                    act.activation(wt[:, i, :, :].rearrange("p k e -> p (k e)"),
                                              ps[:, 1 + i, :].bitcast(BF16)[:, 0:KD * D], ACT.Copy).then_inc(copied.sem, 1)

            @block.vector
            def _(dve):
                link = Chain(chain)
                dve.memset(ones[:, :], 1.0).then_inc(totals.sem, 1)
                dve.wait_ge(w_in.sem, w_in.at(16 * NW))
                flat = w[:, :, :, :].rearrange("p i b d -> p i (b d)")
                dve.tensor_reduce(total[:, :], flat, AX.X, ALU.add, apply_absolute_value=True).then_inc(totals.sem, 1)
                dve.wait_ge(summed.sem, summed.at(1))
                dve.tensor_scalar(unit[:, :], ps[:, 0, 0:NW], 1.0 / (D * D), 1e-5, ALU.mult, ALU.max).then_inc(link.sem, 1)
                dve.wait_ge(link.sem, link.next())
                dve.reciprocal(inverse[:, :], unit[:, :]).then_inc(link.sem, 1)
                dve.wait_ge(link.sem, link.next())
                for i in range(NW):
                    dve.tensor_scalar(flat[:, i, :], flat[:, i, :], inverse[:, i:i + 1], ROUND,
                                                ALU.mult, ALU.add).then_inc(chain.sem, 1)
                link.n += NW
                dve.wait_ge(chain.sem, chain.at(link.n))
                dve.tensor_scalar(flat, flat, ROUND, 1.0, ALU.subtract, ALU.min).then_inc(link.sem, 1)
                dve.wait_ge(link.sem, link.next())
                dve.tensor_scalar(wq[:, :, :, :].rearrange("p i b d -> p i (b d)"), flat, -1.0, None,
                                            ALU.max).then_inc(quant.sem, 1)
                c.chained = link.n
    for s, k in ((w_in, 16 * NW), (chain, c.chained), (totals, 2), (summed, 1), (quant, 1), (turned, NW),
                 (copied, NW)):
        s.passed(k)
    return wt, unit


class Rms:

    def __init__(self, c, ctx, name):
        self.sum = c.sb(ctx, name + "_sum", [P, NT], F32)
        self.mean = c.sb(ctx, name + "_mean", [P, NT], F32)
        self.root = c.sb(ctx, name + "_root", [P, NT], F32)
        self.inverse = c.sb(ctx, name + "_inverse", [P, NT], F32)
        self.square = c.sb(ctx, name + "_square", [P, 2, D], F32)
        self.squared, self.meaned, self.rooted, self.inverted = (c.sig(name + k) for k in (
            "_squared", "_meaned", "_rooted", "_inverted"))

    def scalar(self, act, src, ready):
        for t in range(NT):
            ready(act, t)
            if t >= 2:
                act.wait_ge(self.squared.sem, self.squared.at(t - 1))
            act.activation(self.square[:, t % 2, :], src(t), ACT.Square,
                                            accum_out=self.sum[:, t:t + 1]).then_inc(self.squared.sem, 1)
        act.wait_ge(self.meaned.sem, self.meaned.at(1))
        act.activation(self.root[:, :], self.mean[:, :], ACT.Sqrt).then_inc(self.rooted.sem, 1)

    def vector(self, dve):
        dve.wait_ge(self.squared.sem, self.squared.at(NT))
        dve.tensor_scalar(self.mean[:, :], self.sum[:, :], 1.0 / D, EPS, ALU.mult, ALU.add).then_inc(self.meaned.sem, 1)
        dve.wait_ge(self.rooted.sem, self.rooted.at(1))
        dve.reciprocal(self.inverse[:, :], self.root[:, :]).then_inc(self.inverted.sem, 1)
        dve.wait_ge(self.inverted.sem, self.inverted.at(1))

    def done(self):
        for s, k in ((self.squared, NT), (self.meaned, 1), (self.rooted, 1), (self.inverted, 1)):
            s.passed(k)


class BitInput:

    def __init__(self, c, ctx, name, weights, units):
        self.c, self.name, self.weights, self.units = c, name, weights, units
        self.nw = nw = len(weights)
        self.rms = Rms(c, ctx, name + "_rms")
        self.norm = c.sb(ctx, name + "_norm", [P, nw, D], F32)
        self.y = c.sb(ctx, name + "_y", [P, NT, nw, D], F32)
        self.top = c.sb(ctx, name + "_top", [P, NT, nw], F32)
        self.scale = c.sb(ctx, name + "_scale", [P, NT, nw], F32)
        self.unit = c.sb(ctx, name + "_unit", [P, NT, nw], F32)
        self.q = c.sb(ctx, name + "_q", [P, 2, nw, D], BF16)
        self.qt = c.sb(ctx, name + "_qt", [P, 2, nw * KD * P], BF16)
        self.norm_in, self.chain, self.steps, self.clipped, self.ints, self.turned, self.copied = (
            c.sig(name + k) for k in ("_norm_in", "_chain", "_steps", "_clipped", "_ints", "_turned", "_copied"))

    def load(self, sp):
        for i, w in enumerate(self.weights):
            sp.dma_start(self.norm[:, i, :], self.c.arg[w].rearrange("(a b) -> a b", a=1)
                                          .partition_broadcast(P)).then_inc(self.norm_in.sem, 16)

    def vector(self, dve, src):
        link = Chain(self.chain)
        self.rms.vector(dve)
        dve.wait_ge(self.norm_in.sem, self.norm_in.at(16 * self.nw))
        nw = self.nw
        for t in range(NT):
            for i in range(nw):
                dve.scalar_tensor_tensor(self.y[:, t, i, :], src(t), self.rms.inverse[:, t:t + 1],
                                                        self.norm[:, i, :], ALU.mult, ALU.mult).then_inc(self.steps.sem, 1)
        for t in range(NT):
            dve.wait_ge(self.steps.sem, self.steps.at(nw * (t + 1)))
            dve.tensor_reduce(self.top[:, t, :], self.y[:, t, :, :], AX.X, ALU.max,
                                             apply_absolute_value=True).then_inc(self.chain.sem, 1)
        link.n += NT
        dve.wait_ge(self.chain.sem, self.chain.at(link.n))
        dve.tensor_scalar(self.top[:, :, :], self.top[:, :, :], 1e-5, 1.0 / 127.0, ALU.max, ALU.mult).then_inc(link.sem, 1)
        dve.wait_ge(link.sem, link.next())
        dve.reciprocal(self.scale[:, :, :], self.top[:, :, :]).then_inc(link.sem, 1)
        dve.wait_ge(link.sem, link.next())
        dve.tensor_tensor(self.unit[:, :, :], self.top[:, :, :],
                               self.units.unsqueeze(1).to_broadcast([P, NT, nw]), ALU.mult).then_inc(link.sem, 1)
        dve.wait_ge(link.sem, link.next())
        for t in range(NT):
            for i in range(nw):
                dve.tensor_scalar(self.y[:, t, i, :], self.y[:, t, i, :], self.scale[:, t, i:i + 1],
                                                 ROUND, ALU.mult, ALU.add).then_inc(self.steps.sem, 1)
            dve.wait_ge(self.steps.sem, self.steps.at(nw * (NT + t + 1)))
            dve.tensor_scalar(self.y[:, t, :, :], self.y[:, t, :, :], ROUND - 128.0, ROUND + 127.0,
                                               ALU.max, ALU.min).then_inc(self.clipped.sem, 1)
        self.chained = link.n

    def pool_ints(self, pool):
        for t in range(NT):
            pool.wait_ge(self.clipped.sem, self.clipped.at(t + 1))
            if t >= 2:
                pool.wait_ge(self.turned.sem, self.turned.at(t - 1))
            pool.tensor_scalar(self.q[:, t % 2, :, :], self.y[:, t, :, :], ROUND, None, ALU.subtract).then_inc(self.ints.sem, 1)

    def turn(self, pe, t, bank):
        pe.wait_ge(self.ints.sem, self.ints.at(t + 1))
        if t >= 1:
            pe.wait_ge(self.copied.sem, self.copied.at(t))
        out = self.c.ps[:, bank, :].bitcast(BF16)
        for i in range(self.nw):
            for k in range(KD):
                j = P * (KD * i + k)
                last = pe.transpose(out[:, j:j + P], self.q[:, t % 2, i, P * k:P * k + P], self.c.identb[:, :])
        last.then_inc(self.turned.sem, 1)

    def copy(self, act, t, bank):
        act.wait_ge(self.turned.sem, self.turned.at(t + 1))
        act.activation(self.qt[:, t % 2, :],
                                       self.c.ps[:, bank, :].bitcast(BF16)[:, 0:self.nw * KD * P], ACT.Copy).then_inc(self.copied.sem, 1)

    def part(self, t, i, k):
        j = P * (KD * i + k)
        return self.qt[:, t % 2, j:j + P]

    def done(self):
        self.rms.done()
        for s, k in ((self.norm_in, 16 * self.nw), (self.chain, self.chained), (self.steps, 2 * NT * self.nw),
                     (self.clipped, NT), (self.ints, NT), (self.turned, NT), (self.copied, NT)):
            s.passed(k)


def recurrent(c):
    with ExitStack() as ctx:
        wt, unit = quantize_weights(c, ctx)
        gate = c.sb(ctx, "hg_gate", [P, NT, D], F32)
        h = c.sb(ctx, "hg_h", [P, KD, N], F32)
        recur(c, wt, unit, gate, h)
        recur_out(c, wt, unit, gate, h)


def recur(c, wt, unit, gate, h):
    nc, ps = c.nc, c.ps
    TURN, GATE, FI, SCAN = 0, 1, 2, 4
    with ExitStack() as ctx:
        ln = LayerNorm(c, ctx, "lnr")
        bits = BitInput(c, ctx, "bi", ("L1_attn_nw_i", "L1_attn_nw_f", "L1_attn_nw_g"), unit[:, 0:3])
        forget = c.sb(ctx, "hg_forget", [P, 2, D], F32)
        keep = c.sb(ctx, "hg_keep", [P, 2, D], F32)
        sig_g = c.sb(ctx, "hg_sig_g", [P, 2, D], F32)
        new = c.sb(ctx, "hg_new", [P, 2, D], F32)
        forget_t = c.sb(ctx, "hg_forget_t", [P, 2, KD * 2 * P], F32)
        mm, s_forget, s_keep, s_gate, s_new, turned, s_forget_t, scanned = (c.sig(k) for k in (
            "hg_mm", "hg_forget", "hg_keep", "hg_gate", "hg_new", "hg_turned", "hg_forget_t", "hg_scanned"))
        with nc.Block() as block:
            @block.sync
            def _(sp):
                bits.load(sp)

            @block.gpsimd
            def _(pool):
                bits.pool_ints(pool)

            @block.tensor
            def _(pe):
                def turn_out(t):
                    pe.wait_ge(s_new.sem, s_new.at(t + 1))
                    pair = t // 2
                    if t % 2 == 0 and pair >= 2:
                        pe.wait_ge(scanned.sem, scanned.at(KD * (pair - 1)))
                    for i, src in enumerate((forget, new)):
                        for k in range(KD):
                            col = 2 * P * k + P * (t % 2)
                            last = pe.transpose(ps[:, SCAN + 2 * (pair % 2) + i, col:col + P],
                                                src[:, t % 2, P * k:P * k + P], c.ident[:, :])
                    last.then_inc(turned.sem, 1)

                bits.turn(pe, 0, TURN)
                for t in range(NT):
                    pe.wait_ge(bits.copied.sem, bits.copied.at(t + 1))
                    if t >= 2:
                        pe.wait_ge(s_new.sem, s_new.at(t - 1))
                    for i, out in ((1, ps[:, FI + t % 2, 0:D]), (0, ps[:, FI + t % 2, D:2 * D]),
                                   (2, ps[:, GATE, 0:D])):
                        if i == 2 and t:
                            pe.wait_ge(s_gate.sem, s_gate.at(2 * t))
                        for k in range(KD):
                            last = pe.matmul(out, bits.part(t, i, k), wt[:, i, k, :], start=(k == 0),
                                             stop=(k == KD - 1))
                        last.then_inc(mm.sem, 1)
                    if t + 1 < NT:
                        bits.turn(pe, t + 1, TURN)
                    if t >= 1:
                        turn_out(t - 1)
                turn_out(NT - 1)

            @block.scalar
            def _(act):
                ln.scalar(act)

                def ready(eng, t):
                    eng.wait_ge(ln.s["xn"].sem, ln.s["xn"].at(t + 1))
                bits.rms.scalar(act, lambda t: ln.xn[:, t, :], ready)
                bits.copy(act, 0, TURN)

                def copy_forget(pair):
                    act.wait_ge(turned.sem, turned.at(2 * pair + 2))
                    if pair >= 2:
                        act.wait_ge(scanned.sem, scanned.at(KD * (pair - 1)))
                    act.activation(forget_t[:, pair % 2, :], ps[:, SCAN + 2 * (pair % 2), :],
                                                  ACT.Copy).then_inc(s_forget_t.sem, 1)
                for t in range(NT):
                    act.wait_ge(mm.sem, mm.at(3 * t + 2))
                    if t >= 2:
                        act.wait_ge(turned.sem, turned.at(t - 1))
                        act.wait_ge(s_gate.sem, s_gate.at(2 * (t - 1)))
                    act.activation(forget[:, t % 2, :], ps[:, FI + t % 2, 0:D], ACT.Sigmoid,
                                                scale=bits.unit[:, t, 1:2]).then_inc(s_forget.sem, 1)
                    act.wait_ge(mm.sem, mm.at(3 * t + 3))
                    act.activation(sig_g[:, t % 2, :], ps[:, GATE, 0:D],
                                              ACT.Sigmoid, scale=bits.unit[:, t, 2:3]).then_inc(s_gate.sem, 1)
                    if t + 1 < NT:
                        bits.copy(act, t + 1, TURN)
                    if t % 2 == 0 and t >= 2:
                        copy_forget(t // 2 - 1)
                copy_forget(NT // 2 - 1)

            @block.vector
            def _(dve):
                ln.vector(dve)
                dve.wait_ge(ln.s["xn"].sem, ln.s["xn"].at(NT))
                bits.vector(dve, lambda t: ln.xn[:, t, :])

                def scan(pair):
                    dve.wait_ge(s_forget_t.sem, s_forget_t.at(pair + 1))
                    t = 2 * pair
                    if pair:
                        dve.wait_ge(scanned.sem, scanned.at(KD * pair))
                    for k in range(KD):
                        bank = SCAN + 2 * (pair % 2)
                        first = 0.0 if t % ST == 0 else h[:, k, P * t - 1:P * t]
                        dve.tensor_tensor_scan(h[:, k, P * t:P * t + 2 * P],
                                                           forget_t[:, pair % 2, 2 * P * k:2 * P * k + 2 * P],
                                                           ps[:, bank + 1, 2 * P * k:2 * P * k + 2 * P],
                                                           first, ALU.mult, ALU.add).then_inc(scanned.sem, 1)
                for t in range(NT):
                    dve.wait_ge(s_forget.sem, s_forget.at(t + 1))
                    if t >= 2:
                        dve.wait_ge(s_new.sem, s_new.at(t - 1))
                    dve.tensor_scalar(keep[:, t % 2, :], forget[:, t % 2, :], -1.0, 1.0, ALU.mult,
                                                 ALU.add).then_inc(s_keep.sem, 1)
                    dve.wait_ge(s_gate.sem, s_gate.at(2 * t + 1))
                    dve.scalar_tensor_tensor(gate[:, t, :], ps[:, GATE, 0:D],
                                                        bits.unit[:, t, 2:3], sig_g[:, t % 2, :], ALU.mult, ALU.mult).then_inc(s_gate.sem, 1)
                    dve.wait_ge(s_keep.sem, s_keep.at(t + 1))
                    if t >= 2:
                        dve.wait_ge(turned.sem, turned.at(t - 1))
                    dve.scalar_tensor_tensor(new[:, t % 2, :], ps[:, FI + t % 2, D:2 * D],
                                                       bits.unit[:, t, 0:1], keep[:, t % 2, :], ALU.mult, ALU.mult).then_inc(s_new.sem, 1)
                    if t % 2 == 1 and t >= 3:
                        scan((t - 3) // 2)
                scan(NT // 2 - 1)
        ln.done(turned=False)
        bits.done()
        for s, k in ((mm, 3 * NT), (s_forget, NT), (s_keep, NT), (s_gate, 2 * NT), (s_new, NT), (turned, NT),
                     (s_forget_t, NT // 2), (scanned, KD * NT // 2)):
            s.passed(k)


def recur_out(c, wt, unit, gate, h):
    nc, ps = c.nc, c.ps
    with ExitStack() as ctx:
        rms = Rms(c, ctx, "rh")
        bits = BitInput(c, ctx, "bo", ("L1_attn_nw_o",), unit[:, 3:4])
        norm = c.sb(ctx, "hg_norm", [P, D], F32)
        y = c.sb(ctx, "hg_y", [P, NT, D], F32)
        n_in, turned, normed, gated, mm, added = (c.sig(k) for k in ("ho_norm", "ho_turned", "ho_normed", "ho_gated",
                                                                     "ho_mm", "ho_added"))

        def out_t(t):
            return ps[:, t // 2, D * (t % 2):D * (t % 2) + D]
        with nc.Block() as block:
            @block.sync
            def _(sp):
                sp.dma_start(norm[:, :], c.arg["L1_attn_g_norm_w"].rearrange("(a b) -> a b", a=1)
                                      .partition_broadcast(P)).then_inc(n_in.sem, 16)
                bits.load(sp)

            @block.gpsimd
            def _(pool):
                bits.pool_ints(pool)

            @block.tensor
            def _(pe):
                for t in range(NT):
                    for k in range(KD):
                        last = pe.transpose(out_t(t)[:, P * k:P * k + P], h[:, k, P * t:P * t + P], c.ident[:, :])
                    last.then_inc(turned.sem, 1)
                pe.wait_ge(normed.sem, normed.at(NT))
                bits.turn(pe, 0, 0)
                for t in range(NT):
                    pe.wait_ge(bits.copied.sem, bits.copied.at(t + 1))
                    if t >= 2:
                        pe.wait_ge(added.sem, added.at(t - 1))
                    for k in range(KD):
                        last = pe.matmul(ps[:, 1 + t % 2, 0:D], bits.part(t, 0, k), wt[:, 3, k, :], start=(k == 0),
                                         stop=(k == KD - 1))
                    last.then_inc(mm.sem, 1)
                    if t + 1 < NT:
                        bits.turn(pe, t + 1, 0)

            @block.scalar
            def _(act):
                rms.scalar(act, out_t, lambda eng, t: eng.wait_ge(turned.sem, turned.at(2 * (t // 2) + 2)))
                bits.rms.scalar(act, lambda t: y[:, t, :], lambda eng, t: eng.wait_ge(gated.sem, gated.at(t + 1)))
                for t in range(NT):
                    if t >= 2:
                        act.wait_ge(mm.sem, mm.at(t - 1))
                    bits.copy(act, t, 0)

            @block.vector
            def _(dve):
                rms.vector(dve)
                dve.wait_ge(n_in.sem, n_in.at(16))
                for t in range(NT):
                    dve.scalar_tensor_tensor(y[:, t, :], out_t(t), rms.inverse[:, t:t + 1], norm[:, :],
                                                        ALU.mult, ALU.mult).then_inc(normed.sem, 1)
                for t in range(NT):
                    dve.wait_ge(normed.sem, normed.at(t + 1))
                    dve.tensor_tensor(y[:, t, :], y[:, t, :], gate[:, t, :], ALU.mult).then_inc(gated.sem, 1)
                dve.wait_ge(gated.sem, gated.at(NT))
                bits.vector(dve, lambda t: y[:, t, :])
                for t in range(NT):
                    dve.wait_ge(mm.sem, mm.at(t + 1))
                    x = c.x[:, t, :]
                    dve.scalar_tensor_tensor(x, ps[:, 1 + t % 2, 0:D], bits.unit[:, t, 0:1], x, ALU.mult,
                                                       ALU.add).then_inc(added.sem, 1)
        rms.done()
        bits.done()
        for s, k in ((n_in, 16), (turned, NT), (normed, NT), (gated, NT), (mm, NT), (added, NT)):
            s.passed(k)


DM = 1024
HB = DM // P
NG = N // 512


def moe(c):
    with ExitStack() as ctx:
        acc = c.sb(ctx, "moe_acc", [P, NT, D], F32)
        with ExitStack() as inner:
            h = c.sb(inner, "moe_h", [P, KD, 2, N], F32R)
            bias = c.sb(inner, "moe_bias", [P, E8 * HB + KD], F32)
            weight = c.sb(inner, "rt1_weight", [P, NT, E8], F32)
            moe_prepare(c, h, bias, weight, acc)
            moe_experts(c, h, bias, weight, acc)
        project_out(c, "po_moe", acc, KD, c.arg["L1_ffn_W_out"], c.arg["L1_ffn_b_out"])


def moe_prepare(c, h, bias, weight, acc):
    nc, ps = c.nc, c.ps
    NB = E8 * HB + KD
    with ExitStack() as ctx:
        ln = LayerNorm(c, ctx, "lnm")
        route = Route(c, ctx, "rt1", True, weight)
        xt = c.sb(ctx, "mp_xt", [P, KD, N], F32)
        full = c.sb(ctx, "mp_full", [P, KD, N], F32)
        w = c.sb(ctx, "mp_w", [P, KD, D], F32)
        w_gate = c.sb(ctx, "mp_gate", [P, KD, E8], F32)
        bias_rows = c.sb(ctx, "mp_bias_rows", [NB, P], F32)
        b2 = c.sb(ctx, "mp_b2", [E8, D], F32)
        rt = c.sb(ctx, "mp_rt", [E8, N], F32)
        w_in, bturn, bset, mm, s_full, high, low, rturn, rset, started, set_ = (c.sig(k) for k in (
            "w_in", "mp_bturn", "mp_bset", "mp_mm", "mp_full", "mp_high", "mp_low", "mp_rturn", "mp_rset",
            "mp_start", "mp_set"))
        loads = 3 + 2 * KD + 1
        jobs = [(g, m) for g in range(NG) for m in range(KD)]
        with nc.Block() as block:
            @block.sync
            def _(sp):
                sp.dma_start(bias_rows[0:E8 * HB, :], c.arg["L1_ffn_b1"].rearrange("e (k p) -> (e k) p", p=P)).then_inc(w_in.sem, 16)
                sp.dma_start(bias_rows[E8 * HB:NB, :], c.arg["L1_ffn_b_in"].rearrange("(k p) -> k p", p=P)).then_inc(w_in.sem, 16)
                for k in range(KD):
                    sp.dma_start(w[:, k, :], c.arg["L1_ffn_W_in"][P * k:P * k + P, :]).then_inc(w_in.sem, 16)
                    sp.dma_start(w_gate[:, k, :], c.arg["L1_ffn_W_gate"][P * k:P * k + P, :]).then_inc(w_in.sem, 16)
                sp.dma_start(b2[:, :], c.arg["L1_ffn_b2"]).then_inc(w_in.sem, 16)
                sp.dma_start(route.bias[:, :], c.arg["L1_ffn_b_gate"].rearrange("(a b) -> a b", a=1)
                                      .partition_broadcast(P)).then_inc(w_in.sem, 16)

            @block.tensor
            def _(pe):
                ln.tensor(pe)
                pe.wait_ge(w_in.sem, w_in.at(16 * loads))
                ln.wait_xt(pe, NG - 1)
                pe.transpose(ps[:, 7, 0:NB], bias_rows[:, :], c.ident[0:NB, 0:NB]).then_inc(bturn.sem, 1)
                for n, (g, m) in enumerate(jobs):
                    if n >= 4:
                        pe.wait_ge(high.sem, high.at(n - 3))
                    for k in range(KD):
                        last = pe.matmul(ps[:, n % 4, :], w[:, k, P * m:P * m + P], xt[:, k, 512 * g:512 * g + 512],
                                         start=(k == 0), stop=(k == KD - 1))
                    last.then_inc(mm.sem, 1)
                pe.wait_ge(s_full.sem, s_full.at(len(jobs)))
                pe.wait_ge(bset.sem, bset.at(1))
                route.tensor(pe, full, w_gate)
                pe.wait_ge(high.sem, high.at(len(jobs)))
                pe.wait_ge(route.weighted.sem, route.weighted.at(1))
                for t in range(NT):
                    last = pe.transpose(ps[0:E8, t // 4, P * (t % 4):P * (t % 4) + P], route.weight[:, t, :],
                                        c.ident[:, :])
                last.then_inc(rturn.sem, 1)
                pe.wait_ge(rset.sem, rset.at(1))
                for t in range(NT):
                    if t >= 4:
                        pe.wait_ge(set_.sem, set_.at(t - 3))
                    pe.matmul(ps[:, 4 + t % 4, 0:D], rt[:, P * t:P * t + P], b2[:, :], start=True,
                                          stop=True).then_inc(started.sem, 1)

            @block.scalar
            def _(act):
                ln.scalar(act)
                ln.scalar_xt(act, xt)
                act.wait_ge(bset.sem, bset.at(1))
                for n, (g, m) in enumerate(jobs):
                    act.wait_ge(mm.sem, mm.at(n + 1))
                    cols = slice(512 * g, 512 * g + 512)
                    b = bias[:, E8 * HB + m:E8 * HB + m + 1]
                    act.activation(full[:, m, cols], ps[:, n % 4, :], ACT.Identity, bias=b).then_inc(s_full.sem, 1)
                    act.activation(h[:, m, 0, cols], ps[:, n % 4, :], ACT.Identity, bias=b).then_inc(high.sem, 1)
                route.scalar(act)
                act.wait_ge(rturn.sem, rturn.at(1))
                act.activation(rt[:, :], ps[0:E8, 0:4, :].rearrange("p b s -> p (b s)"), ACT.Copy).then_inc(rset.sem, 1)
                for t in range(NT):
                    act.wait_ge(started.sem, started.at(t + 1))
                    act.activation(acc[:, t, :], ps[:, 4 + t % 4, 0:D], ACT.Copy).then_inc(set_.sem, 1)

            @block.vector
            def _(dve):
                ln.vector(dve)
                ln.vector_xt(dve, xt)
                dve.wait_ge(bturn.sem, bturn.at(1))
                dve.tensor_copy(bias[:, :], ps[:, 7, 0:NB]).then_inc(bset.sem, 1)
                for n, (g, m) in enumerate(jobs):
                    dve.wait_ge(s_full.sem, s_full.at(n + 1))
                    dve.wait_ge(high.sem, high.at(n + 1))
                    cols = slice(512 * g, 512 * g + 512)
                    dve.tensor_tensor(h[:, m, 1, cols], full[:, m, cols], h[:, m, 0, cols].bitcast(F32),
                                              ALU.subtract).then_inc(low.sem, 1)
                route.vector(dve)
        ln.done()
        route.done()
        nj = len(jobs)
        for s, k in ((w_in, 16 * loads), (bturn, 1), (bset, 1), (mm, nj), (s_full, nj), (high, nj), (low, nj),
                     (rturn, 1), (rset, 1), (started, NT), (set_, NT)):
            s.passed(k)


def moe_experts(c, h, bias, weight, acc):
    nc, ps = c.nc, c.ps
    with ExitStack() as ctx:
        wide = 2 * DM
        chunk = c.sb(ctx, "me_chunk", [P, 2, DM], F32)
        w = c.sb(ctx, "me_w_parts", [P, 2, 2, 2, wide], F32R)
        full = c.sb(ctx, "me_full", [P, 2, 512], F32)
        mid = c.sb(ctx, "me_mid", [P, 2, HB, 2, 512], F32R)
        w_in = [c.sig("me_w_in0"), c.sig("me_w_in1")]
        w_high, w_low, mm, s_full, high, low, out, added = (c.sig(k) for k in (
            "me_w_high", "me_w_low", "me_mm", "me_full", "me_high", "me_low", "me_out", "me_added"))
        units = [(e, g) for e in range(E8) for g in range(NG)]
        nu = len(units)
        TERMS = ((0, 0), (1, 0), (0, 1))

        def part(e, q, i):
            return w[:, e % 2, q // 2, i, DM * (q % 2):DM * (q % 2) + DM]
        with nc.Block() as block:
            @block.sync
            def _(sp):
                for n in range(4 * E8):
                    e, q = divmod(n, 4)
                    if n >= 2:
                        sp.wait_ge(w_low.sem, w_low.at(n - 1))
                    if q < 2:
                        src = c.arg["L1_ffn_W1"][e][P * q:P * q + P, :]
                        dst = chunk[:, n % 2, :]
                    else:
                        rows = DM // 2 * (q - 2)
                        src = c.arg["L1_ffn_W2"][e][rows:rows + DM // 2, :].rearrange("(k p) n -> p k n", p=P)
                        dst = chunk[:, n % 2, :].rearrange("p (k n) -> p k n", n=D)
                    sp.dma_start(dst, src).then_inc(w_in[n % 2].sem, 16)

            @block.tensor
            def _(pe):
                def hidden(u):
                    e, g = units[u]
                    if g == 0:
                        pe.wait_ge(w_low.sem, w_low.at(4 * e + 2))
                    for b in range(HB):
                        n = HB * u + b
                        if n >= 4:
                            pe.wait_ge(high.sem, high.at(n - 3))
                        terms = [(k, i, j) for k in range(KD) for i, j in TERMS]
                        for m, (k, i, j) in enumerate(terms):
                            last = pe.matmul(ps[:, n % 4, :], w[:, e % 2, 0, i, DM * k + P * b:DM * k + P * b + P],
                                             h[:, k, j, 512 * g:512 * g + 512], start=(m == 0),
                                             stop=(m == len(terms) - 1))
                        last.then_inc(mm.sem, 1)

                def outputs(u):
                    e, g = units[u]
                    if g == 0:
                        pe.wait_ge(w_low.sem, w_low.at(4 * e + 4))
                    pe.wait_ge(low.sem, low.at(HB * (u + 1)))
                    for t in range(4):
                        n = 4 * u + t
                        if n >= 4:
                            pe.wait_ge(added.sem, added.at(n - 3))
                        terms = [(b, i, j) for b in range(HB) for i, j in TERMS]
                        for m, (b, i, j) in enumerate(terms):
                            last = pe.matmul(ps[:, 4 + t, 0:D], mid[:, u % 2, b, i, P * t:P * t + P],
                                             w[:, e % 2, 1, j, D * b:D * b + D], start=(m == 0),
                                             stop=(m == len(terms) - 1))
                        last.then_inc(out.sem, 1)

                hidden(0)
                for u in range(nu):
                    if u + 1 < nu:
                        hidden(u + 1)
                    outputs(u)

            @block.scalar
            def _(act):
                def split(e, qs):
                    for q in qs:
                        n = 4 * e + q
                        act.wait_ge(w_in[n % 2].sem, w_in[n % 2].at(16 * (n // 2 + 1)))
                        if e >= 2:
                            act.wait_ge(out.sem, out.at(4 * NG * (e - 1)))
                        act.activation(part(e, q, 0), chunk[:, n % 2, :], ACT.Copy).then_inc(w_high.sem, 1)
                split(0, range(4))
                for u in range(nu):
                    e, g = units[u]
                    for b in range(HB):
                        n = HB * u + b
                        act.wait_ge(mm.sem, mm.at(n + 1))
                        if n >= 2:
                            act.wait_ge(low.sem, low.at(n - 1))
                        if b == 0 and u >= 2:
                            act.wait_ge(out.sem, out.at(4 * (u - 1)))
                        col = bias[:, HB * e + b:HB * e + b + 1]
                        act.activation(full[:, n % 2, :], ps[:, n % 4, :], ACT.Relu, bias=col).then_inc(s_full.sem, 1)
                        act.activation(mid[:, u % 2, b, 0, :], ps[:, n % 4, :], ACT.Relu, bias=col).then_inc(high.sem, 1)
                    if g in (1, 2) and e + 1 < E8:
                        split(e + 1, range(2 * g - 2, 2 * g))

            @block.vector
            def _(dve):
                def split(e, qs):
                    for q in qs:
                        n = 4 * e + q
                        dve.wait_ge(w_high.sem, w_high.at(n + 1))
                        dve.tensor_tensor(part(e, q, 1), chunk[:, n % 2, :], raw(part(e, q, 0)),
                                                    ALU.subtract).then_inc(w_low.sem, 1)

                def outputs(u):
                    e, g = units[u]
                    for t in range(4):
                        dve.wait_ge(out.sem, out.at(4 * u + t + 1))
                        if u >= NG:
                            dve.wait_ge(added.sem, added.at(4 * (u - NG) + t + 1))
                        a = acc[:, 4 * g + t, :]
                        dve.scalar_tensor_tensor(a, ps[:, 4 + t, 0:D],
                                                           weight[:, 4 * g + t, e:e + 1], a, ALU.mult, ALU.add).then_inc(added.sem, 1)
                split(0, range(4))
                for u in range(nu):
                    e, g = units[u]
                    for b in range(HB):
                        n = HB * u + b
                        dve.wait_ge(s_full.sem, s_full.at(n + 1))
                        dve.wait_ge(high.sem, high.at(n + 1))
                        dve.tensor_tensor(mid[:, u % 2, b, 1, :], full[:, n % 2, :],
                                                  mid[:, u % 2, b, 0, :].bitcast(F32), ALU.subtract).then_inc(low.sem, 1)
                    if g in (1, 2) and e + 1 < E8:
                        split(e + 1, range(2 * g - 2, 2 * g))
                    if u:
                        outputs(u - 1)
                outputs(nu - 1)
        for s, k in ((w_in[0], 32 * E8), (w_in[1], 32 * E8), (w_high, 4 * E8), (w_low, 4 * E8), (mm, HB * nu),
                     (s_full, HB * nu), (high, HB * nu), (low, HB * nu), (out, 4 * nu), (added, 4 * nu)):
            s.passed(k)


def store(c, out):
    nc = c.nc
    sent = c.sig("stored")
    with nc.Block() as block:
        @block.sync
        def _(sp):
            for b in range(4):
                sp.dma_start(out.rearrange("b (t p) d -> p (b t) d", p=P)[:, 4 * b:4 * b + 4, :],
                                      c.x[:, 4 * b:4 * b + 4, :]).then_inc(sent.sem, 16)
            sp.wait_ge(sent.sem, sent.at(64))


def build(nc, arg, out):
    def scratch(name, shape, dt):
        return nc.dram_tensor(name, shape, dt, kind="Internal").ap()

    with ExitStack() as ctx:
        c = Core(nc, ctx, arg)
        setup(c)
        with ExitStack() as with_context:
            ct = c.sb(with_context, "ct", [96, 2, B * M], F32)
            make_context(c, ct)
            self_layer(c, scratch)
            cross(c, 0, True, ct, scratch)
            ffn_shared(c)
            recurrent(c)
            cross(c, 1, False, ct, scratch)
        moe(c)
        store(c, out)


def self_layer(c, scratch):
    with ExitStack() as c0:
        o_tok = c.sb(c0, "o_tok0", [P, NT, D], F32)
        scr_q, scr_k = scratch("scr_q0", [PARTS, D, N], BF16), scratch("scr_k0", [PARTS, D, N], BF16)
        with ExitStack() as c1:
            v_all = c.sb(c1, "v_all0", [P, NT, H, VW], F32)
            project_self(c, v_all, scr_q, scr_k)
            SelfAttention(c, c1, v_all, scr_q, scr_k, o_tok).run()
        project_out(c, "po0", o_tok, KD, c.arg["L0_attn_Wout"], c.arg["L0_attn_bout"])


def cross(c, layer, wide, ct, scratch):
    width = 64 if wide else DH
    dt = F32 if wide else BF16
    parts = 2 if wide else PARTS
    with ExitStack() as c0:
        o_tok = c.sb(c0, f"o_tokx{layer}", [P, NT, H * width], F32)
        scr_q = scratch(f"scr_qx{layer}", [parts, H * width, N], dt)
        scr_k = scratch(f"scr_kx{layer}", [parts, H * width, B * M], dt)
        with ExitStack() as c1:
            v_all = c.sb(c1, f"v_allx{layer}", [MH, 2 * B, H, width + 1 if wide else VW], F32)
            project_cross(c, layer, wide, ct, v_all, scr_q, scr_k)
            CrossAttention(c, c1, wide, v_all, scr_q, scr_k, o_tok).run()
        project_out(c, f"pox{layer}", o_tok, H * width // P, c.arg[f"L{layer}_xattn_Wo"], c.arg[f"L{layer}_xattn_bo"])


_INS = [
    "x",
    "ctx_768",
    "L0_attn_Wqkv",
    "L0_attn_bqkv",
    "L0_attn_Wout",
    "L0_attn_bout",
    "L0_xattn_Wq",
    "L0_xattn_Wk",
    "L0_xattn_Wv",
    "L0_xattn_Wo",
    "L0_xattn_bo",
    "L0_ffn_w_shared_in",
    "L0_ffn_w_shared_out",
    "L0_ffn_w1_shared",
    "L0_ffn_w2",
    "L0_ffn_w_gate",
    "L0_ffn_gate_bias",
    "L1_attn_w_i",
    "L1_attn_w_f",
    "L1_attn_w_g",
    "L1_attn_w_o",
    "L1_attn_nw_i",
    "L1_attn_nw_f",
    "L1_attn_nw_g",
    "L1_attn_nw_o",
    "L1_attn_g_norm_w",
    "L1_xattn_Wq",
    "L1_xattn_bq",
    "L1_xattn_Wk",
    "L1_xattn_bk",
    "L1_xattn_Wv",
    "L1_xattn_bv",
    "L1_xattn_Wo",
    "L1_xattn_bo",
    "L1_ffn_W_in",
    "L1_ffn_b_in",
    "L1_ffn_W_gate",
    "L1_ffn_b_gate",
    "L1_ffn_W1",
    "L1_ffn_b1",
    "L1_ffn_W2",
    "L1_ffn_b2",
    "L1_ffn_W_out",
    "L1_ffn_b_out",
]


def kernel(**inputs):
    import numpy as _np
    import concourse.bacc as _bacc
    from concourse import mybir as _mybir
    from concourse.bass_utils import run_bass_kernel_spmd as _run

    nc = _bacc.Bacc("TRN2", target_bir_lowering=False, num_devices=1)
    arrays, arg = {}, {}
    for name in _INS:
        a = _np.ascontiguousarray(inputs[name])
        arrays[f"in_{name}_dram"] = a
        arg[name] = nc.dram_tensor(f"in_{name}_dram", a.shape, _mybir.dt.from_np(a.dtype), kind="ExternalInput").ap()
    out = nc.dram_tensor("out_0_dram", (B, S, D), F32, kind="ExternalOutput").ap()
    build(nc, arg, out)
    r = _run(nc, [arrays], core_ids=[0])
    return r.results[0]["out_0_dram"]
```

```python
from contextlib import ExitStack

import concourse.bass as bass
from concourse import mybir

ALU = mybir.AluOpType
ACT = mybir.ActivationFunctionType
AX = mybir.AxisListType
F32 = mybir.dt.float32
F32R = mybir.dt.float32r
BF16 = mybir.dt.bfloat16
U32 = mybir.dt.uint32

P = 128
B = 2
S = 1024
D = 256
N = B * S
NT = N // P
ST = S // P
KD = D // P
H = 16
DH = D // H
M = 154
MH = M // 2
DC = 192
EPS = 1e-5
MASKED = -1e30
VW = 32
HPU = 4
PARTS = 3
Q_ROWS = (0, 0, 1, 1, 0, 2)
K_ROWS = (0, 1, 0, 1, 2, 0)
KROWS = len(Q_ROWS) * DH + PARTS


def raw(ap):
    return ap.bitcast(F32) if ap.dtype == F32R else ap


class Signal:

    def __init__(self, sem):
        self.sem = sem
        self.base = 0

    def at(self, n):
        return self.base + n

    def passed(self, n):
        self.base += n


class Chain:

    def __init__(self, signal):
        self.sem, self.base, self.n = signal.sem, signal.base, 0

    def next(self):
        self.n = self.n + 1
        return self.base + self.n


class Core:

    def __init__(self, nc, ctx, arg):
        self.nc, self.ctx, self.arg = nc, ctx, arg
        self.signals, self.semaphores = {}, []
        self.named = {}
        self.x = self.sb(ctx, "x", [P, NT, D], F32)
        self.ident = self.sb(ctx, "ident", [P, P], F32)
        self.identb = self.sb(ctx, "identb", [P, P], BF16)
        self.maxmask = self.sb(ctx, "maxmask", [P, P], BF16)
        self.expmask = self.sb(ctx, "expmask", [P, P], BF16)
        self.iota = self.sb(ctx, "iota8", [P, 8], F32)
        self.ps = ctx.enter_context(nc.psum_tensor("ps", [P, 8, 512], F32))

    def sb(self, ctx, name, shape, dt):
        self.named[name] = self.named.get(name, 0) + 1
        if self.named[name] > 1:
            name = f"{name}_{self.named[name]}"
        return ctx.enter_context(self.nc.sbuf_tensor(name, shape, dt))

    def sig(self, name):
        if name not in self.signals:
            k = len(self.signals)
            if k == len(self.semaphores):
                self.semaphores.append(Signal(self.ctx.enter_context(self.nc.semaphore(f"signal{k}"))))
            self.signals[name] = self.semaphores[k]
        return self.signals[name]

    def own_sig(self, name):
        return Signal(self.ctx.enter_context(self.nc.semaphore(name)))

    def new_stage(self):
        self.signals = {}


def setup(c):
    nc = c.nc
    x_in, const, cast = c.sig("x_in"), c.sig("const"), c.sig("const_cast")
    with nc.Block() as block:
        @block.sync
        def _(sp):
            for b in range(4):
                sp.dma_start(c.x[:, 4 * b:4 * b + 4, :],
                                      c.arg["x"].rearrange("b (t p) d -> p (b t) d", p=P)[:, 4 * b:4 * b + 4, :]).then_inc(x_in.sem, 16)
            sp.wait_ge(x_in.sem, x_in.at(64))

        @block.gpsimd
        def _(pool):
            link = Chain(const)
            pool.memset(c.ident[:, :], 0.0).then_inc(link.sem, 1)
            pool.wait_ge(link.sem, link.next())
            pool.affine_select(out=c.ident[:, :], in_=c.ident[:, :], compare_op=ALU.not_equal, fill=1.0,
                                    base=0, pattern=[[-1, P]], channel_multiplier=1).then_inc(link.sem, 1)
            pool.wait_ge(link.sem, link.next())
            pool.memset(c.maxmask[:, :], 0.0).then_inc(link.sem, 1)
            pool.wait_ge(link.sem, link.next())
            pool.affine_select(out=c.maxmask[:, :], in_=c.maxmask[:, :], compare_op=ALU.is_ge, fill=MASKED,
                                    base=0, pattern=[[-1, P]], channel_multiplier=1).then_inc(link.sem, 1)
            pool.wait_ge(link.sem, link.next())
            pool.memset(c.expmask[:, :], 0.0).then_inc(link.sem, 1)
            pool.wait_ge(link.sem, link.next())
            pool.affine_select(out=c.expmask[:, :], in_=c.expmask[:, :], compare_op=ALU.is_ge, fill=MASKED,
                                    base=0, pattern=[[1, P]], channel_multiplier=-1).then_inc(link.sem, 1)
            pool.wait_ge(link.sem, link.next())
            pool.iota(c.iota[:, :], [[1, 8]], base=0, channel_multiplier=0,
                           allow_small_or_imprecise_dtypes=True).then_inc(link.sem, 1)
            pool.wait_ge(link.sem, link.next())

        @block.vector
        def _(dve):
            dve.wait_ge(const.sem, const.at(2))
            dve.tensor_copy(c.identb[:, :], c.ident[:, :]).then_inc(cast.sem, 1)
    for signal, n in ((x_in, 64), (const, 7), (cast, 1)):
        signal.passed(n)


class LayerNorm:

    def __init__(self, c, ctx, name):
        self.c = c
        self.stats = c.sb(ctx, name + "_stats", [P, NT, 6], F32)
        self.mv = c.sb(ctx, name + "_mv", [P, NT, 2], F32)
        self.ve = c.sb(ctx, name + "_ve", [P, NT], F32)
        self.sd = c.sb(ctx, name + "_sd", [P, NT], F32)
        self.rstd = c.sb(ctx, name + "_rstd", [P, NT], F32)
        self.xn = c.sb(ctx, name + "_xn", [P, NT, D], F32)
        self.s = {k: c.sig("ln_" + k) for k in ("stats", "meanvar", "vareps", "std", "rstd", "xn", "turned",
                                                "xt_act", "xt_dve")}

    def vector(self, dve):
        c, s = self.c, self.s

        def moments(g):
            for t in range(4 * g, 4 * g + 4):
                dve.bn_stats(self.stats[:, t, :], c.x[:, t, :]).then_inc(s["stats"].sem, 1)
            for t in range(4 * g, 4 * g + 4):
                dve.wait_ge(s["stats"].sem, s["stats"].at(t + 1))
                dve.bn_aggr(self.mv[:, t, :], self.stats[:, t, :]).then_inc(s["meanvar"].sem, 1)
            dve.wait_ge(s["meanvar"].sem, s["meanvar"].at(4 * g + 4))
            dve.tensor_scalar(self.ve[:, 4 * g:4 * g + 4], self.mv[:, 4 * g:4 * g + 4, 1], EPS, None,
                              ALU.add).then_inc(s["vareps"].sem, 1)

        moments(0)
        for g in range(NT // 4):
            if g + 1 < NT // 4:
                moments(g + 1)
            dve.wait_ge(s["std"].sem, s["std"].at(g + 1))
            dve.reciprocal(self.rstd[:, 4 * g:4 * g + 4], self.sd[:, 4 * g:4 * g + 4]).then_inc(s["rstd"].sem, 1)
            dve.wait_ge(s["rstd"].sem, s["rstd"].at(g + 1))
            for t in range(4 * g, 4 * g + 4):
                dve.tensor_scalar(self.xn[:, t, :], c.x[:, t, :], self.mv[:, t, 0:1], self.rstd[:, t:t + 1],
                                  ALU.subtract, ALU.mult).then_inc(s["xn"].sem, 1)

    def vector_xt(self, dve, xt):
        for g in range(NT // 4):
            dve.wait_ge(self.s["turned"].sem, self.s["turned"].at(2 * g + 2))
            dve.tensor_copy(xt[:, 1, 512 * g:512 * g + 512], self.c.ps[:, 2 * g + 1, :]).then_inc(self.s["xt_dve"].sem, 1)

    def scalar(self, act):
        for g in range(NT // 4):
            act.wait_ge(self.s["vareps"].sem, self.s["vareps"].at(g + 1))
            act.activation(self.sd[:, 4 * g:4 * g + 4], self.ve[:, 4 * g:4 * g + 4],
                           ACT.Sqrt).then_inc(self.s["std"].sem, 1)

    def scalar_xt(self, act, xt):
        for g in range(NT // 4):
            act.wait_ge(self.s["turned"].sem, self.s["turned"].at(2 * g + 1))
            act.activation(xt[:, 0, 512 * g:512 * g + 512], self.c.ps[:, 2 * g, :], ACT.Copy).then_inc(self.s["xt_act"].sem, 1)

    def tensor(self, pe):
        c = self.c
        for g in range(NT // 4):
            for k in range(KD):
                for j in range(4):
                    t = 4 * g + j
                    if k == 0:
                        pe.wait_ge(self.s["xn"].sem, self.s["xn"].at(t + 1))
                    last = pe.transpose(c.ps[:, 2 * g + k, P * j:P * j + P], self.xn[:, t, P * k:P * k + P],
                                        c.ident[:, :])
                last.then_inc(self.s["turned"].sem, 1)

    def wait_xt(self, eng, g):
        eng.wait_ge(self.s["xt_act"].sem, self.s["xt_act"].at(g + 1))
        eng.wait_ge(self.s["xt_dve"].sem, self.s["xt_dve"].at(g + 1))

    def done(self, turned=True):
        for k, n in (("stats", NT), ("meanvar", NT), ("vareps", NT // 4), ("std", NT // 4), ("rstd", NT // 4), ("xn", NT),
                     ("turned", 8 * turned), ("xt_act", 4 * turned), ("xt_dve", 4 * turned)):
            self.s[k].passed(n)


def head_parts(c, ctx, name):
    t = {}
    t["full"] = c.sb(ctx, name + "_full", [P, 2, 512], F32)
    t["rest"] = c.sb(ctx, name + "_rest", [P, 2, 512], F32)
    t["part"] = c.sb(ctx, name + "_part", [P, 2, PARTS, N], BF16)
    return t


def project_self(c, v_all, scr_q, scr_k):
    nc, ps = c.nc, c.ps
    wqkv, bqkv = c.arg["L0_attn_Wqkv"], c.arg["L0_attn_bqkv"]
    with ExitStack() as ctx:
        ln = LayerNorm(c, ctx, "ln0")
        xt = c.sb(ctx, "xt0", [P, KD, N], F32)
        w = c.sb(ctx, "w_qkv", [P, KD, H, 3 * DH], F32)
        w_qk = c.sb(ctx, "w_qk", [P, 2, KD, D], F32)
        bias = c.sb(ctx, "b_qk", [P, 2, KD], F32)
        bias_v = c.sb(ctx, "b_v", [P, H, DH], F32)
        t = head_parts(c, ctx, "h0")
        w_in, full, high, rest, mid, low, sent, v_set, v_zero = (
            c.sig("w_in"), c.sig("pr_full"), c.sig("pr_high"), c.sig("pr_rest"), c.sig("pr_mid"), c.sig("pr_low"),
            c.sig("pr_sent"), c.sig("pr_v"), c.sig("pr_vzero"))
        mm = c.sig("pr_mm")
        w_set = c.sig("pr_wset")
        blocks = [(i, mb) for i in range(2) for mb in range(KD)]
        NC = N // 512
        with nc.Block() as block:
            @block.sync
            def _(sp):
                for k in range(KD):
                    sp.dma_start(w[:, k, :, :], wqkv.rearrange("h (k p) e -> k p h e", p=P)[k]).then_inc(w_in.sem, 16)
                for i in range(2):
                    for h in range(H):
                        sp.dma_start(bias[DH * (h % 8):DH * (h % 8) + DH, i, h // 8:h // 8 + 1],
                                              bqkv[h:h + 1, DH * i:DH * i + DH].rearrange("a b -> b a")).then_inc(w_in.sem, 16)
                sp.dma_start(bias_v[:, :, :], bqkv[:, 2 * DH:3 * DH].partition_broadcast(P)).then_inc(w_in.sem, 16)
                for n, (i, mb) in enumerate(blocks):
                    sp.wait_ge(mid.sem, mid.at(NC * (n + 1)))
                    sp.wait_ge(low.sem, low.at(NC * (n + 1)))
                    for part in range(PARTS):
                        sp.dma_start((scr_q, scr_k)[i][part, P * mb:P * mb + P, :],
                                              t["part"][:, n % 2, part, :]).then_inc(sent.sem, 16)
                sp.wait_ge(sent.sem, sent.at(16 * PARTS * len(blocks)))

            @block.gpsimd
            def _(pool):
                pool.memset(v_all[:, :, :, DH:VW], 0.0).then_inc(v_zero.sem, 1)
                pool.wait_ge(v_zero.sem, v_zero.at(1))
                pool.memset(v_all[:, :, :, DH:DH + 1], 1.0).then_inc(v_zero.sem, 1)
                pool.wait_ge(w_in.sem, w_in.at(16 * (KD + 2 * H + 1)))
                for i in range(2):
                    for k in range(KD):
                        pool.tensor_copy(w_qk[:, i, k, :].rearrange("p (h e) -> p h e", h=H),
                                                   w[:, k, :, DH * i:DH * i + DH]).then_inc(w_set.sem, 1)

            @block.tensor
            def _(pe):
                ln.tensor(pe)
                pe.wait_ge(w_in.sem, w_in.at(16 * (KD + 2 * H + 1)))
                pe.wait_ge(w_set.sem, w_set.at(2 * KD))
                n = 0
                for i, mb in blocks:
                    for g in range(NC):
                        if n < NC:
                            ln.wait_xt(pe, 3)
                        if n >= 8:
                            pe.wait_ge(high.sem, high.at(n - 7))
                        for k in range(KD):
                            last = pe.matmul(ps[:, n % 8, :], w_qk[:, i, k, P * mb:P * mb + P],
                                             xt[:, k, 512 * g:512 * g + 512], start=(k == 0), stop=(k == KD - 1))
                        last.then_inc(mm.sem, 1)
                        n += 1
                for u in range(NT):
                    if u < 8:
                        pe.wait_ge(high.sem, high.at(n - 7 + u))
                    else:
                        pe.wait_ge(v_set.sem, v_set.at(u - 7))
                    for k in range(KD):
                        last = pe.matmul(ps[:, (n + u) % 8, 0:D], xt[:, k, P * u:P * u + P],
                                         w[:, k, :, 2 * DH:3 * DH], start=(k == 0), stop=(k == KD - 1))
                    last.then_inc(mm.sem, 1)

            @block.scalar
            def _(act):
                ln.scalar(act)
                ln.scalar_xt(act, xt)
                act.wait_ge(w_in.sem, w_in.at(16 * (KD + 2 * H + 1)))
                n = 0
                for m, (i, mb) in enumerate(blocks):
                    for g in range(NC):
                        act.wait_ge(mm.sem, mm.at(n + 1))
                        if n >= 2:
                            act.wait_ge(rest.sem, rest.at(n - 1))
                        if m >= 2 and g == 0:
                            act.wait_ge(sent.sem, sent.at(16 * PARTS * (m - 1)))
                        act.activation(t["full"][:, n % 2, :], ps[:, n % 8, :], ACT.Identity,
                                                bias=bias[:, i, mb:mb + 1]).then_inc(full.sem, 1)
                        act.activation(t["part"][:, m % 2, 0, 512 * g:512 * g + 512], ps[:, n % 8, :],
                                                ACT.Identity, bias=bias[:, i, mb:mb + 1]).then_inc(high.sem, 1)
                        if n >= 1:
                            act.wait_ge(rest.sem, rest.at(n))
                            o, q = (n - 1) % 2, n - 1
                            act.activation(t["part"][:, (q // NC) % 2, 1, 512 * (q % NC):512 * (q % NC) + 512],
                                                   t["rest"][:, o, :], ACT.Copy).then_inc(mid.sem, 1)
                        n += 1
                act.wait_ge(rest.sem, rest.at(n))
                act.activation(t["part"][:, (n - 1) // NC % 2, 1, 512 * (NC - 1):], t["rest"][:, (n - 1) % 2, :],
                                       ACT.Copy).then_inc(mid.sem, 1)

            @block.vector
            def _(dve):
                ln.vector(dve)
                ln.vector_xt(dve, xt)
                dve.wait_ge(w_in.sem, w_in.at(16 * (KD + 2 * H + 1)))

                def lows(q):
                    dve.wait_ge(mid.sem, mid.at(q + 1))
                    a = slice(512 * (q % NC), 512 * (q % NC) + 512)
                    dve.tensor_tensor(t["part"][:, (q // NC) % 2, 2, a], t["rest"][:, q % 2, :],
                                              t["part"][:, (q // NC) % 2, 1, a], ALU.subtract).then_inc(low.sem, 1)
                for n in range(len(blocks) * NC):
                    a = slice(512 * (n % NC), 512 * (n % NC) + 512)
                    dve.wait_ge(full.sem, full.at(n + 1))
                    dve.wait_ge(high.sem, high.at(n + 1))
                    if n >= 2:
                        dve.wait_ge(low.sem, low.at(n - 1))
                    dve.tensor_tensor(t["rest"][:, n % 2, :], t["full"][:, n % 2, :],
                                               t["part"][:, (n // NC) % 2, 0, a], ALU.subtract).then_inc(rest.sem, 1)
                    if n >= 1:
                        lows(n - 1)
                n = len(blocks) * NC
                lows(n - 1)
                dve.wait_ge(v_zero.sem, v_zero.at(2))
                for u in range(NT):
                    dve.wait_ge(mm.sem, mm.at(n + u + 1))
                    dve.tensor_tensor(v_all[:, u, :, 0:DH],
                                                ps[:, (n + u) % 8, 0:D].rearrange("p (h e) -> p h e", h=H),
                                                bias_v[:, :, :], ALU.add).then_inc(v_set.sem, 1)
        ln.done()
        n = len(blocks) * NC
        for s, k in ((w_in, 16 * (KD + 2 * H + 1)), (mm, n + NT), (full, n), (high, n), (rest, n), (mid, n), (low, n),
                     (sent, 16 * PARTS * len(blocks)), (v_set, NT), (v_zero, 2), (w_set, 2 * KD)):
            s.passed(k)


MAX_BANK = (0, 1)
EXP_BANK = (2, 4)
OUT_BANK = 6


class Turns:

    def __init__(self, filled, freed):
        self.filled, self.freed, self.n = filled, freed, 0

    def used(self):
        self.n = self.n + 1


class Alternation:

    def __init__(self):
        self.n = 0

    def take(self):
        self.n = self.n + 1
        return (self.n - 1) % 2


class Attention:

    def __init__(self, c, ctx, name, units, heads, width, v_width, ahead, slots, neg_parts, neg_dt):
        self.c, self.units, self.heads, self.width, self.v_width = c, units, heads, width, v_width
        self.ahead, self.ring, self.slots = ahead, ahead + 1, slots
        self.qb = heads * ST
        self.rows = heads * v_width
        self.neg_parts = neg_parts
        self.o_raw = c.sb(ctx, name + "_o_raw", [self.rows, 2, S], F32)
        self.top = c.sb(ctx, name + "_top", [P, self.ring, self.qb], F32)
        self.neg_rest = c.sb(ctx, name + "_neg_rest", [self.qb, 2, P], F32)
        self.neg = c.sb(ctx, name + "_neg", [self.qb, self.ring, neg_parts, P], neg_dt)
        self.rinv = c.sb(ctx, name + "_rinv", [P, 4, heads], F32)
        self.staged = [c.sig(f"a_staged{i}") for i in range(self.slots)]
        self.rows_in = [c.sig(f"a_rows{i}") for i in range(self.ring)]
        self.top_ready, self.neg_ready, self.weighed = c.sig("a_top"), c.sig("a_neg"), c.sig("a_weighed")
        self.chain, self.made = c.sig("a_chain"), c.sig("a_made")
        self.area = {k: (c.sig(f"a_{k}_filled"), c.sig(f"a_{k}_freed")) for k in ("max0", "max1", "exp0", "exp1")}
        self.out_freed = c.sig("a_out_freed")

    def turns(self):
        return {k: Turns(*v) for k, v in self.area.items()}

    def order(self):
        nu, nc = len(self.units), self.n_chunks
        weighs = [(nc * u + need, u, k) for u in range(nu) for k, need in enumerate(self.steps)]
        tops = []
        for u in range(nu):
            end = nc * u - self.margin
            tops += [(end - nc + nc * n / self.n_pieces, "piece", u, n) for n in range(self.n_pieces)]
            tops.append((end, "turn", u, 0))
        while tops and (tops[0][0] < 0 or tops[0][2] == 0):
            yield tops.pop(0)[1:]
        for u in range(nu):
            for n in range(nc):
                yield "chunk", u, n
                while weighs and weighs[0][0] + self.lag <= nc * u + n + 1:
                    yield "weigh", *weighs.pop(0)[1:]
                while tops and tops[0][0] < nc * u + n + 1:
                    yield tops.pop(0)[1:]
                if n == self.out_chunk and u > 0:
                    yield "out", u - 1, 0
        yield from (("weigh", u, k) for _, u, k in weighs)
        yield "out", nu - 1, 0

    def freed_after_out(self, u):
        n, bank = [0, 0], Alternation()
        for what, v, m in self.order():
            if what in ("piece", "turn"):
                n[bank.take()] += 1
            elif what == "out":
                n[bank.take()] += 1
                n[bank.take()] += 1
                if v == u:
                    return n

    def run(self):
        c, nc = self.c, self.c.nc
        ps, nu, ahead = c.ps, len(self.units), self.ahead
        with nc.Block() as block:
            @block.gpsimd
            def _(pool):
                self.pool(pool)

            @block.sync
            def _(sp):
                sp.wait_ge(self.made.sem, self.made.at(self.n_made))
                self.load(sp)

                def stage(u):
                    if u >= self.slots:
                        sp.wait_ge(self.weighed.sem, self.weighed.at(len(self.steps) * (u - self.slots + 1)))
                    self.stage(sp, u)

                def max_rows(u):
                    sp.wait_ge(self.neg_ready.sem, self.neg_ready.at(u + 1))
                    for part in range(self.neg_parts):
                        sp.dma_start(
                            raw(self.neg_row(u, part)).rearrange("p h (b s) -> p (h b) s", s=P),
                            raw(self.neg[:, u % self.ring, part:part + 1, :])).then_inc(self.rows_in[u % self.ring].sem, 16)

                for u in range(min(ahead + 1, nu)):
                    stage(u)
                for u in range(ahead):
                    max_rows(u)
                for u in range(nu):
                    if u + ahead + 1 < nu:
                        stage(u + ahead + 1)
                    if u + ahead < nu:
                        max_rows(u + ahead)

            @block.tensor
            def _(pe):
                t, bank = self.turns(), Alternation()
                self.loaded(pe)

                def piece(u, n):
                    i = bank.take()
                    a = t[f"max{i}"]
                    if n == 0:
                        pe.wait_ge(self.staged[u % self.slots].sem, self.staged[u % self.slots].at(self.stage_dmas * 16 * (u // self.slots + 1)))
                    pe.wait_ge(a.freed.sem, a.freed.at(a.n))
                    self.piece_scores(pe, u, n, MAX_BANK[i]).then_inc(a.filled.sem, 1)
                    a.used()

                def turn(u, _):
                    i = bank.take()
                    a = t[f"max{i}"]
                    pe.wait_ge(a.freed.sem, a.freed.at(a.n))
                    pe.wait_ge(self.top_ready.sem, self.top_ready.at(u + 1))
                    pe.transpose(ps[0:self.qb, MAX_BANK[i], 0:P], self.top[:, u % self.ring, :],
                                        c.ident[:, :]).then_inc(a.filled.sem, 1)
                    a.used()

                def chunk(u, n):
                    if n == 0:
                        pe.wait_ge(self.rows_in[u % self.ring].sem, self.rows_in[u % self.ring].at(16 * self.neg_parts * (u // self.ring + 1)))
                    a = t[f"exp{n % 2}"]
                    pe.wait_ge(a.freed.sem, a.freed.at(a.n))
                    self.chunk_scores(pe, u, n, EXP_BANK[n % 2]).then_inc(a.filled.sem, 1)
                    a.used()

                def weigh(u, k):
                    if k == 0:
                        pe.wait_ge(self.out_freed.sem, self.out_freed.at(u))
                    for i in range(2):
                        pe.wait_ge(self.area[f"exp{i}"][1].sem, self.area[f"exp{i}"][1].at(self.n_chunks // 2 * u + (self.steps[k] + 1 - i) // 2))
                    self.weigh(pe, u, k).then_inc(self.weighed.sem, 1)

                def turn_out(u, _):
                    pe.wait_ge(self.out_freed.sem, self.out_freed.at(u + 1))
                    for half in range(2):
                        i = bank.take()
                        a = t[f"max{i}"]
                        pe.wait_ge(a.freed.sem, a.freed.at(a.n))
                        for j in range(4):
                            q = 512 * half + P * j
                            last = pe.transpose(ps[:, MAX_BANK[i], P * j:P * j + self.rows],
                                                self.o_raw[:, u % 2, q:q + P], c.ident[0:self.rows, 0:self.rows])
                        last.then_inc(a.filled.sem, 1)
                        a.used()

                for what, u, n in self.order():
                    {"piece": piece, "turn": turn, "chunk": chunk, "weigh": weigh, "out": turn_out}[what](u, n)

            @block.scalar
            def _(act):
                t = self.turns()

                def copy_out(u):
                    act.wait_ge(self.weighed.sem, self.weighed.at(len(self.steps) * (u + 1)))
                    if u >= 2:
                        for i, n in enumerate(self.freed_after_out(u - 2)):
                            act.wait_ge(self.area[f"max{i}"][1].sem, self.area[f"max{i}"][1].at(n))
                    act.activation(
                        self.o_raw[:, u % 2, :],
                        ps[0:self.rows, OUT_BANK:OUT_BANK + 2, :].rearrange("p b s -> p (b s)"), ACT.Copy).then_inc(self.out_freed.sem, 1)

                for u in range(nu):
                    for n in range(self.n_chunks):
                        a = t[f"exp{n % 2}"]
                        act.wait_ge(a.filled.sem, a.filled.at(a.n + 1))
                        g = len(self.steps) * u + self.step_of(n)
                        if g >= 2:
                            act.wait_ge(self.weighed.sem, self.weighed.at(g - 1))
                        self.chunk_exp(act, u, n, EXP_BANK[n % 2]).then_inc(a.freed.sem, 1)
                        a.used()
                        if n == self.copy_chunk and u > 0:
                            copy_out(u - 1)
                copy_out(nu - 1)

            @block.vector
            def _(dve):
                t, bank = self.turns(), Alternation()
                link = Chain(self.chain)
                self.prepare(dve, link)

                def piece(u, n):
                    i = bank.take()
                    a = t[f"max{i}"]
                    dve.wait_ge(a.filled.sem, a.filled.at(a.n + 1))
                    if n == 0 and u >= self.ring:
                        dve.wait_ge(self.neg_ready.sem, self.neg_ready.at(u - self.ring + 1))
                    self.piece_max(dve, u, n, MAX_BANK[i]).then_inc(a.freed.sem, 1)
                    a.used()

                def minus(u, _):
                    for k in ("max0", "max1"):
                        dve.wait_ge(t[k].freed.sem, t[k].freed.at(t[k].n))
                    self.join_max(dve, u).then_inc(self.top_ready.sem, 1)
                    i = bank.take()
                    a = t[f"max{i}"]
                    dve.wait_ge(a.filled.sem, a.filled.at(a.n + 1))
                    src = ps[0:self.qb, MAX_BANK[i], 0:P]
                    if u >= self.ring:
                        dve.wait_ge(self.rows_in[u % self.ring].sem, self.rows_in[u % self.ring].at(16 * self.neg_parts * (u // self.ring)))
                    neg = self.neg[:, u % self.ring, :, :]
                    rest = self.neg_rest
                    dve.tensor_scalar(rest[:, 0, :], src, -1.0, None, ALU.mult).then_inc(a.freed.sem, 1)
                    a.used()
                    dve.wait_ge(a.freed.sem, a.freed.at(a.n))
                    dve.tensor_copy(neg[:, 0, :], rest[:, 0, :]).then_inc(link.sem, 1)
                    dve.wait_ge(link.sem, link.next())
                    for part in range(1, self.neg_parts):
                        former = raw(neg[:, part - 1, :])
                        if part < self.neg_parts - 1:
                            dve.tensor_tensor(rest[:, part, :], rest[:, part - 1, :], former, ALU.subtract).then_inc(link.sem, 1)
                            dve.wait_ge(link.sem, link.next())
                            dve.tensor_copy(neg[:, part, :], rest[:, part, :]).then_inc(link.sem, 1)
                            dve.wait_ge(link.sem, link.next())
                        else:
                            dve.tensor_tensor(neg[:, part, :], rest[:, part - 1, :], former,
                                                                 ALU.subtract).then_inc(self.neg_ready.sem, 1)

                def normalize(u, _):
                    b, g = self.units[u]
                    for half in range(2):
                        i = bank.take()
                        a = t[f"max{i}"]
                        dve.wait_ge(a.filled.sem, a.filled.at(a.n + 1))
                        src = ps[:, MAX_BANK[i], :].rearrange("p (t r) -> p t r", t=4)[:, :, 0:self.rows]
                        src = src.rearrange("p t (h e) -> p t h e", h=self.heads)
                        w = self.width
                        dve.reciprocal(self.rinv[:, :, :], src[:, :, :, w]).then_inc(link.sem, 1)
                        dve.wait_ge(link.sem, link.next())
                        tile = ST * b + 4 * half
                        dst = self.o_tok[:, tile:tile + 4, self.heads * w * g:self.heads * w * (g + 1)]
                        dve.tensor_tensor(dst.rearrange("p t (h e) -> p t h e", h=self.heads),
                                                 src[:, :, :, 0:w],
                                                 self.rinv[:, :, :].unsqueeze(3).to_broadcast([P, 4, self.heads, w]),
                                                 ALU.mult).then_inc(a.freed.sem, 1)
                        a.used()
                        dve.wait_ge(a.freed.sem, a.freed.at(a.n))

                for what, u, n in self.order():
                    if what in ("piece", "turn", "out"):
                        {"piece": piece, "turn": minus, "out": normalize}[what](u, n)
                self.chained = link.n
        n = self.freed_after_out(nu - 1)
        for i in range(2):
            for s in self.area[f"max{i}"]:
                s.passed(n[i])
            for s in self.area[f"exp{i}"]:
                s.passed(nu * self.n_chunks // 2)
        for i in range(self.slots):
            self.staged[i].passed(16 * self.stage_dmas * len(range(i, nu, self.slots)))
        for i in range(self.ring):
            self.rows_in[i].passed(16 * self.neg_parts * len(range(i, nu, self.ring)))
        for s, k in ((self.top_ready, nu), (self.neg_ready, nu), (self.weighed, len(self.steps) * nu),
                     (self.out_freed, nu), (self.made, self.n_made), (self.chain, self.chained)):
            s.passed(k)


class SelfAttention(Attention):

    def __init__(self, c, ctx, v_all, scr_q, scr_k, o_tok):
        gps = H // HPU
        super().__init__(c, ctx, "sa", [(b, g) for b in range(B) for g in range(gps)], HPU, DH, VW, 2, 4, PARTS, BF16)
        self.v_all, self.scr, self.o_tok = v_all, (scr_q, scr_k), o_tok
        self.q_st = c.sb(ctx, "sa_q", [P, self.slots, HPU, S], BF16)
        self.k_st = c.sb(ctx, "sa_k", [P, self.slots, HPU, S], BF16)
        self.probs = c.sb(ctx, "sa_probs", [P, 2, HPU, S], F32)
        self.top2 = c.sb(ctx, "sa_top2", [P, 2, self.qb], F32)
        self.pieces = [(h, sb, k0, min(512, (sb + 1) * P - k0)) for sb in reversed(range(ST)) for h in range(HPU)
                       for k0 in range(0, (sb + 1) * P, 512)]
        self.chunks = [(kb, (h,)) for kb in range(ST // 2) for h in range(HPU)]
        self.chunks += [(kb, (h, h + 1)) for kb in range(ST // 2, ST) for h in range(0, HPU, 2)]
        self.n_pieces, self.n_chunks = len(self.pieces), len(self.chunks)
        self.steps = [sum(kb <= k for kb, _ in self.chunks) for k in range(ST)]
        self.lag, self.margin, self.copy_chunk, self.out_chunk = 3, 7, 1, 7
        self.n_made, self.stage_dmas = self.slots, 12

    def load(self, sp):
        pass

    def loaded(self, pe):
        pass

    def step_of(self, n):
        return self.chunks[n][0]

    def pool(self, pool):
        for i in range(self.slots):
            pool.memset(self.k_st[96:P, i, :, :], 1.0).then_inc(self.made.sem, 1)

    def prepare(self, dve, link):
        dve.memset(self.q_st[96:P, :, :, :].rearrange("p a h s -> p (a h s)").bitcast(U32), 0).then_inc(link.sem, 1)
        dve.wait_ge(link.sem, link.next())
        dve.memset(self.top2[:, :, :], -3e38).then_inc(link.sem, 1)
        dve.wait_ge(link.sem, link.next())

    def stage(self, sp, u):
        b, g = self.units[u]
        done = self.staged[u % self.slots]
        rows = slice(HPU * DH * g, HPU * DH * (g + 1))
        for dst, src, parts in ((self.q_st, self.scr[0], Q_ROWS), (self.k_st, self.scr[1], K_ROWS)):
            for j, part in enumerate(parts):
                sp.dma_start(dst[DH * j:DH * j + DH, u % self.slots, :, :],
                                      src[part, rows, S * b:S * b + S].rearrange("(h e) s -> e h s", e=DH)).then_inc(done.sem, 16)

    def neg_row(self, u, part):
        r = len(Q_ROWS) * DH + part
        return self.q_st[r:r + 1, u % self.slots, :, :]

    def piece_scores(self, pe, u, n, bank):
        c, slot = self.c, u % self.slots
        h, sb, k0, w = self.pieces[n]
        diagonal = k0 + w == (sb + 1) * P
        last = pe.matmul(c.ps[:, bank, 0:w], self.q_st[0:96, slot, h, P * sb:P * sb + P],
                         self.k_st[0:96, slot, h, k0:k0 + w], start=True, stop=not diagonal)
        if diagonal:
            last = pe.matmul(c.ps[:, bank, w - P:w], c.identb[:, :], c.maxmask[:, :], start=False, stop=True)
        return last

    def piece_max(self, dve, u, n, bank):
        h, sb, k0, w = self.pieces[n]
        return dve.tensor_reduce(self.top2[:, k0 // 512, ST * h + sb:ST * h + sb + 1], self.c.ps[:, bank, 0:w],
                                 AX.X, ALU.max)

    def join_max(self, dve, u):
        return dve.tensor_tensor(self.top[:, u % self.ring, :], self.top2[:, 0, :], self.top2[:, 1, :], ALU.max)

    def chunk_scores(self, pe, u, n, bank):
        c, slot = self.c, u % self.slots
        kb, heads = self.chunks[n]
        for j, h in enumerate(heads):
            for q0 in range(0, S - P * kb, 512):
                qw = min(512, S - P * kb - q0)
                out = c.ps[:, bank + j + q0 // 512, :]
                last = pe.matmul(out[:, 0:qw], self.k_st[0:KROWS, slot, h, P * kb:P * kb + P],
                                 self.q_st[0:KROWS, slot, h, P * kb + q0:P * kb + q0 + qw],
                                 start=True, stop=q0 > 0)
                if q0 == 0:
                    last = pe.matmul(out[:, 0:P], c.identb[:, :], c.expmask[:, :], start=False, stop=True)
        return last

    def chunk_exp(self, act, u, n, bank):
        kb, heads = self.chunks[n]
        w = S - P * kb
        if len(heads) == 2:
            src, dst = self.c.ps[:, bank:bank + 2, 0:w], self.probs[:, kb % 2, heads[0]:heads[0] + 2, 0:w]
        else:
            src = self.c.ps[:, bank:bank + 2, :].rearrange("p b s -> p (b s)")[:, 0:w]
            dst = self.probs[:, kb % 2, heads[0], 0:w]
        return act.activation(dst, src, ACT.Exp, scale=self.width ** -0.5)

    def weigh(self, pe, u, kb):
        b, g = self.units[u]
        for half in range(2):
            q0, q1 = max(P * kb, 512 * half), 512 * (half + 1)
            if q0 >= q1:
                continue
            for h in range(HPU):
                last = pe.matmul(self.c.ps[VW * h:VW * h + VW, OUT_BANK + half, q0 - 512 * half:512],
                                 self.v_all[:, ST * b + kb, HPU * g + h, :], self.probs[:, kb % 2, h, q0 - P * kb:q1 - P * kb],
                                 start=(kb == 0), stop=(kb == 4 * half + 3))
        return last


class CrossAttention(Attention):

    def __init__(self, c, ctx, wide, v_all, scr_q, scr_k, o_tok):
        heads, width = (1, 64) if wide else (HPU, DH)
        ahead, slots = (2, 5) if wide else (1, 3)
        super().__init__(c, ctx, "ca", [(b, g) for b in range(B) for g in range(H // heads)], heads, width,
                         width + 1 if wide else VW, ahead, slots, 2 if wide else PARTS, F32R if wide else BF16)
        self.wide, self.v_all, self.scr, self.o_tok = wide, v_all, (scr_q, scr_k), o_tok
        self.dt = F32R if wide else BF16
        self.q_st = c.sb(ctx, "ca_q", [P, self.slots, heads, S], self.dt)
        self.kcols = self.slots * 256 if wide else H * B * M
        self.k_st = c.sb(ctx, "ca_k", [P, self.kcols], self.dt)
        if wide:
            self.qb_st = c.sb(ctx, "ca_qb", [P, self.slots, heads, S], self.dt)
            self.kb_max = c.sb(ctx, "ca_kb_max", [P, self.kcols], self.dt)
            self.kb_exp = c.sb(ctx, "ca_kb_exp", [P, self.kcols], self.dt)
        self.probs = c.sb(ctx, "ca_probs", [MH, 2, heads, S], F32)
        self.top_raw = c.sb(ctx, "ca_top_raw", [P, self.qb], F32)
        self.group = 2 if wide else 3
        self.step = 256 if wide else M
        self.n_pieces = -(-self.qb // self.group)
        self.n_chunks = 2 * heads
        self.steps = [heads, 2 * heads]
        if wide:
            self.lag, self.margin, self.copy_chunk, self.out_chunk = 1, 3, 0, 1
        else:
            self.lag, self.margin, self.copy_chunk, self.out_chunk = 1, 4, 1, 3
        self.n_made = 5 if wide else 2
        self.stage_dmas = 7 if wide else 6
        self.k_in = c.sig("ca_k_in")

    def step_of(self, n):
        return n // self.heads

    def key(self, u, h):
        if self.wide:
            return 256 * (u % self.slots)
        b, g = self.units[u]
        return M * (B * (self.heads * g + h) + b)

    def pool(self, pool):
        if self.wide:
            link = Chain(self.made)
            pool.memset(self.kb_max[:, :].bitcast(F32), 0.0).then_inc(link.sem, 1)
            pool.wait_ge(link.sem, link.next())
            pool.memset(self.kb_exp[:, :].bitcast(F32), 0.0).then_inc(link.sem, 1)
            pool.wait_ge(link.sem, link.next())
            pool.memset(self.kb_exp[64:66, :].bitcast(F32), 1.0).then_inc(link.sem, 1)
            pool.wait_ge(link.sem, link.next())
            pool.memset(self.k_st[:, :].bitcast(F32), 0.0).then_inc(link.sem, 1)
            pool.wait_ge(link.sem, link.next())
            pool.memset(self.qb_st[64:P, :, :, :].bitcast(F32), 0.0).then_inc(link.sem, 1)
            pool.wait_ge(link.sem, link.next())
        else:
            pool.memset(self.k_st[96:P, :], 1.0).then_inc(self.made.sem, 1)
            pool.memset(self.q_st[96:P, :, :, :], 0.0).then_inc(self.made.sem, 1)

    def prepare(self, dve, link):
        pass

    def load(self, sp):
        scr = self.scr[1]
        n = H * B * M
        if not self.wide:
            for j, part in enumerate(K_ROWS):
                sp.dma_start(self.k_st[DH * j:DH * j + DH, 0:n].rearrange("e (h k) -> e h k", h=H),
                                           scr[part].rearrange("(h e) k -> e h k", e=DH)).then_inc(self.k_in.sem, 16)

    def loaded(self, pe):
        if not self.wide:
            pe.wait_ge(self.k_in.sem, self.k_in.at(16 * len(K_ROWS)))

    def stage(self, sp, u):
        b, g = self.units[u]
        done = self.staged[u % self.slots]
        slot = u % self.slots
        if self.wide:
            for dst, part, row in ((self.q_st, 0, 0), (self.q_st, 1, 64), (self.qb_st, 0, 0)):
                sp.dma_start(raw(dst[row:row + 64, slot, 0, :]),
                                      self.scr[0][part, 64 * g:64 * g + 64, S * b:S * b + S]).then_inc(done.sem, 16)
            k0 = self.key(u, 0)
            for dst, part, row in ((self.k_st, 0, 0), (self.k_st, 0, 64), (self.kb_max, 1, 0), (self.kb_exp, 1, 0)):
                sp.dma_start(raw(dst[row:row + 64, k0:k0 + M]),
                                      self.scr[1][part, 64 * g:64 * g + 64, M * b:M * b + M]).then_inc(done.sem, 16)
        else:
            rows = slice(HPU * DH * g, HPU * DH * (g + 1))
            for j, part in enumerate(Q_ROWS):
                sp.dma_start(self.q_st[DH * j:DH * j + DH, slot, :, :],
                                      self.scr[0][part, rows, S * b:S * b + S].rearrange("(h e) s -> e h s", e=DH)).then_inc(done.sem, 16)

    def neg_row(self, u, part):
        if self.wide:
            return self.qb_st[64 + part:65 + part, u % self.slots, :, :]
        r = len(Q_ROWS) * DH + part
        return self.q_st[r:r + 1, u % self.slots, :, :]

    def piece_scores(self, pe, u, n, bank):
        slot = u % self.slots
        for j in range(min(self.group, self.qb - self.group * n)):
            h, sb = divmod(self.group * n + j, ST)
            k0 = self.key(u, h)
            out = self.c.ps[:, bank, self.step * j:self.step * (j + 1)]
            q = slice(P * sb, P * sb + P)
            if self.wide:
                pe.matmul(out, self.q_st[:, slot, h, q], self.k_st[:, k0:k0 + 256], start=True, stop=False)
                last = pe.matmul(out, self.qb_st[:, slot, h, q], self.kb_max[:, k0:k0 + 256], start=False, stop=True)
            else:
                last = pe.matmul(out, self.q_st[0:96, slot, h, q], self.k_st[0:96, k0:k0 + M], start=True, stop=True)
        return last

    def piece_max(self, dve, u, n, bank):
        k = min(self.group, self.qb - self.group * n)
        src = self.c.ps[:, bank, 0:self.step * k].rearrange("p (k m) -> p k m", k=k)[:, :, 0:M]
        return dve.tensor_reduce(self.top_raw[:, self.group * n:self.group * n + k], src, AX.X, ALU.max)

    def join_max(self, dve, u):
        return dve.tensor_copy(self.top[:, u % self.ring, :], self.top_raw[:, :])

    def chunk_scores(self, pe, u, n, bank):
        slot = u % self.slots
        half, h = divmod(n, self.heads)
        k0 = self.key(u, h) + MH * half
        for q in range(2):
            out = self.c.ps[0:MH, bank + q, :]
            cols = slice(512 * q, 512 * q + 512)
            if self.wide:
                pe.matmul(out, self.k_st[:, k0:k0 + MH], self.q_st[:, slot, h, cols], start=True, stop=False)
                last = pe.matmul(out, self.kb_exp[:, k0:k0 + MH], self.qb_st[:, slot, h, cols],
                                 start=False, stop=True)
            else:
                last = pe.matmul(out, self.k_st[0:KROWS, k0:k0 + MH], self.q_st[0:KROWS, slot, h, cols],
                                 start=True, stop=True)
        return last

    def chunk_exp(self, act, u, n, bank):
        half, h = divmod(n, self.heads)
        return act.activation(self.probs[:, half, h, :],
                              self.c.ps[0:MH, bank:bank + 2, :].rearrange("p b s -> p (b s)"), ACT.Exp,
                              scale=self.width ** -0.5)

    def weigh(self, pe, u, half):
        b, g = self.units[u]
        for q in range(2):
            for h in range(self.heads):
                w = self.v_width
                last = pe.matmul(self.c.ps[w * h:w * h + w, OUT_BANK + q, :],
                                 self.v_all[:, 2 * b + half, self.heads * g + h, :],
                                 self.probs[:, half, h, 512 * q:512 * q + 512], start=(half == 0), stop=(half == 1))
        return last


def make_context(c, ct):
    nc = c.nc
    with ExitStack() as ctx:
        raw = c.sb(ctx, "ctx_raw", [MH, 4, DC], F32)
        c_in, turned, set_ = c.sig("c_in"), c.sig("c_turned"), c.sig("c_set")
        with nc.Block() as block:
            @block.sync
            def _(sp):
                sp.dma_start(raw[:, :, :], c.arg["ctx_768"].rearrange("b (i m) d -> m (b i) d", m=MH)).then_inc(c_in.sem, 16)

            @block.tensor
            def _(pe):
                pe.wait_ge(c_in.sem, c_in.at(16))
                for k in range(2):
                    for j in range(4):
                        last = pe.transpose(c.ps[0:96, k, MH * j:MH * j + MH], raw[:, j, 96 * k:96 * k + 96],
                                            c.ident[0:MH, 0:MH])
                last.then_inc(turned.sem, 1)

            @block.vector
            def _(dve):
                dve.wait_ge(turned.sem, turned.at(1))
                dve.tensor_copy(ct[:, :, :], c.ps[0:96, 0:2, 0:B * M]).then_inc(set_.sem, 1)
    for s, k in ((c_in, 16), (turned, 1), (set_, 1)):
        s.passed(k)


def project_cross(c, layer, wide, ct, v_all, scr_q, scr_k):
    nc, ps = c.nc, c.ps
    width = 64 if wide else DH
    rows = H * width
    blocks = rows // P
    dt = F32R if wide else BF16
    parts = 2 if wide else PARTS
    biased = not wide
    arg = {k: c.arg[f"L{layer}_xattn_{k}"] for k in ("Wq", "Wk", "Wv") + (("bq", "bk", "bv") if biased else ())}
    vw = v_all.shape[3]
    with ExitStack() as ctx:
        ln = LayerNorm(c, ctx, f"lnx{layer}")
        xt = c.sb(ctx, "xc_t", [P, KD, N], F32)
        wq = c.sb(ctx, "xc_wq", [P, KD, rows], F32)
        wk = c.sb(ctx, "xc_wk", [96, 2, rows], F32)
        wv = c.sb(ctx, "xc_wv", [96, 2, rows], F32)
        bias = c.sb(ctx, "xc_bias", [P, 2, KD], F32)
        bias_v = c.sb(ctx, "xc_bias_v", [P, D], F32)
        full = c.sb(ctx, "xc_full", [P, 2, 512], F32)
        rest = c.sb(ctx, "xc_rest", [P, 2, 512], F32)
        part = c.sb(ctx, "xc_part", [P, 2, parts, 512], dt)
        w_in, mm, s_full, high, s_rest, mid, low, sent, v_set, v_zero = (
            c.sig(k) for k in ("w_in", "pr_mm", "pr_full", "pr_high", "pr_rest", "pr_mid", "pr_low", "xc_sent",
                               "pr_v", "pr_vzero"))
        sent2 = c.sig("xc_sent2")
        sents = (sent, sent2)
        jobs = [(1, m, 0, B * M) for m in range(blocks)]
        jobs += [(0, m, 512 * g, 512) for g in range(N // 512) for m in range(blocks)]
        nj = len(jobs)
        vjobs = [(j, n0) for j in range(4) for n0 in range(0, rows, 512)]
        vcols = min(512, rows)
        loads = 2 * KD + 2 + (2 * KD + 1 if biased else 0)
        with nc.Block() as block:
            @block.sync
            def _(sp):
                for k in range(2):
                    sp.dma_start(wk[:, k, :], arg["Wk"][96 * k:96 * k + 96, :]).then_inc(w_in.sem, 16)
                    sp.dma_start(wv[:, k, :], arg["Wv"][96 * k:96 * k + 96, :]).then_inc(w_in.sem, 16)
                for k in range(KD):
                    sp.dma_start(wq[:, k, :], arg["Wq"][P * k:P * k + P, :]).then_inc(w_in.sem, 16)
                if biased:
                    for i, b in enumerate(("bq", "bk")):
                        for k in range(KD):
                            sp.dma_start(bias[:, i, k:k + 1],
                                                  arg[b].rearrange("(a b) -> b a", a=KD)[:, k:k + 1]).then_inc(w_in.sem, 16)
                    sp.dma_start(bias_v[:, :], arg["bv"].rearrange("(a b) -> a b", a=1)
                                          .partition_broadcast(P)).then_inc(w_in.sem, 16)
                for n, (i, m, c0, w) in enumerate(jobs):
                    if biased:
                        sp.wait_ge(low.sem, low.at(n + 1))
                    else:
                        sp.wait_ge(s_rest.sem, s_rest.at(n + 1))
                    for k in range(parts):
                        sp.dma_start((scr_q, scr_k)[i][k, P * m:P * m + P, c0:c0 + w],
                                                      raw(part[:, n % 2, k, 0:w])).then_inc(sents[n % 2].sem, 16)
                for i in range(2):
                    sp.wait_ge(sents[i].sem, sents[i].at(16 * parts * len(range(i, nj, 2))))

            @block.gpsimd
            def _(pool):
                pool.memset(v_all[:, :, :, width:vw], 0.0).then_inc(v_zero.sem, 1)
                pool.wait_ge(v_zero.sem, v_zero.at(1))
                pool.memset(v_all[:, :, :, width:width + 1], 1.0).then_inc(v_zero.sem, 1)

            @block.tensor
            def _(pe):
                ln.tensor(pe)
                pe.wait_ge(w_in.sem, w_in.at(16 * loads))
                ln.wait_xt(pe, 3)
                for n, (i, m, c0, w) in enumerate(jobs):
                    if n >= 8:
                        pe.wait_ge(s_rest.sem, s_rest.at(n - 7))
                    for k in range(2):
                        src, wt = (ct, wk) if i else (xt, wq)
                        last = pe.matmul(ps[:, n % 8, 0:w], wt[:, k, P * m:P * m + P], src[:, k, c0:c0 + w],
                                         start=(k == 0), stop=(k == 1))
                    last.then_inc(mm.sem, 1)
                for u, (j, n0) in enumerate(vjobs):
                    if u < 8:
                        pe.wait_ge(s_rest.sem, s_rest.at(nj - 7 + u))
                    else:
                        pe.wait_ge(v_set.sem, v_set.at(u - 7))
                    for k in range(2):
                        last = pe.matmul(ps[0:MH, (nj + u) % 8, 0:vcols], ct[:, k, MH * j:MH * j + MH],
                                         wv[:, k, n0:n0 + vcols], start=(k == 0), stop=(k == 1))
                    last.then_inc(mm.sem, 1)

            @block.scalar
            def _(act):
                ln.scalar(act)
                ln.scalar_xt(act, xt)
                act.wait_ge(w_in.sem, w_in.at(16 * loads))
                for n, (i, m, c0, w) in enumerate(jobs):
                    act.wait_ge(mm.sem, mm.at(n + 1))
                    if n >= 2:
                        act.wait_ge(s_rest.sem, s_rest.at(n - 1))
                        act.wait_ge(sents[n % 2].sem, sents[n % 2].at(16 * parts * (n // 2)))
                    b = bias[:, i, m:m + 1] if biased else 0.0
                    if biased:
                        act.activation(full[:, n % 2, 0:w], ps[:, n % 8, 0:w], ACT.Identity, bias=b).then_inc(s_full.sem, 1)
                        act.activation(part[:, n % 2, 0, 0:w], ps[:, n % 8, 0:w], ACT.Identity, bias=b).then_inc(high.sem, 1)
                        if n >= 1:
                            pw = jobs[n - 1][3]
                            act.wait_ge(s_rest.sem, s_rest.at(n))
                            act.activation(part[:, (n - 1) % 2, 1, 0:pw], rest[:, (n - 1) % 2, 0:pw], ACT.Copy).then_inc(mid.sem, 1)
                    else:
                        act.activation(part[:, n % 2, 0, 0:w], ps[:, n % 8, 0:w], ACT.Copy).then_inc(high.sem, 1)
                if biased:
                    act.wait_ge(s_rest.sem, s_rest.at(nj))
                    pw = jobs[-1][3]
                    act.activation(part[:, (nj - 1) % 2, 1, 0:pw], rest[:, (nj - 1) % 2, 0:pw], ACT.Copy).then_inc(mid.sem, 1)

            @block.vector
            def _(dve):
                ln.vector(dve)
                ln.vector_xt(dve, xt)
                dve.wait_ge(w_in.sem, w_in.at(16 * loads))

                def lows(q):
                    w = jobs[q][3]
                    dve.wait_ge(mid.sem, mid.at(q + 1))
                    dve.tensor_tensor(part[:, q % 2, 2, 0:w], rest[:, q % 2, 0:w], part[:, q % 2, 1, 0:w],
                                              ALU.subtract).then_inc(low.sem, 1)
                for n, (i, m, c0, w) in enumerate(jobs):
                    dve.wait_ge(high.sem, high.at(n + 1))
                    if biased:
                        dve.wait_ge(s_full.sem, s_full.at(n + 1))
                        if n >= 2:
                            dve.wait_ge(low.sem, low.at(n - 1))
                        dve.tensor_tensor(rest[:, n % 2, 0:w], full[:, n % 2, 0:w], part[:, n % 2, 0, 0:w],
                                                     ALU.subtract).then_inc(s_rest.sem, 1)
                        if n >= 1:
                            lows(n - 1)
                    else:
                        dve.tensor_tensor(part[:, n % 2, 1, 0:w], ps[:, n % 8, 0:w],
                                                     part[:, n % 2, 0, 0:w].bitcast(F32), ALU.subtract).then_inc(s_rest.sem, 1)
                if biased:
                    lows(nj - 1)
                dve.wait_ge(v_zero.sem, v_zero.at(2))
                for u, (j, n0) in enumerate(vjobs):
                    dve.wait_ge(mm.sem, mm.at(nj + u + 1))
                    h0, hn = n0 // width, vcols // width
                    src = ps[0:MH, (nj + u) % 8, 0:vcols].rearrange("p (h e) -> p h e", h=hn)
                    dst = v_all[:, j, h0:h0 + hn, 0:width]
                    if biased:
                        dve.tensor_tensor(dst, src, bias_v[0:MH, :].rearrange("p (h e) -> p h e", h=hn),
                                                    ALU.add).then_inc(v_set.sem, 1)
                    else:
                        dve.tensor_copy(dst, src).then_inc(v_set.sem, 1)
        ln.done()
        for s, k in ((w_in, 16 * loads), (mm, nj + len(vjobs)), (s_full, nj * biased), (high, nj), (s_rest, nj),
                     (mid, nj * biased), (low, nj * biased), (v_set, len(vjobs)), (v_zero, 2),
                     (sent, 16 * parts * ((nj + 1) // 2)), (sent2, 16 * parts * (nj // 2))):
            s.passed(k)


def project_out(c, name, o_tok, blocks, weight, bias):
    nc, ps = c.nc, c.ps
    banks = -(-blocks // 4)
    with ExitStack() as ctx:
        w = c.sb(ctx, name + "_w", [P, blocks, D], F32)
        bb = c.sb(ctx, name + "_b", [P, D], F32)
        ot = c.sb(ctx, name + "_ot", [P, 2, blocks * P], F32)
        w_in, turned, copied, mm, added, biased = (c.sig(k) for k in ("w_in", "po_turned", "po_copied", "po_mm",
                                                                      "po_added", "po_biased"))
        with nc.Block() as block:
            @block.sync
            def _(sp):
                sp.dma_start(bb[:, :], bias.rearrange("(a b) -> a b", a=1).partition_broadcast(P)).then_inc(w_in.sem, 16)
                sp.dma_start(w[:, :, :], weight.rearrange("(k p) n -> p k n", p=P)).then_inc(w_in.sem, 16)

            @block.gpsimd
            def _(pool):
                pool.wait_ge(w_in.sem, w_in.at(32))
                for t in range(NT):
                    pool.tensor_tensor(c.x[:, t, :], c.x[:, t, :], bb[:, :], ALU.add).then_inc(biased.sem, 1)

            @block.tensor
            def _(pe):
                def turn(t):
                    if t >= 2:
                        pe.wait_ge(copied.sem, copied.at(t - 1))
                    for k in range(blocks):
                        last = pe.transpose(ps[:, 2 * (t % 2) + k // 4, P * (k % 4):P * (k % 4) + P],
                                            o_tok[:, t, P * k:P * k + P], c.ident[:, :])
                    last.then_inc(turned.sem, 1)
                pe.wait_ge(w_in.sem, w_in.at(32))
                turn(0)
                for t in range(NT):
                    if t + 1 < NT:
                        turn(t + 1)
                    pe.wait_ge(copied.sem, copied.at(t + 1))
                    if t >= 2:
                        pe.wait_ge(added.sem, added.at(t - 1))
                    for k in range(blocks):
                        last = pe.matmul(ps[:, 4 + t % 2, 0:D], ot[:, t % 2, P * k:P * k + P], w[:, k, :],
                                         start=(k == 0), stop=(k == blocks - 1))
                    last.then_inc(mm.sem, 1)

            @block.scalar
            def _(act):
                for t in range(NT):
                    act.wait_ge(turned.sem, turned.at(t + 1))
                    if t >= 2:
                        act.wait_ge(mm.sem, mm.at(t - 1))
                    b = 2 * (t % 2)
                    act.activation(ot[:, t % 2, :],
                                              ps[:, b:b + banks, :].rearrange("p b s -> p (b s)")[:, 0:blocks * P],
                                              ACT.Copy).then_inc(copied.sem, 1)

            @block.vector
            def _(dve):
                for t in range(NT):
                    dve.wait_ge(mm.sem, mm.at(t + 1))
                    dve.wait_ge(biased.sem, biased.at(t + 1))
                    dve.tensor_tensor(c.x[:, t, :], ps[:, 4 + t % 2, 0:D], c.x[:, t, :], ALU.add).then_inc(added.sem, 1)
        for s, k in ((w_in, 32), (turned, NT), (copied, NT), (mm, NT), (added, NT), (biased, NT)):
            s.passed(k)


E8 = 8


class Route:

    def __init__(self, c, ctx, name, normalized, weight):
        self.c, self.normalized, self.weight = c, normalized, weight
        self.bias = c.sb(ctx, name + "_bias", [P, E8], F32)
        self.logits = c.sb(ctx, name + "_logits", [P, NT, E8], F32)
        self.exps = c.sb(ctx, name + "_exps", [P, NT, E8], F32)
        self.col = c.sb(ctx, name + "_col", [P, 4, NT], F32)
        self.top = c.sb(ctx, name + "_top", [P, NT, E8], F32)
        self.index = c.sb(ctx, name + "_index", [P, NT, E8], U32)
        self.index_f = c.sb(ctx, name + "_index_f", [P, NT, 2], F32)
        self.pick = c.sb(ctx, name + "_pick", [P, 2, NT, E8], F32)
        self.filled, self.shifted, self.exped, self.chain, self.weighted = (
            c.sig(k) for k in ("rt_logits", "rt_shifted", "rt_exp", "rt_chain", "rt_weighted"))
        self.bank = 7

    def tensor(self, pe, tokens, w):
        for t in range(NT):
            for k in range(KD):
                last = pe.matmul(self.c.ps[:, self.bank, E8 * t:E8 * t + E8], tokens[:, k, P * t:P * t + P],
                                 w[:, k, :], start=(k == 0), stop=(k == KD - 1))
        last.then_inc(self.filled.sem, 1)

    def scalar(self, act):
        act.wait_ge(self.shifted.sem, self.shifted.at(1))
        act.activation(self.exps[:, :, :], self.logits[:, :, :], ACT.Exp).then_inc(self.exped.sem, 1)

    def vector(self, dve):
        def rows(a):
            return a.unsqueeze(2).to_broadcast([P, NT, E8])
        link = Chain(self.chain)
        dve.wait_ge(self.filled.sem, self.filled.at(1))
        ps = self.c.ps[:, self.bank, 0:NT * E8].rearrange("p (t e) -> p t e", e=E8)
        dve.tensor_tensor(self.logits[:, :, :], ps, self.bias[:, :].unsqueeze(1).to_broadcast([P, NT, E8]),
                               ALU.add).then_inc(link.sem, 1)
        dve.wait_ge(link.sem, link.next())
        top, total, inverse, scale = (self.col[:, i, :] for i in range(4))
        dve.tensor_reduce(top, self.logits[:, :, :], AX.X, ALU.max).then_inc(link.sem, 1)
        dve.wait_ge(link.sem, link.next())
        dve.tensor_tensor(self.logits[:, :, :], self.logits[:, :, :], rows(top), ALU.subtract).then_inc(self.shifted.sem, 1)
        dve.wait_ge(self.exped.sem, self.exped.at(1))
        dve.tensor_reduce(total, self.exps[:, :, :], AX.X, ALU.add).then_inc(link.sem, 1)
        dve.wait_ge(link.sem, link.next())
        dve.reciprocal(inverse, total).then_inc(link.sem, 1)
        dve.wait_ge(link.sem, link.next())
        probs = self.logits
        dve.tensor_tensor(probs[:, :, :], self.exps[:, :, :], rows(inverse), ALU.mult).then_inc(link.sem, 1)
        dve.wait_ge(link.sem, link.next())
        for t in range(NT):
            dve.max(self.top[:, t, :], probs[:, t, :]).then_inc(self.chain.sem, 1)
        link.n += NT
        dve.wait_ge(self.chain.sem, self.chain.at(link.n))
        for t in range(NT):
            dve.max_index(self.index[:, t, :], self.top[:, t, :], probs[:, t, :]).then_inc(self.chain.sem, 1)
        link.n += NT
        dve.wait_ge(self.chain.sem, self.chain.at(link.n))
        dve.tensor_copy(self.index_f[:, :, :], self.index[:, :, 0:2]).then_inc(link.sem, 1)
        dve.wait_ge(link.sem, link.next())
        iota = self.c.iota[:, :].unsqueeze(1).to_broadcast([P, NT, E8])
        for j in range(2):
            dve.tensor_tensor(self.pick[:, j, :, :], iota, rows(self.index_f[:, :, j]), ALU.is_equal).then_inc(link.sem, 1)
            dve.wait_ge(link.sem, link.next())
        if self.normalized:
            dve.tensor_tensor(total, self.top[:, :, 0], self.top[:, :, 1], ALU.add).then_inc(link.sem, 1)
            dve.wait_ge(link.sem, link.next())
            dve.reciprocal(scale, total).then_inc(self.weighted.sem, 1)
        else:
            for j in range(2):
                dve.tensor_tensor(self.pick[:, j, :, :], self.pick[:, j, :, :], rows(self.top[:, :, j]), ALU.mult
                                  ).then_inc(link.sem, 1)
                dve.wait_ge(link.sem, link.next())
            dve.tensor_tensor(self.weight[:, :, :], self.pick[:, 0, :, :], self.pick[:, 1, :, :], ALU.add
                              ).then_inc(self.weighted.sem, 1)
        dve.wait_ge(self.weighted.sem, self.weighted.at(1))
        self.chained = link.n

    def done(self):
        for s, n in ((self.filled, 1), (self.shifted, 1), (self.exped, 1), (self.weighted, 1),
                     (self.chain, self.chained)):
            s.passed(n)


def ffn_shared(c):
    nc, ps = c.nc, c.ps
    NC, HB = N // 512, D // P
    with ExitStack() as ctx:
        ln = LayerNorm(c, ctx, "lnf0")
        route = Route(c, ctx, "rt0", False, c.sb(ctx, "rt0_weight", [P, NT, E8], F32))
        xt = c.sb(ctx, "f0_xt", [P, KD, N], F32)
        w1 = c.sb(ctx, "f0_w1", [P, 2, KD, 2 * D], F32)
        w_gate = c.sb(ctx, "f0_gate", [P, KD, E8], F32)
        w2 = c.sb(ctx, "f0_w2", [P, HB, (E8 + 1) * D], F32)
        w2_high = c.sb(ctx, "f0_w2_high", [P, HB, (E8 + 1) * D], F32R)
        w2_low = c.sb(ctx, "f0_w2_low", [P, HB, (E8 + 1) * D], F32R)
        silu = c.sb(ctx, "f0_silu", [P, 2, 512], F32)
        full = c.sb(ctx, "f0_full", [P, 2, 512], F32)
        hid = c.sb(ctx, "f0_hid", [P, 2, 2, HB, 2, 512], F32R)
        w_in, w2_in, w2_h, w2_l = (c.sig(k) for k in ("w_in", "f0_w2_in", "f0_w2_high", "f0_w2_low"))
        pair, s_silu, s_full, s_high, s_low, out, added = (
            c.sig(k) for k in ("f0_pair", "f0_silu", "f0_full", "f0_high", "f0_low", "f0_out", "f0_added"))
        loads = 2 * KD + KD + 1
        pairs = [(g, net, m) for g in range(NC) for net in range(2) for m in range(HB)]
        ppg, OUTS = 2 * HB, E8 // 2 + 1
        with nc.Block() as block:
            @block.sync
            def _(sp):
                for k in range(KD):
                    sp.dma_start(w_gate[:, k, :], c.arg["L0_ffn_w_gate"][P * k:P * k + P, :]).then_inc(w_in.sem, 16)
                    for net, name in enumerate(("L0_ffn_w_shared_in", "L0_ffn_w1_shared")):
                        sp.dma_start(w1[:, net, k, :], c.arg[name][P * k:P * k + P, :]).then_inc(w_in.sem, 16)
                sp.dma_start(route.bias[:, :], c.arg["L0_ffn_gate_bias"].rearrange("(a b) -> a b", a=1)
                                      .partition_broadcast(P)).then_inc(w_in.sem, 16)
                for k in range(HB):
                    sp.dma_start(w2[:, k, 0:E8 * D].rearrange("p (e n) -> p e n", e=E8),
                                           c.arg["L0_ffn_w2"].rearrange("e (k p) n -> k p e n", p=P)[k]).then_inc(w2_in.sem, 16)
                    sp.dma_start(w2[:, k, E8 * D:], c.arg["L0_ffn_w_shared_out"][P * k:P * k + P, :]).then_inc(w2_in.sem, 16)

            @block.tensor
            def _(pe):
                ln.tensor(pe)
                pe.wait_ge(w_in.sem, w_in.at(16 * loads))
                ln.wait_xt(pe, NC - 1)
                route.tensor(pe, xt, w_gate)

                def hidden(g):
                    for n in range(ppg * g, ppg * g + ppg):
                        _, net, m = pairs[n]
                        if n >= 2:
                            pe.wait_ge(s_full.sem, s_full.at(n - 1))
                        for half in range(2):
                            for k in range(KD):
                                last = pe.matmul(ps[:, 2 * (n % 2) + half, :],
                                                 w1[:, net, k, D * half + P * m:D * half + P * m + P],
                                                 xt[:, k, 512 * g:512 * g + 512], start=(k == 0), stop=(k == KD - 1))
                        last.then_inc(pair.sem, 1)

                def outputs(g):
                    pe.wait_ge(s_low.sem, s_low.at(ppg * (g + 1)))
                    if g == 0:
                        pe.wait_ge(w2_h.sem, w2_h.at(HB))
                        pe.wait_ge(w2_l.sem, w2_l.at(HB))
                        pe.wait_ge(route.shifted.sem, route.shifted.at(1))
                    for t in range(4):
                        cols = slice(P * t, P * t + P)
                        for q in range(OUTS):
                            n = OUTS * (4 * g + t) + q
                            if n >= 4:
                                pe.wait_ge(added.sem, added.at(n - 3))
                            net, w = (1, 2 * D) if q < OUTS - 1 else (0, D)
                            w0 = 2 * D * q
                            terms = [(m, part, wt) for m in range(HB)
                                     for part, wt in ((0, w2_high), (1, w2_high), (0, w2_low))]
                            for i, (m, part, wt) in enumerate(terms):
                                last = pe.matmul(ps[:, 4 + n % 4, 0:w], hid[:, g % 2, net, m, part, cols],
                                                 wt[:, m, w0:w0 + w], start=(i == 0), stop=(i == len(terms) - 1))
                            last.then_inc(out.sem, 1)

                hidden(0)
                for g in range(NC):
                    if g + 1 < NC:
                        hidden(g + 1)
                    outputs(g)

            @block.scalar
            def _(act):
                ln.scalar(act)
                ln.scalar_xt(act, xt)
                route.scalar(act)
                act.wait_ge(w2_in.sem, w2_in.at(16 * 2 * HB))
                for k in range(HB):
                    act.activation(w2_high[:, k, :], w2[:, k, :], ACT.Copy).then_inc(w2_h.sem, 1)

                def high(n):
                    g, net, m = pairs[n]
                    if n % ppg == 0 and g >= 2:
                        act.wait_ge(out.sem, out.at(4 * OUTS * (g - 1)))
                    act.wait_ge(s_full.sem, s_full.at(n + 1))
                    act.activation(hid[:, g % 2, net, m, 0, :], full[:, n % 2, :], ACT.Copy).then_inc(s_high.sem, 1)
                for n in range(len(pairs)):
                    act.wait_ge(pair.sem, pair.at(n + 1))
                    if n >= 2:
                        act.wait_ge(s_full.sem, s_full.at(n - 1))
                    act.activation(silu[:, n % 2, :], ps[:, 2 * (n % 2), :], ACT.Silu).then_inc(s_silu.sem, 1)
                    if n % ppg:
                        high(n - 1)
                    if n % ppg == ppg - 1:
                        high(n)

            @block.vector
            def _(dve):
                ln.vector(dve)
                ln.vector_xt(dve, xt)
                dve.wait_ge(w_in.sem, w_in.at(16 * loads))
                route.vector(dve)

                def low(n):
                    g, net, m = pairs[n]
                    dve.wait_ge(s_high.sem, s_high.at(n + 1))
                    dve.tensor_tensor(hid[:, g % 2, net, m, 1, :], full[:, n % 2, :],
                                                hid[:, g % 2, net, m, 0, :].bitcast(F32), ALU.subtract).then_inc(s_low.sem, 1)

                def hidden(g):
                    for n in range(ppg * g, ppg * g + ppg):
                        dve.wait_ge(s_silu.sem, s_silu.at(n + 1))
                        if n >= 2:
                            dve.wait_ge(s_low.sem, s_low.at(n - 1))
                        dve.tensor_tensor(full[:, n % 2, :], silu[:, n % 2, :], ps[:, 2 * (n % 2) + 1, :],
                                                     ALU.mult).then_inc(s_full.sem, 1)
                        if n > ppg * g:
                            low(n - 1)
                    low(ppg * g + ppg - 1)

                def outputs(g):
                    for t in range(4 * g, 4 * g + 4):
                        x = c.x[:, t, :]
                        for q in range(OUTS):
                            n = OUTS * t + q
                            dve.wait_ge(out.sem, out.at(n + 1))
                            o = ps[:, 4 + n % 4, :]
                            if q == OUTS - 1:
                                dve.tensor_tensor(x, o[:, 0:D], x, ALU.add).then_inc(added.sem, 1)
                            else:
                                dve.scalar_tensor_tensor(x, o[:, 0:D], route.weight[:, t, 2 * q:2 * q + 1], x,
                                                               ALU.mult, ALU.add).then_inc(chain.sem, 1)
                                dve.wait_ge(chain.sem, chain.next())
                                dve.scalar_tensor_tensor(x, o[:, D:2 * D],
                                                                   route.weight[:, t, 2 * q + 1:2 * q + 2], x,
                                                                   ALU.mult, ALU.add).then_inc(added.sem, 1)
                            dve.wait_ge(added.sem, added.at(n + 1))

                dve.wait_ge(w2_in.sem, w2_in.at(16 * 2 * HB))
                for k in range(HB):
                    dve.wait_ge(w2_h.sem, w2_h.at(k + 1))
                    dve.tensor_tensor(w2_low[:, k, :], w2[:, k, :], w2_high[:, k, :].bitcast(F32),
                                               ALU.subtract).then_inc(w2_l.sem, 1)
                chain = Chain(c.sig("f0_chain"))
                hidden(0)
                for g in range(NC):
                    if g + 1 < NC:
                        hidden(g + 1)
                    outputs(g)
                c.chained = chain.n
        ln.done()
        route.done()
        c.sig("f0_chain").passed(c.chained)
        np_, no = len(pairs), NT * OUTS
        for s, k in ((w_in, 16 * loads), (w2_in, 32 * HB), (w2_h, HB), (w2_l, HB), (pair, np_), (s_silu, np_),
                     (s_full, np_), (s_high, np_), (s_low, np_), (out, no), (added, no)):
            s.passed(k)


ROUND = 1.5 * 2 ** 23


def quantize_weights(c, ctx):
    nc, ps = c.nc, c.ps
    names = ("w_i", "w_f", "w_g", "w_o")
    NW, EB = len(names), D // P
    wt = c.sb(ctx, "hg_wt", [P, NW, KD, D], BF16)
    unit = c.sb(ctx, "hg_unit", [P, NW], F32)
    with ExitStack() as tmp:
        w = c.sb(tmp, "hg_w", [P, NW, EB, D], F32)
        wq = c.sb(tmp, "hg_wq", [P, NW, EB, D], BF16)
        ones = c.sb(tmp, "hg_ones", [P, P], F32)
        total = c.sb(tmp, "hg_total", [P, NW], F32)
        inverse = c.sb(tmp, "hg_inverse", [P, NW], F32)
        w_in, chain, totals, summed, quant, turned, copied = (c.sig(k) for k in (
            "w_in", "hw_chain", "hw_totals", "hw_summed", "hw_quant", "hw_turned", "hw_copied"))
        with nc.Block() as block:
            @block.sync
            def _(sp):
                for i, name in enumerate(names):
                    sp.dma_start(w[:, i, :, :], c.arg["L1_attn_" + name].rearrange("(b p) d -> p b d", p=P)).then_inc(w_in.sem, 16)

            @block.tensor
            def _(pe):
                pe.wait_ge(totals.sem, totals.at(2))
                pe.matmul(ps[:, 0, 0:NW], ones[:, :], total[:, :], start=True, stop=True).then_inc(summed.sem, 1)
                pe.wait_ge(quant.sem, quant.at(1))
                for i in range(NW):
                    for k in range(KD):
                        for e in range(EB):
                            last = pe.transpose(ps[:, 1 + i, :].bitcast(BF16)[:, D * k + P * e:D * k + P * e + P],
                                                wq[:, i, e, P * k:P * k + P], c.identb[:, :])
                    last.then_inc(turned.sem, 1)

            @block.scalar
            def _(act):
                for i in range(NW):
                    act.wait_ge(turned.sem, turned.at(i + 1))
                    act.activation(wt[:, i, :, :].rearrange("p k e -> p (k e)"),
                                              ps[:, 1 + i, :].bitcast(BF16)[:, 0:KD * D], ACT.Copy).then_inc(copied.sem, 1)

            @block.vector
            def _(dve):
                link = Chain(chain)
                dve.memset(ones[:, :], 1.0).then_inc(totals.sem, 1)
                dve.wait_ge(w_in.sem, w_in.at(16 * NW))
                flat = w[:, :, :, :].rearrange("p i b d -> p i (b d)")
                dve.tensor_reduce(total[:, :], flat, AX.X, ALU.add, apply_absolute_value=True).then_inc(totals.sem, 1)
                dve.wait_ge(summed.sem, summed.at(1))
                dve.tensor_scalar(unit[:, :], ps[:, 0, 0:NW], 1.0 / (D * D), 1e-5, ALU.mult, ALU.max).then_inc(link.sem, 1)
                dve.wait_ge(link.sem, link.next())
                dve.reciprocal(inverse[:, :], unit[:, :]).then_inc(link.sem, 1)
                dve.wait_ge(link.sem, link.next())
                for i in range(NW):
                    dve.tensor_scalar(flat[:, i, :], flat[:, i, :], inverse[:, i:i + 1], ROUND,
                                                ALU.mult, ALU.add).then_inc(chain.sem, 1)
                link.n += NW
                dve.wait_ge(chain.sem, chain.at(link.n))
                dve.tensor_scalar(flat, flat, ROUND, 1.0, ALU.subtract, ALU.min).then_inc(link.sem, 1)
                dve.wait_ge(link.sem, link.next())
                dve.tensor_scalar(wq[:, :, :, :].rearrange("p i b d -> p i (b d)"), flat, -1.0, None,
                                            ALU.max).then_inc(quant.sem, 1)
                c.chained = link.n
    for s, k in ((w_in, 16 * NW), (chain, c.chained), (totals, 2), (summed, 1), (quant, 1), (turned, NW),
                 (copied, NW)):
        s.passed(k)
    return wt, unit


class Rms:

    def __init__(self, c, ctx, name):
        self.sum = c.sb(ctx, name + "_sum", [P, NT], F32)
        self.mean = c.sb(ctx, name + "_mean", [P, NT], F32)
        self.root = c.sb(ctx, name + "_root", [P, NT], F32)
        self.inverse = c.sb(ctx, name + "_inverse", [P, NT], F32)
        self.square = c.sb(ctx, name + "_square", [P, 2, D], F32)
        self.squared, self.meaned, self.rooted, self.inverted = (c.sig(name + k) for k in (
            "_squared", "_meaned", "_rooted", "_inverted"))

    def scalar(self, act, src, ready):
        for t in range(NT):
            ready(act, t)
            if t >= 2:
                act.wait_ge(self.squared.sem, self.squared.at(t - 1))
            act.activation(self.square[:, t % 2, :], src(t), ACT.Square,
                                            accum_out=self.sum[:, t:t + 1]).then_inc(self.squared.sem, 1)
        act.wait_ge(self.meaned.sem, self.meaned.at(1))
        act.activation(self.root[:, :], self.mean[:, :], ACT.Sqrt).then_inc(self.rooted.sem, 1)

    def vector(self, dve):
        dve.wait_ge(self.squared.sem, self.squared.at(NT))
        dve.tensor_scalar(self.mean[:, :], self.sum[:, :], 1.0 / D, EPS, ALU.mult, ALU.add).then_inc(self.meaned.sem, 1)
        dve.wait_ge(self.rooted.sem, self.rooted.at(1))
        dve.reciprocal(self.inverse[:, :], self.root[:, :]).then_inc(self.inverted.sem, 1)
        dve.wait_ge(self.inverted.sem, self.inverted.at(1))

    def done(self):
        for s, k in ((self.squared, NT), (self.meaned, 1), (self.rooted, 1), (self.inverted, 1)):
            s.passed(k)


AHEAD_BITS = 8


class BitInput:

    def __init__(self, c, ctx, name, weights, units):
        self.c, self.name, self.weights, self.units = c, name, weights, units
        self.nw = nw = len(weights)
        self.rms = Rms(c, ctx, name + "_rms")
        self.norm = c.sb(ctx, name + "_norm", [P, nw, D], F32)
        self.shift = c.sb(ctx, name + "_shift", [P, 2], F32)
        self.y = c.sb(ctx, name + "_y", [P, NT, nw, D], F32)
        self.top = c.sb(ctx, name + "_top", [P, NT, nw], F32)
        self.scale = c.sb(ctx, name + "_scale", [P, NT, nw], F32)
        self.unit = c.sb(ctx, name + "_unit", [P, NT, nw], F32)
        self.minus = c.sb(ctx, name + "_minus", [P, NT, nw], F32)
        self.q = c.sb(ctx, name + "_q", [P, 2, nw, D], BF16)
        self.qt = c.sb(ctx, name + "_qt", [P, 2, nw * KD * P], BF16)
        self.norm_in, self.set_, self.chain, self.weighted, self.scaled, self.shifted, self.clipped, self.ints, \
            self.turned, self.copied = (c.sig(name + k) for k in (
                "_norm_in", "_set", "_chain", "_weighted", "_scaled", "_shifted", "_clipped", "_ints", "_turned",
                "_copied"))
        self.chained = 0

    def load(self, sp):
        for i, w in enumerate(self.weights):
            sp.dma_start(self.norm[:, i, :], self.c.arg[w].rearrange("(a b) -> a b", a=1)
                         .partition_broadcast(P)).then_inc(self.norm_in.sem, 16)

    def start(self, dve):
        self.rms.vector(dve)
        dve.wait_ge(self.norm_in.sem, self.norm_in.at(16 * self.nw))

    def rows(self, dve, link, src, t):
        nw = self.nw
        for i in range(nw):
            dve.scalar_tensor_tensor(self.y[:, t, i, :], src, self.rms.inverse[:, t:t + 1], self.norm[:, i, :],
                                     ALU.mult, ALU.mult).then_inc(self.weighted.sem, 1)
        dve.wait_ge(self.weighted.sem, self.weighted.at(nw * (t + 1)))
        dve.tensor_reduce(self.top[:, t, :], self.y[:, t, :, :], AX.X, ALU.max,
                          apply_absolute_value=True).then_inc(link.sem, 1)
        at = link.next()
        if t % 4 == 3:
            g = t // 4
            dve.wait_ge(link.sem, at)
            top, scale, unit, minus = (a[:, 4 * g:4 * g + 4, :] for a in (self.top, self.scale, self.unit, self.minus))
            dve.tensor_scalar(top, top, 1e-5, 1.0 / 127.0, ALU.max, ALU.mult).then_inc(link.sem, 1)
            dve.wait_ge(link.sem, link.next())
            dve.reciprocal(scale, top).then_inc(self.scaled.sem, 1)
            dve.tensor_tensor(unit, top, self.units.unsqueeze(1).to_broadcast([P, 4, nw]),
                              ALU.mult).then_inc(self.scaled.sem, 1)
            dve.wait_ge(self.scaled.sem, self.scaled.at(3 * g + 2))
            dve.tensor_scalar(minus, unit, -1.0, None, ALU.mult).then_inc(self.scaled.sem, 1)
        self.chained = link.n

    def scalar_shift(self, act, t):
        if t == 0:
            act.wait_ge(self.set_.sem, self.set_.at(2))
        act.wait_ge(self.scaled.sem, self.scaled.at(3 * (t // 4) + 3))
        for i in range(self.nw):
            act.activation(self.y[:, t, i, :], self.y[:, t, i, :], ACT.Identity, bias=self.shift[:, 0:1],
                           scale=self.scale[:, t, i:i + 1]).then_inc(self.shifted.sem, 1)

    def scalar_ints(self, act, t):
        act.wait_ge(self.clipped.sem, self.clipped.at(t + 1))
        if t >= 2:
            act.wait_ge(self.turned.sem, self.turned.at(t - 1))
        act.activation(self.q[:, t % 2, :, :], self.y[:, t, :, :], ACT.Identity,
                       bias=self.shift[:, 1:2]).then_inc(self.ints.sem, 1)

    def pool(self, pool):
        pool.memset(self.shift[:, 0:1], ROUND).then_inc(self.set_.sem, 1)
        pool.wait_ge(self.set_.sem, self.set_.at(1))
        pool.memset(self.shift[:, 1:2], -ROUND).then_inc(self.set_.sem, 1)
        for t in range(NT):
            pool.wait_ge(self.shifted.sem, self.shifted.at(self.nw * (t + 1)))
            pool.tensor_scalar(self.y[:, t, :, :], self.y[:, t, :, :], ROUND - 128.0, ROUND + 127.0, ALU.max,
                               ALU.min).then_inc(self.clipped.sem, 1)

    def turn(self, pe, t, bank):
        pe.wait_ge(self.ints.sem, self.ints.at(t + 1))
        if t >= 1:
            pe.wait_ge(self.copied.sem, self.copied.at(t))
        out = self.c.ps[:, bank, :].bitcast(BF16)
        for i in range(self.nw):
            for k in range(KD):
                j = P * (KD * i + k)
                last = pe.transpose(out[:, j:j + P], self.q[:, t % 2, i, P * k:P * k + P], self.c.identb[:, :])
        last.then_inc(self.turned.sem, 1)

    def copy(self, act, t, bank):
        act.wait_ge(self.turned.sem, self.turned.at(t + 1))
        act.activation(self.qt[:, t % 2, :], self.c.ps[:, bank, :].bitcast(BF16)[:, 0:self.nw * KD * P],
                       ACT.Copy).then_inc(self.copied.sem, 1)

    def part(self, t, i, k):
        j = P * (KD * i + k)
        return self.qt[:, t % 2, j:j + P]

    def done(self):
        self.rms.done()
        for s, k in ((self.norm_in, 16 * self.nw), (self.set_, 2), (self.chain, self.chained),
                     (self.weighted, NT * self.nw), (self.scaled, 3 * NT // 4), (self.shifted, NT * self.nw),
                     (self.clipped, NT), (self.ints, NT), (self.turned, NT), (self.copied, NT)):
            s.passed(k)


def recurrent(c):
    with ExitStack() as ctx:
        wt, unit = quantize_weights(c, ctx)
        gate = c.sb(ctx, "hg_gate", [P, NT, D], F32)
        h = c.sb(ctx, "hg_h", [P, KD, N], F32)
        recur(c, wt, unit, gate, h)
        recur_out(c, wt, unit, gate, h)


def recur(c, wt, unit, gate, h):
    nc, ps = c.nc, c.ps
    TURN, GATE, FI, SCAN = 0, 1, 2, 4
    with ExitStack() as ctx:
        ln = LayerNorm(c, ctx, "lnr")
        bits = BitInput(c, ctx, "bi", ("L1_attn_nw_i", "L1_attn_nw_f", "L1_attn_nw_g"), unit[:, 0:3])
        forget = c.sb(ctx, "hg_forget", [P, 2, D], F32)
        keep = c.sb(ctx, "hg_keep", [P, 2, D], F32)
        sig_g = c.sb(ctx, "hg_sig_g", [P, 2, D], F32)
        new = c.sb(ctx, "hg_new", [P, 2, D], F32)
        forget_t = c.sb(ctx, "hg_forget_t", [P, 2, KD * 2 * P], F32)
        mm, s_forget, s_keep, s_gate, s_new, turned, s_forget_t, scanned = (c.sig(k) for k in (
            "hg_mm", "hg_forget", "hg_keep", "hg_gate", "hg_new", "hg_turned", "hg_forget_t", "hg_scanned"))
        with nc.Block() as block:
            @block.sync
            def _(sp):
                bits.load(sp)

            @block.gpsimd
            def _(pool):
                bits.pool(pool)

            @block.tensor
            def _(pe):
                def turn_out(t):
                    pe.wait_ge(s_new.sem, s_new.at(t + 1))
                    pair = t // 2
                    if t % 2 == 0 and pair >= 2:
                        pe.wait_ge(scanned.sem, scanned.at(KD * (pair - 1)))
                    for i, src in enumerate((forget, new)):
                        for k in range(KD):
                            col = 2 * P * k + P * (t % 2)
                            last = pe.transpose(ps[:, SCAN + 2 * (pair % 2) + i, col:col + P],
                                                src[:, t % 2, P * k:P * k + P], c.ident[:, :])
                    last.then_inc(turned.sem, 1)

                bits.turn(pe, 0, TURN)
                for t in range(NT):
                    pe.wait_ge(bits.copied.sem, bits.copied.at(t + 1))
                    if t >= 2:
                        pe.wait_ge(s_new.sem, s_new.at(t - 1))
                    for i, out in ((1, ps[:, FI + t % 2, 0:D]), (0, ps[:, FI + t % 2, D:2 * D]),
                                   (2, ps[:, GATE, 0:D])):
                        if i == 2 and t:
                            pe.wait_ge(s_gate.sem, s_gate.at(2 * t))
                        for k in range(KD):
                            last = pe.matmul(out, bits.part(t, i, k), wt[:, i, k, :], start=(k == 0),
                                             stop=(k == KD - 1))
                        last.then_inc(mm.sem, 1)
                    if t + 1 < NT:
                        bits.turn(pe, t + 1, TURN)
                    if t >= 1:
                        turn_out(t - 1)
                turn_out(NT - 1)

            @block.scalar
            def _(act):
                ln.scalar(act)

                def ready(eng, t):
                    eng.wait_ge(ln.s["xn"].sem, ln.s["xn"].at(t + 1))
                bits.rms.scalar(act, lambda t: ln.xn[:, t, :], ready)

                def copy_forget(pair):
                    act.wait_ge(turned.sem, turned.at(2 * pair + 2))
                    if pair >= 2:
                        act.wait_ge(scanned.sem, scanned.at(KD * (pair - 1)))
                    act.activation(forget_t[:, pair % 2, :], ps[:, SCAN + 2 * (pair % 2), :],
                                   ACT.Copy).then_inc(s_forget_t.sem, 1)

                def gates(t):
                    act.wait_ge(mm.sem, mm.at(3 * t + 2))
                    if t >= 2:
                        act.wait_ge(turned.sem, turned.at(t - 1))
                        act.wait_ge(s_gate.sem, s_gate.at(2 * (t - 1)))
                        act.wait_ge(s_new.sem, s_new.at(t - 1))
                    src = ps[:, FI + t % 2, 0:D]
                    act.activation(forget[:, t % 2, :], src, ACT.Sigmoid, scale=bits.unit[:, t, 1:2]
                                   ).then_inc(s_forget.sem, 1)
                    act.activation(keep[:, t % 2, :], src, ACT.Sigmoid, scale=bits.minus[:, t, 1:2]
                                   ).then_inc(s_keep.sem, 1)
                    act.wait_ge(mm.sem, mm.at(3 * t + 3))
                    act.activation(sig_g[:, t % 2, :], ps[:, GATE, 0:D], ACT.Sigmoid, scale=bits.unit[:, t, 2:3]
                                   ).then_inc(s_gate.sem, 1)

                for t in range(3):
                    bits.scalar_shift(act, t)
                bits.scalar_ints(act, 0)
                for t in range(NT):
                    if t + 3 < NT:
                        bits.scalar_shift(act, t + 3)
                    if t + 1 < NT:
                        bits.scalar_ints(act, t + 1)
                    bits.copy(act, t, TURN)
                    if t >= 1:
                        gates(t - 1)
                    if t % 2 == 1 and t >= 3:
                        copy_forget((t - 3) // 2)
                gates(NT - 1)
                copy_forget(NT // 2 - 1)

            @block.vector
            def _(dve):
                ln.vector(dve)
                dve.wait_ge(ln.s["xn"].sem, ln.s["xn"].at(NT))
                link = Chain(bits.chain)
                bits.start(dve)
                for t in range(AHEAD_BITS):
                    bits.rows(dve, link, ln.xn[:, t, :], t)

                def scan(pair):
                    dve.wait_ge(s_forget_t.sem, s_forget_t.at(pair + 1))
                    t = 2 * pair
                    if pair:
                        dve.wait_ge(scanned.sem, scanned.at(KD * pair))
                    for k in range(KD):
                        bank = SCAN + 2 * (pair % 2)
                        first = 0.0 if t % ST == 0 else h[:, k, P * t - 1:P * t]
                        dve.tensor_tensor_scan(h[:, k, P * t:P * t + 2 * P],
                                                           forget_t[:, pair % 2, 2 * P * k:2 * P * k + 2 * P],
                                                           ps[:, bank + 1, 2 * P * k:2 * P * k + 2 * P],
                                                           first, ALU.mult, ALU.add).then_inc(scanned.sem, 1)
                for t in range(NT):
                    dve.wait_ge(s_gate.sem, s_gate.at(2 * t + 1))
                    dve.scalar_tensor_tensor(gate[:, t, :], ps[:, GATE, 0:D], bits.unit[:, t, 2:3], sig_g[:, t % 2, :],
                                             ALU.mult, ALU.mult).then_inc(s_gate.sem, 1)
                    dve.wait_ge(s_keep.sem, s_keep.at(t + 1))
                    if t >= 2:
                        dve.wait_ge(turned.sem, turned.at(t - 1))
                    dve.scalar_tensor_tensor(new[:, t % 2, :], ps[:, FI + t % 2, D:2 * D], bits.unit[:, t, 0:1],
                                             keep[:, t % 2, :], ALU.mult, ALU.mult).then_inc(s_new.sem, 1)
                    if t % 2 == 1 and t >= 3:
                        scan((t - 3) // 2)
                    if t + AHEAD_BITS < NT:
                        bits.rows(dve, link, ln.xn[:, t + AHEAD_BITS, :], t + AHEAD_BITS)
                scan(NT // 2 - 1)
        ln.done(turned=False)
        bits.done()
        for s, k in ((mm, 3 * NT), (s_forget, NT), (s_keep, NT), (s_gate, 2 * NT), (s_new, NT), (turned, NT),
                     (s_forget_t, NT // 2), (scanned, KD * NT // 2)):
            s.passed(k)


def recur_out(c, wt, unit, gate, h):
    nc, ps = c.nc, c.ps
    with ExitStack() as ctx:
        rms = Rms(c, ctx, "rh")
        bits = BitInput(c, ctx, "bo", ("L1_attn_nw_o",), unit[:, 3:4])
        norm = c.sb(ctx, "hg_norm", [P, D], F32)
        y = c.sb(ctx, "hg_y", [P, NT, D], F32)
        n_in, turned, normed, gated, mm, added = (c.sig(k) for k in ("ho_norm", "ho_turned", "ho_normed", "ho_gated",
                                                                     "ho_mm", "ho_added"))

        def out_t(t):
            return ps[:, t // 2, D * (t % 2):D * (t % 2) + D]
        with nc.Block() as block:
            @block.sync
            def _(sp):
                sp.dma_start(norm[:, :], c.arg["L1_attn_g_norm_w"].rearrange("(a b) -> a b", a=1)
                                      .partition_broadcast(P)).then_inc(n_in.sem, 16)
                bits.load(sp)

            @block.gpsimd
            def _(pool):
                bits.pool(pool)

            @block.tensor
            def _(pe):
                for t in range(NT):
                    for k in range(KD):
                        last = pe.transpose(out_t(t)[:, P * k:P * k + P], h[:, k, P * t:P * t + P], c.ident[:, :])
                    last.then_inc(turned.sem, 1)
                pe.wait_ge(normed.sem, normed.at(NT))
                bits.turn(pe, 0, 0)
                for t in range(NT):
                    pe.wait_ge(bits.copied.sem, bits.copied.at(t + 1))
                    if t >= 2:
                        pe.wait_ge(added.sem, added.at(t - 1))
                    for k in range(KD):
                        last = pe.matmul(ps[:, 1 + t % 2, 0:D], bits.part(t, 0, k), wt[:, 3, k, :], start=(k == 0),
                                         stop=(k == KD - 1))
                    last.then_inc(mm.sem, 1)
                    if t + 1 < NT:
                        bits.turn(pe, t + 1, 0)

            @block.scalar
            def _(act):
                rms.scalar(act, out_t, lambda eng, t: eng.wait_ge(turned.sem, turned.at(2 * (t // 2) + 2)))
                bits.rms.scalar(act, lambda t: y[:, t, :], lambda eng, t: eng.wait_ge(gated.sem, gated.at(t + 1)))
                for t in range(3):
                    bits.scalar_shift(act, t)
                bits.scalar_ints(act, 0)
                for t in range(NT):
                    if t + 3 < NT:
                        bits.scalar_shift(act, t + 3)
                    if t + 1 < NT:
                        bits.scalar_ints(act, t + 1)
                    if t >= 2:
                        act.wait_ge(mm.sem, mm.at(t - 1))
                    bits.copy(act, t, 0)

            @block.vector
            def _(dve):
                rms.vector(dve)
                dve.wait_ge(n_in.sem, n_in.at(16))
                for t in range(NT):
                    dve.scalar_tensor_tensor(y[:, t, :], out_t(t), rms.inverse[:, t:t + 1], norm[:, :],
                                                        ALU.mult, ALU.mult).then_inc(normed.sem, 1)
                for t in range(NT):
                    dve.wait_ge(normed.sem, normed.at(t + 1))
                    dve.tensor_tensor(y[:, t, :], y[:, t, :], gate[:, t, :], ALU.mult).then_inc(gated.sem, 1)
                dve.wait_ge(gated.sem, gated.at(NT))
                link = Chain(bits.chain)
                bits.start(dve)
                for t in range(AHEAD_BITS):
                    bits.rows(dve, link, y[:, t, :], t)

                def add(t):
                    dve.wait_ge(mm.sem, mm.at(t + 1))
                    x = c.x[:, t, :]
                    dve.scalar_tensor_tensor(x, ps[:, 1 + t % 2, 0:D], bits.unit[:, t, 0:1], x, ALU.mult,
                                             ALU.add).then_inc(added.sem, 1)
                for t in range(NT):
                    if t >= 4:
                        add(t - 4)
                    if t + AHEAD_BITS < NT:
                        bits.rows(dve, link, y[:, t + AHEAD_BITS, :], t + AHEAD_BITS)
                for t in range(NT - 4, NT):
                    add(t)
        rms.done()
        bits.done()
        for s, k in ((n_in, 16), (turned, NT), (normed, NT), (gated, NT), (mm, NT), (added, NT)):
            s.passed(k)


DM = 1024
HB = DM // P
NG = N // 512
TK = 2
RT = 2 * P
TILES = (TK * N + E8 * (RT - 1)) // RT
BUF = 4


def moe(c, scratch):
    with ExitStack() as ctx:
        rows = scratch("moe_rows", [TILES * RT, D], F32)
        results = scratch("moe_results", [TILES * RT, D], F32)
        b1_cols = scratch("moe_b1", [E8, P, HB], F32)
        place = c.sb(ctx, "moe_place", [P, NT, TK], U32)
        share = c.sb(ctx, "moe_share", [P, NT, TK], F32)
        expert = c.sb(ctx, "moe_expert", [P, TILES], U32)
        moe_prepare(c, rows, b1_cols, place, share, expert)
        moe_experts(c, rows, results, b1_cols, expert)
        moe_collect(c, results, place, share)


class Places:

    def __init__(self, c, ctx):
        self.c = c
        self.ones = c.sb(ctx, "pl_ones", [P, P], F32)
        self.before = c.sb(ctx, "pl_before", [P, P], F32)
        self.tile = c.sb(ctx, "pl_tile", [P, TILES], F32)
        self.chosen = c.sb(ctx, "pl_chosen", [P, NT, E8], F32)
        self.run = c.sb(ctx, "pl_run", [P, NT, E8], F32)
        self.total = c.sb(ctx, "pl_total", [P, E8], F32)
        self.tiles = c.sb(ctx, "pl_tiles", [P, E8], F32)
        self.end = c.sb(ctx, "pl_end", [P, E8], F32)
        self.first = c.sb(ctx, "pl_first", [P, E8], F32)
        self.mine = c.sb(ctx, "pl_mine", [P, TK, NT, E8], F32)
        self.number = c.sb(ctx, "pl_number", [P, NT, TK], F32)
        self.past = c.sb(ctx, "pl_past", [P, TILES, E8], F32)
        self.owner = c.sb(ctx, "pl_owner", [P, TILES], F32)
        self.made, self.counted, self.summed, self.placed = (c.sig(k) for k in ("pl_made", "pl_counted", "pl_summed",
                                                                                "pl_placed"))
        self.bank = 6

    def pool(self, pool):
        link = Chain(self.made)
        pool.memset(self.ones[:, :], 1.0).then_inc(link.sem, 1)
        pool.wait_ge(link.sem, link.next())
        pool.memset(self.before[:, :], 1.0).then_inc(link.sem, 1)
        pool.wait_ge(link.sem, link.next())
        pool.affine_select(out=self.before[:, :], in_=self.before[:, :], compare_op=ALU.is_gt, fill=0.0, base=0,
                           pattern=[[1, P]], channel_multiplier=-1).then_inc(link.sem, 1)
        pool.wait_ge(link.sem, link.next())
        pool.iota(self.tile[:, :], [[1, TILES]], base=0, channel_multiplier=0,
                  allow_small_or_imprecise_dtypes=True).then_inc(link.sem, 1)

    def tensor(self, pe):
        pe.wait_ge(self.made.sem, self.made.at(4))
        pe.wait_ge(self.counted.sem, self.counted.at(1))
        count = self.run[:, NT - 1, :]
        pe.matmul(self.c.ps[:, self.bank, 0:E8], self.before[:, :], count, start=True, stop=True)
        pe.matmul(self.c.ps[:, self.bank, E8:2 * E8], self.ones[:, :], count, start=True,
                  stop=True).then_inc(self.summed.sem, 1)

    def vector(self, dve, link, pick, place, expert):
        dve.wait_ge(self.made.sem, self.made.at(4))
        dve.tensor_tensor(self.chosen[:, :, :], pick[:, 0, :, :], pick[:, 1, :, :], ALU.add).then_inc(link.sem, 1)
        dve.wait_ge(link.sem, link.next())
        for e in range(E8):
            last = dve.tensor_tensor_scan(self.run[:, :, e], self.ones[:, 0:NT], self.chosen[:, :, e], 0.0, ALU.mult,
                                          ALU.add)
            last.then_inc(link.sem, 1)
            at = link.next()
        dve.wait_ge(link.sem, at)
        dve.memset(self.total[:, :], 0.0).then_inc(self.counted.sem, 1)
        dve.wait_ge(self.summed.sem, self.summed.at(1))
        ps = self.c.ps[:, self.bank, :]
        dve.tensor_scalar(self.tiles[:, :], ps[:, E8:2 * E8], 1.0 / RT, (RT - 1.0) / RT - (0.5 - 0.5 / RT), ALU.mult,
                          ALU.add).then_inc(link.sem, 1)
        dve.wait_ge(link.sem, link.next())
        dve.tensor_scalar(self.tiles[:, :], self.tiles[:, :], ROUND, None, ALU.add).then_inc(link.sem, 1)
        dve.wait_ge(link.sem, link.next())
        dve.tensor_scalar(self.tiles[:, :], self.tiles[:, :], ROUND, None, ALU.subtract).then_inc(link.sem, 1)
        dve.wait_ge(link.sem, link.next())
        dve.tensor_tensor_scan(self.end[:, :], self.ones[:, 0:E8], self.tiles[:, :], 0.0, ALU.mult,
                               ALU.add).then_inc(link.sem, 1)
        dve.wait_ge(link.sem, link.next())
        dve.tensor_tensor(self.first[:, :], self.end[:, :], self.tiles[:, :], ALU.subtract).then_inc(link.sem, 1)
        dve.wait_ge(link.sem, link.next())
        dve.tensor_scalar(self.first[:, :], self.first[:, :], float(RT), -1.0, ALU.mult,
                          ALU.add).then_inc(link.sem, 1)
        dve.wait_ge(link.sem, link.next())
        dve.tensor_tensor(self.first[:, :], self.first[:, :], ps[:, 0:E8], ALU.add).then_inc(link.sem, 1)
        dve.wait_ge(link.sem, link.next())
        dve.tensor_tensor(self.run[:, :, :], self.run[:, :, :],
                          self.first[:, :].unsqueeze(1).to_broadcast([P, NT, E8]), ALU.add).then_inc(link.sem, 1)
        dve.wait_ge(link.sem, link.next())
        for j in range(TK):
            dve.tensor_tensor(self.mine[:, j, :, :], self.run[:, :, :], pick[:, j, :, :],
                              ALU.mult).then_inc(link.sem, 1)
            dve.wait_ge(link.sem, link.next())
            dve.tensor_reduce(self.number[:, :, j], self.mine[:, j, :, :], AX.X, ALU.add).then_inc(link.sem, 1)
            dve.wait_ge(link.sem, link.next())
        dve.tensor_copy(place[:, :, :], self.number[:, :, :]).then_inc(self.placed.sem, 1)
        dve.tensor_tensor(self.past[:, :, :], self.tile[:, :].unsqueeze(2).to_broadcast([P, TILES, E8]),
                          self.end[:, :].unsqueeze(1).to_broadcast([P, TILES, E8]), ALU.is_ge).then_inc(link.sem, 1)
        dve.wait_ge(link.sem, link.next())
        dve.tensor_reduce(self.owner[:, :], self.past[:, :, :], AX.X, ALU.add).then_inc(link.sem, 1)
        dve.wait_ge(link.sem, link.next())
        dve.tensor_scalar(self.owner[:, :], self.owner[:, :], E8 - 1.0, None, ALU.min).then_inc(link.sem, 1)
        dve.wait_ge(link.sem, link.next())
        dve.tensor_copy(expert[:, :], self.owner[:, :]).then_inc(self.placed.sem, 1)

    def done(self):
        for s, k in ((self.made, 4), (self.counted, 1), (self.summed, 1), (self.placed, 2)):
            s.passed(k)


def moe_prepare(c, rows, b1_cols, place, share, expert):
    nc, ps = c.nc, c.ps
    NB = E8 * HB + KD
    ZERO = 2
    with ExitStack() as ctx:
        ln = LayerNorm(c, ctx, "lnm")
        route = Route(c, ctx, "rt1", True, c.sb(ctx, "rt1_weight", [P, NT, E8], F32))
        places = Places(c, ctx)
        xt = c.sb(ctx, "mp_xt", [P, KD, N], F32)
        full = c.sb(ctx, "mp_full", [P, KD, N], F32)
        token = c.sb(ctx, "mp_token", [P, NT, D], F32)
        w = c.sb(ctx, "mp_w", [P, KD, D], F32)
        w_gate = c.sb(ctx, "mp_gate", [P, KD, E8], F32)
        bias_rows = c.sb(ctx, "mp_bias_rows", [NB, P], F32)
        bias = c.sb(ctx, "mp_bias", [P, NB], F32)
        per = TILES * RT // ZERO // P
        zeros = c.sb(ctx, "mp_zeros", [P, per * D], F32)
        w_in, bturn, bset, mm, s_full, zero, zeroed, bsent, tturn, tset = (c.sig(k) for k in (
            "w_in", "mp_bturn", "mp_bset", "mp_mm", "mp_full", "mp_zero", "mp_zeroed", "mp_bsent", "mp_tturn",
            "mp_tset"))
        sent = c.own_sig("mp_sent")
        loads = 3 + 2 * KD
        jobs = [(g, m) for g in range(NG) for m in range(KD)]
        with nc.Block() as block:
            @block.sync
            def _(sp):
                sp.dma_start(bias_rows[0:E8 * HB, :],
                             c.arg["L1_ffn_b1"].rearrange("e (k p) -> (e k) p", p=P)).then_inc(w_in.sem, 16)
                sp.dma_start(bias_rows[E8 * HB:NB, :],
                             c.arg["L1_ffn_b_in"].rearrange("(k p) -> k p", p=P)).then_inc(w_in.sem, 16)
                for k in range(KD):
                    sp.dma_start(w[:, k, :], c.arg["L1_ffn_W_in"][P * k:P * k + P, :]).then_inc(w_in.sem, 16)
                    sp.dma_start(w_gate[:, k, :], c.arg["L1_ffn_W_gate"][P * k:P * k + P, :]).then_inc(w_in.sem, 16)
                sp.dma_start(route.bias[:, :], c.arg["L1_ffn_b_gate"].rearrange("(a b) -> a b", a=1)
                             .partition_broadcast(P)).then_inc(w_in.sem, 16)
                sp.wait_ge(zero.sem, zero.at(1))
                for i in range(ZERO):
                    sp.dma_start(rows[P * per * i:P * per * (i + 1), :].rearrange("(p r) d -> p (r d)", p=P),
                                 zeros[:, :]).then_inc(zeroed.sem, 16)
                sp.wait_ge(bset.sem, bset.at(1))
                sp.dma_start(b1_cols.rearrange("e p k -> p e k"),
                             bias[:, 0:E8 * HB].rearrange("p (e k) -> p e k", e=E8)).then_inc(bsent.sem, 16)
                sp.wait_ge(bsent.sem, bsent.at(16))
                sp.wait_ge(zeroed.sem, zeroed.at(16 * ZERO))

            @block.gpsimd
            def _(pool):
                pool.memset(zeros[:, :], 0.0).then_inc(zero.sem, 1)
                places.pool(pool)
                pool.wait_ge(zeroed.sem, zeroed.at(16 * ZERO))
                pool.wait_ge(places.placed.sem, places.placed.at(1))
                for t in range(NT):
                    pool.wait_ge(tset.sem, tset.at(t + 1))
                    for j in range(TK):
                        pool.indirect_dma_start(rows, bass.IndirectOffsetOnAxis(ap=place[:, t, j:j + 1], axis=0),
                                                token[:, t, :], None).then_inc(sent.sem, 16)
                pool.wait_ge(sent.sem, sent.at(16 * NT * TK))

            @block.tensor
            def _(pe):
                ln.tensor(pe)
                pe.wait_ge(w_in.sem, w_in.at(16 * loads))
                ln.wait_xt(pe, NG - 1)
                pe.transpose(ps[:, 7, 0:NB], bias_rows[:, :], c.ident[0:NB, 0:NB]).then_inc(bturn.sem, 1)
                for n, (g, m) in enumerate(jobs):
                    if n >= 4:
                        pe.wait_ge(s_full.sem, s_full.at(n - 3))
                    for k in range(KD):
                        last = pe.matmul(ps[:, n % 4, :], w[:, k, P * m:P * m + P], xt[:, k, 512 * g:512 * g + 512],
                                         start=(k == 0), stop=(k == KD - 1))
                    last.then_inc(mm.sem, 1)
                pe.wait_ge(s_full.sem, s_full.at(len(jobs)))
                pe.wait_ge(bset.sem, bset.at(1))
                route.tensor(pe, full, w_gate)
                for t in range(NT):
                    if t >= 8 and t % 2 == 0:
                        pe.wait_ge(tset.sem, tset.at(t - 6))
                    for k in range(KD):
                        last = pe.transpose(ps[:, t // 2 % 4, D * (t % 2) + P * k:D * (t % 2) + P * k + P],
                                            full[:, k, P * t:P * t + P], c.ident[:, :])
                    last.then_inc(tturn.sem, 1)
                places.tensor(pe)

            @block.scalar
            def _(act):
                ln.scalar(act)
                ln.scalar_xt(act, xt)
                act.wait_ge(bset.sem, bset.at(1))
                for n, (g, m) in enumerate(jobs):
                    act.wait_ge(mm.sem, mm.at(n + 1))
                    act.activation(full[:, m, 512 * g:512 * g + 512], ps[:, n % 4, :], ACT.Identity,
                                   bias=bias[:, E8 * HB + m:E8 * HB + m + 1]).then_inc(s_full.sem, 1)
                for t in range(NT):
                    act.wait_ge(tturn.sem, tturn.at(2 * (t // 2) + 2))
                    act.activation(token[:, t, :], ps[:, t // 2 % 4, D * (t % 2):D * (t % 2) + D],
                                   ACT.Copy).then_inc(tset.sem, 1)
                    if t == 3:
                        route.scalar(act)

            @block.vector
            def _(dve):
                ln.vector(dve)
                ln.vector_xt(dve, xt)
                dve.wait_ge(bturn.sem, bturn.at(1))
                dve.tensor_copy(bias[:, :], ps[:, 7, 0:NB]).then_inc(bset.sem, 1)
                route.vector(dve)
                link = Chain(c.sig("mp_chain"))
                dve.tensor_tensor(share[:, :, :], route.top[:, :, 0:TK],
                                  route.col[:, 3, :].unsqueeze(2).to_broadcast([P, NT, TK]),
                                  ALU.mult).then_inc(link.sem, 1)
                dve.wait_ge(link.sem, link.next())
                places.vector(dve, link, route.pick, place, expert)
                c.chained = link.n
        ln.done()
        route.done()
        places.done()
        nj = len(jobs)
        for s, k in ((w_in, 16 * loads), (bturn, 1), (bset, 1), (mm, nj), (s_full, nj), (zero, 1),
                     (zeroed, 16 * ZERO), (bsent, 16), (tturn, NT), (tset, NT), (sent, 16 * NT * TK),
                     (c.sig("mp_chain"), c.chained)):
            s.passed(k)


def moe_experts(c, rows, results, b1_cols, expert):
    nc, ps = c.nc, c.ps
    TURN, MID, OUT = (0, 7), 1, 5
    with ExitStack() as ctx:
        chunk = c.sb(ctx, "me_chunk", [P, BUF, DM], F32)
        w = c.sb(ctx, "me_w_parts", [P, 2, 2, 2, 2 * DM], F32R)
        b1 = c.sb(ctx, "me_b1", [P, BUF, HB], F32)
        b2 = c.sb(ctx, "me_b2", [P, BUF, D], F32)
        row = c.sb(ctx, "me_row", [P, 2, RT // P, D], F32)
        h = c.sb(ctx, "me_h", [P, 2, 2, KD, RT], F32R)
        full = c.sb(ctx, "me_full", [P, 4, RT], F32)
        mid = c.sb(ctx, "me_mid", [P, 2, HB, 2, RT], F32R)
        result = c.sb(ctx, "me_result", [P, 2, RT // P, D], F32)
        w_in = [c.sig(f"me_w_in{i}") for i in range(BUF)]
        b_in = [c.sig(f"me_b_in{i}") for i in range(BUF)]
        row_in = [c.sig(f"me_row_in{i}") for i in range(2)]
        stored = [c.own_sig(f"me_stored{i}") for i in range(2)]
        turned, h_high, h_low, w_high, w_low, mm, s_full, high, low, out, added = (c.sig(k) for k in (
            "me_turned", "me_h_high", "me_h_low", "me_w_high", "me_w_low", "me_mm", "me_full", "me_high", "me_low",
            "me_out", "me_added"))
        TERMS = ((0, 0), (1, 0), (0, 1))
        SUB = RT // P
        SPLITS = {2: (2,), 5: (3,), HB - 2: (4,), HB - 1: (5,)}

        def part(n, i):
            u, q = divmod(n, 4)
            return w[:, u % 2, q // 2, i, DM * (q % 2):DM * (q % 2) + DM]

        def chunks_at(u, b):
            return [n for n in (4 * u + q for q in SPLITS.get(b, ())) if n < 4 * TILES]

        with nc.Block() as block:
            @block.sync
            def _(sp):
                for u in range(TILES):
                    e = sp.value_load(expert[0:1, u:u + 1], min_val=0, max_val=E8 - 1)
                    if u >= 2:
                        sp.wait_ge(turned.sem, turned.at(u - 1))
                    sp.dma_start(row[:, u % 2, :, :], rows[RT * u:RT * u + RT, :].rearrange("(a p) d -> p a d", p=P)
                                 ).then_inc(row_in[u % 2].sem, 16)
                    if u >= BUF:
                        sp.wait_ge(added.sem, added.at(SUB * (u - BUF + 1)))
                    sp.dma_start(b1[:, u % BUF, :], b1_cols[bass.ds(e, 1), :, :].rearrange("a p k -> p (a k)")
                                 ).then_inc(b_in[u % BUF].sem, 16)
                    sp.dma_start(b2[:, u % BUF, :], c.arg["L1_ffn_b2"][bass.ds(e, 1), :].partition_broadcast(P)
                                 ).then_inc(b_in[u % BUF].sem, 16)
                    for q in range(4):
                        n = 4 * u + q
                        if n >= BUF:
                            sp.wait_ge(w_low.sem, w_low.at(n - BUF + 1))
                        if q < 2:
                            src = c.arg["L1_ffn_W1"][bass.ds(e, 1), P * q:P * q + P, :].rearrange("a p n -> p (a n)")
                            dst = chunk[:, n % BUF, :]
                        else:
                            r0 = DM // 2 * (q - 2)
                            src = c.arg["L1_ffn_W2"][bass.ds(e, 1), r0:r0 + DM // 2, :].rearrange(
                                "a (k p) n -> p (a k) n", p=P)
                            dst = chunk[:, n % BUF, :].rearrange("p (k n) -> p k n", n=D)
                        sp.dma_start(dst, src).then_inc(w_in[n % BUF].sem, 16)

            @block.gpsimd
            def _(pool):
                for u in range(TILES):
                    pool.wait_ge(added.sem, added.at(SUB * (u + 1)))
                    pool.dma_start(results[RT * u:RT * u + RT, :].rearrange("(a p) d -> p a d", p=P),
                                   result[:, u % 2, :, :]).then_inc(stored[u % 2].sem, 16)
                for i in range(2):
                    pool.wait_ge(stored[i].sem, stored[i].at(16 * len(range(i, TILES, 2))))

            @block.tensor
            def _(pe):
                def turn(u):
                    pe.wait_ge(row_in[u % 2].sem, row_in[u % 2].at(16 * (u // 2 + 1)))
                    if u >= 2:
                        pe.wait_ge(h_low.sem, h_low.at(u - 1))
                    for k in range(KD):
                        for a in range(SUB):
                            last = pe.transpose(ps[:, TURN[u % 2], RT * k + P * a:RT * k + P * a + P],
                                                row[:, u % 2, a, P * k:P * k + P], c.ident[:, :])
                    last.then_inc(turned.sem, 1)

                def first(u):
                    pe.wait_ge(h_low.sem, h_low.at(u + 1))
                    pe.wait_ge(w_low.sem, w_low.at(4 * u + 2))
                    for b in range(HB):
                        n = HB * u + b
                        if n >= 4:
                            pe.wait_ge(high.sem, high.at(n - 3))
                        terms = [(k, i, j) for k in range(KD) for i, j in TERMS]
                        for m, (k, i, j) in enumerate(terms):
                            last = pe.matmul(ps[:, MID + n % 4, 0:RT],
                                             w[:, u % 2, 0, i, DM * k + P * b:DM * k + P * b + P],
                                             h[:, u % 2, j, k, :], start=(m == 0), stop=(m == len(terms) - 1))
                        last.then_inc(mm.sem, 1)

                def second(u):
                    pe.wait_ge(w_low.sem, w_low.at(4 * u + 4))
                    pe.wait_ge(low.sem, low.at(HB * (u + 1)))
                    for a in range(SUB):
                        n = SUB * u + a
                        if n >= 2:
                            pe.wait_ge(added.sem, added.at(n - 1))
                        terms = [(b, i, j) for b in range(HB) for i, j in TERMS]
                        for m, (b, i, j) in enumerate(terms):
                            last = pe.matmul(ps[:, OUT + n % 2, 0:D], mid[:, u % 2, b, i, P * a:P * a + P],
                                             w[:, u % 2, 1, j, D * b:D * b + D], start=(m == 0),
                                             stop=(m == len(terms) - 1))
                        last.then_inc(out.sem, 1)

                turn(0)
                first(0)
                turn(1)
                for u in range(TILES):
                    if u + 1 < TILES:
                        first(u + 1)
                    if u + 2 < TILES:
                        turn(u + 2)
                    second(u)

            @block.scalar
            def _(act):
                def split(n):
                    u, q = divmod(n, 4)
                    act.wait_ge(w_in[n % BUF].sem, w_in[n % BUF].at(16 * (n // BUF + 1)))
                    if u >= 2 and q < 2:
                        act.wait_ge(mm.sem, mm.at(HB * (u - 1)))
                    elif u >= 2:
                        act.wait_ge(out.sem, out.at(SUB * (u - 1)))
                    act.activation(part(n, 0), chunk[:, n % BUF, :], ACT.Copy).then_inc(w_high.sem, 1)

                def take(u):
                    act.wait_ge(turned.sem, turned.at(u + 1))
                    if u >= 2:
                        act.wait_ge(mm.sem, mm.at(HB * (u - 1)))
                    act.activation(h[:, u % 2, 0, :, :].rearrange("p k r -> p (k r)"), ps[:, TURN[u % 2], :],
                                   ACT.Copy).then_inc(h_high.sem, 1)

                take(0)
                split(0)
                split(1)
                for u in range(TILES):
                    act.wait_ge(b_in[u % BUF].sem, b_in[u % BUF].at(32 * (u // BUF + 1)))
                    for b in range(HB):
                        n = HB * u + b
                        act.wait_ge(mm.sem, mm.at(n + 1))
                        if n >= 4:
                            act.wait_ge(low.sem, low.at(n - 3))
                        if b == 0 and u >= 2:
                            act.wait_ge(out.sem, out.at(SUB * (u - 1)))
                        col = b1[:, u % BUF, b:b + 1]
                        act.activation(full[:, n % 4, :], ps[:, MID + n % 4, 0:RT], ACT.Relu,
                                       bias=col).then_inc(s_full.sem, 1)
                        act.activation(mid[:, u % 2, b, 0, :], ps[:, MID + n % 4, 0:RT], ACT.Relu,
                                       bias=col).then_inc(high.sem, 1)
                        if b == HB - 1 and u + 1 < TILES:
                            take(u + 1)
                        for m in chunks_at(u, b):
                            split(m)

            @block.vector
            def _(dve):
                def split(n):
                    dve.wait_ge(w_high.sem, w_high.at(n + 1))
                    dve.tensor_tensor(part(n, 1), chunk[:, n % BUF, :], raw(part(n, 0)),
                                      ALU.subtract).then_inc(w_low.sem, 1)

                def take(u):
                    dve.wait_ge(h_high.sem, h_high.at(u + 1))
                    dve.tensor_tensor(h[:, u % 2, 1, :, :].rearrange("p k r -> p (k r)"), ps[:, TURN[u % 2], :],
                                      raw(h[:, u % 2, 0, :, :]).rearrange("p k r -> p (k r)"),
                                      ALU.subtract).then_inc(h_low.sem, 1)

                def finish(u):
                    if u >= 2:
                        dve.wait_ge(stored[u % 2].sem, stored[u % 2].at(16 * (u // 2)))
                    dve.wait_ge(b_in[u % BUF].sem, b_in[u % BUF].at(32 * (u // BUF + 1)))
                    for a in range(SUB):
                        n = SUB * u + a
                        dve.wait_ge(out.sem, out.at(n + 1))
                        dve.tensor_tensor(result[:, u % 2, a, :], ps[:, OUT + n % 2, 0:D], b2[:, u % BUF, :],
                                          ALU.add).then_inc(added.sem, 1)

                take(0)
                split(0)
                split(1)
                for u in range(TILES):
                    for b in range(HB):
                        n = HB * u + b
                        dve.wait_ge(s_full.sem, s_full.at(n + 1))
                        dve.wait_ge(high.sem, high.at(n + 1))
                        dve.tensor_tensor(mid[:, u % 2, b, 1, :], full[:, n % 4, :], raw(mid[:, u % 2, b, 0, :]),
                                          ALU.subtract).then_inc(low.sem, 1)
                        if b == HB - 1 and u + 1 < TILES:
                            take(u + 1)
                        for m in chunks_at(u, b):
                            split(m)
                        if b == 4 and u >= 2:
                            finish(u - 2)
                finish(TILES - 2)
                finish(TILES - 1)
        for i in range(BUF):
            w_in[i].passed(16 * len(range(i, 4 * TILES, BUF)))
            b_in[i].passed(32 * len(range(i, TILES, BUF)))
        for i in range(2):
            row_in[i].passed(16 * len(range(i, TILES, 2)))
            stored[i].passed(16 * len(range(i, TILES, 2)))
        for s, k in ((turned, TILES), (h_high, TILES), (h_low, TILES), (w_high, 4 * TILES), (w_low, 4 * TILES),
                     (mm, HB * TILES), (s_full, HB * TILES), (high, HB * TILES), (low, HB * TILES),
                     (out, SUB * TILES), (added, SUB * TILES)):
            s.passed(k)


def moe_collect(c, results, place, share):
    nc, ps = c.nc, c.ps
    RING = 4
    with ExitStack() as ctx:
        w = c.sb(ctx, "mc_w", [P, KD, D], F32)
        bb = c.sb(ctx, "mc_b", [P, D], F32)
        got = c.sb(ctx, "mc_got", [P, RING, TK, D], F32)
        mixed = c.sb(ctx, "mc_mixed", [P, 2, D], F32)
        ot = c.sb(ctx, "mc_ot", [P, 2, KD * P], F32)
        w_in, weighed, summed, turned, copied, mm, added, biased = (c.sig(k) for k in (
            "w_in", "mc_weighed", "mc_summed", "mc_turned", "mc_copied", "mc_mm", "mc_added", "mc_biased"))
        got_in = [c.own_sig(f"mc_got{i}") for i in range(RING)]
        with nc.Block() as block:
            @block.sync
            def _(sp):
                sp.dma_start(bb[:, :], c.arg["L1_ffn_b_out"].rearrange("(a b) -> a b", a=1).partition_broadcast(P)
                             ).then_inc(w_in.sem, 16)
                sp.dma_start(w[:, :, :], c.arg["L1_ffn_W_out"].rearrange("(k p) n -> p k n", p=P)
                             ).then_inc(w_in.sem, 16)

            @block.gpsimd
            def _(pool):
                for t in range(NT):
                    if t >= RING:
                        pool.wait_ge(summed.sem, summed.at(t - RING + 1))
                    for j in range(TK):
                        pool.indirect_dma_start(got[:, t % RING, j, :], None, results,
                                                bass.IndirectOffsetOnAxis(ap=place[:, t, j:j + 1], axis=0)
                                                ).then_inc(got_in[t % RING].sem, 16)

            @block.tensor
            def _(pe):
                def turn(t):
                    pe.wait_ge(summed.sem, summed.at(t + 1))
                    if t >= 2:
                        pe.wait_ge(copied.sem, copied.at(t - 1))
                    for k in range(KD):
                        last = pe.transpose(ps[:, t % 2, P * k:P * k + P], mixed[:, t % 2, P * k:P * k + P],
                                            c.ident[:, :])
                    last.then_inc(turned.sem, 1)
                pe.wait_ge(w_in.sem, w_in.at(32))
                turn(0)
                for t in range(NT):
                    if t + 1 < NT:
                        turn(t + 1)
                    pe.wait_ge(copied.sem, copied.at(t + 1))
                    if t >= 2:
                        pe.wait_ge(added.sem, added.at(t - 1))
                    for k in range(KD):
                        last = pe.matmul(ps[:, 4 + t % 2, 0:D], ot[:, t % 2, P * k:P * k + P], w[:, k, :],
                                         start=(k == 0), stop=(k == KD - 1))
                    last.then_inc(mm.sem, 1)

            @block.scalar
            def _(act):
                for t in range(NT):
                    act.wait_ge(turned.sem, turned.at(t + 1))
                    if t >= 2:
                        act.wait_ge(mm.sem, mm.at(t - 1))
                    act.activation(ot[:, t % 2, :], ps[:, t % 2, 0:KD * P], ACT.Copy).then_inc(copied.sem, 1)

            @block.vector
            def _(dve):
                dve.wait_ge(w_in.sem, w_in.at(32))
                for t in range(NT):
                    dve.tensor_tensor(c.x[:, t, :], c.x[:, t, :], bb[:, :], ALU.add).then_inc(biased.sem, 1)

                def finish(t):
                    dve.wait_ge(mm.sem, mm.at(t + 1))
                    dve.wait_ge(biased.sem, biased.at(t + 1))
                    dve.tensor_tensor(c.x[:, t, :], ps[:, 4 + t % 2, 0:D], c.x[:, t, :], ALU.add
                                      ).then_inc(added.sem, 1)
                for t in range(NT):
                    dve.wait_ge(got_in[t % RING].sem, got_in[t % RING].at(16 * TK * (t // RING + 1)))
                    if t >= 2:
                        dve.wait_ge(turned.sem, turned.at(t - 1))
                    m, g = mixed[:, t % 2, :], got[:, t % RING, :, :]
                    dve.tensor_scalar(m, g[:, 0, :], share[:, t, 0:1], None, ALU.mult).then_inc(weighed.sem, 1)
                    dve.wait_ge(weighed.sem, weighed.at(t + 1))
                    dve.scalar_tensor_tensor(m, g[:, 1, :], share[:, t, 1:2], m, ALU.mult, ALU.add
                                             ).then_inc(summed.sem, 1)
                    if t >= 2:
                        finish(t - 2)
                finish(NT - 2)
                finish(NT - 1)
        for i in range(RING):
            got_in[i].passed(16 * TK * len(range(i, NT, RING)))
        for s, k in ((w_in, 32), (weighed, NT), (summed, NT), (turned, NT), (copied, NT), (mm, NT), (added, NT),
                     (biased, NT)):
            s.passed(k)


def store(c, out):
    nc = c.nc
    sent = c.sig("stored")
    with nc.Block() as block:
        @block.sync
        def _(sp):
            for b in range(4):
                sp.dma_start(out.rearrange("b (t p) d -> p (b t) d", p=P)[:, 4 * b:4 * b + 4, :],
                                      c.x[:, 4 * b:4 * b + 4, :]).then_inc(sent.sem, 16)
            sp.wait_ge(sent.sem, sent.at(64))


def build(nc, arg, out):
    def scratch(name, shape, dt):
        return nc.dram_tensor(name, shape, dt, kind="Internal").ap()

    with ExitStack() as ctx:
        c = Core(nc, ctx, arg)
        setup(c)
        with ExitStack() as with_context:
            ct = c.sb(with_context, "ct", [96, 2, B * M], F32)
            make_context(c, ct)
            c.new_stage()
            self_layer(c, scratch)
            c.new_stage()
            cross(c, 0, True, ct, scratch)
            c.new_stage()
            ffn_shared(c)
            c.new_stage()
            recurrent(c)
            c.new_stage()
            cross(c, 1, False, ct, scratch)
            c.new_stage()
        moe(c, scratch)
        store(c, out)


def self_layer(c, scratch):
    with ExitStack() as c0:
        o_tok = c.sb(c0, "o_tok0", [P, NT, D], F32)
        scr_q, scr_k = scratch("scr_q0", [PARTS, D, N], BF16), scratch("scr_k0", [PARTS, D, N], BF16)
        with ExitStack() as c1:
            v_all = c.sb(c1, "v_all0", [P, NT, H, VW], F32)
            project_self(c, v_all, scr_q, scr_k)
            SelfAttention(c, c1, v_all, scr_q, scr_k, o_tok).run()
        project_out(c, "po0", o_tok, KD, c.arg["L0_attn_Wout"], c.arg["L0_attn_bout"])


def cross(c, layer, wide, ct, scratch):
    width = 64 if wide else DH
    dt = F32 if wide else BF16
    parts = 2 if wide else PARTS
    with ExitStack() as c0:
        o_tok = c.sb(c0, f"o_tokx{layer}", [P, NT, H * width], F32)
        scr_q = scratch(f"scr_qx{layer}", [parts, H * width, N], dt)
        scr_k = scratch(f"scr_kx{layer}", [parts, H * width, B * M], dt)
        with ExitStack() as c1:
            v_all = c.sb(c1, f"v_allx{layer}", [MH, 2 * B, H, width + 1 if wide else VW], F32)
            project_cross(c, layer, wide, ct, v_all, scr_q, scr_k)
            attention = CrossAttention(c, c1, wide, v_all, scr_q, scr_k, o_tok)
            attention.run()
            attention.k_in.passed(0 if wide else 16 * len(K_ROWS))
        project_out(c, f"pox{layer}", o_tok, H * width // P, c.arg[f"L{layer}_xattn_Wo"], c.arg[f"L{layer}_xattn_bo"])


_INS = [
    "x",
    "ctx_768",
    "L0_attn_Wqkv",
    "L0_attn_bqkv",
    "L0_attn_Wout",
    "L0_attn_bout",
    "L0_xattn_Wq",
    "L0_xattn_Wk",
    "L0_xattn_Wv",
    "L0_xattn_Wo",
    "L0_xattn_bo",
    "L0_ffn_w_shared_in",
    "L0_ffn_w_shared_out",
    "L0_ffn_w1_shared",
    "L0_ffn_w2",
    "L0_ffn_w_gate",
    "L0_ffn_gate_bias",
    "L1_attn_w_i",
    "L1_attn_w_f",
    "L1_attn_w_g",
    "L1_attn_w_o",
    "L1_attn_nw_i",
    "L1_attn_nw_f",
    "L1_attn_nw_g",
    "L1_attn_nw_o",
    "L1_attn_g_norm_w",
    "L1_xattn_Wq",
    "L1_xattn_bq",
    "L1_xattn_Wk",
    "L1_xattn_bk",
    "L1_xattn_Wv",
    "L1_xattn_bv",
    "L1_xattn_Wo",
    "L1_xattn_bo",
    "L1_ffn_W_in",
    "L1_ffn_b_in",
    "L1_ffn_W_gate",
    "L1_ffn_b_gate",
    "L1_ffn_W1",
    "L1_ffn_b1",
    "L1_ffn_W2",
    "L1_ffn_b2",
    "L1_ffn_W_out",
    "L1_ffn_b_out",
]


def kernel(**inputs):
    import numpy as _np
    import concourse.bacc as _bacc
    from concourse import mybir as _mybir
    from concourse.bass_utils import run_bass_kernel_spmd as _run

    nc = _bacc.Bacc("TRN2", target_bir_lowering=False, num_devices=1)
    arrays, arg = {}, {}
    for name in _INS:
        a = _np.ascontiguousarray(inputs[name])
        arrays[f"in_{name}_dram"] = a
        arg[name] = nc.dram_tensor(f"in_{name}_dram", a.shape, _mybir.dt.from_np(a.dtype), kind="ExternalInput").ap()
    out = nc.dram_tensor("out_0_dram", (B, S, D), F32, kind="ExternalOutput").ap()
    build(nc, arg, out)
    r = _run(nc, [arrays], core_ids=[0])
    return r.results[0]["out_0_dram"]
```
